# Optimizing a Trainium2 kernel written in Bass

```python
import numpy as np
import jax
import jax.numpy as jnp

def _softmax(x, axis=-1):
    return jax.nn.softmax(x, axis=axis)

def _gelu(x):
    return jax.nn.gelu(x, approximate=True)

def _silu(x):
    return jax.nn.silu(x)

def _sigmoid(x):
    return jax.nn.sigmoid(x)

def _layernorm(x, axis=-1, eps=1e-05):
    m = jnp.mean(x, axis=axis, keepdims=True)
    v = jnp.var(x, axis=axis, keepdims=True)
    return (x - m) / jnp.sqrt(v + eps)

def _scatter_add(tgt, idx, src, axis=0):
    return tgt.at[idx].add(src)

def _segment_sum(src, seg, n):
    return jax.ops.segment_sum(src, seg, n)
kernel_name = 'mk_perceiver_d1_seqx_r2_792ddb'

def setup_inputs(seed: int=0):
    np.random.seed(seed)
    _w = jnp.asarray

    def _rec_inputs():
        import jax
        import jax.numpy as jnp
        _rk = jax.random.key(seed)
        x = 7.22e-05 + 1 * jax.random.normal(jax.random.fold_in(_rk, 1), (2, 128, 512), jnp.float32)
        _lenS = 128 - jax.random.randint(jax.random.fold_in(_rk, 7), (2,), 0, max(1, 128 // 4) + 1, jnp.int32)
        _lenS2 = 2048 - jax.random.randint(jax.random.fold_in(_rk, 8), (2,), 0, max(1, 2048 // 4) + 1, jnp.int32)
        _ctx_1024P = jax.random.normal(jax.random.fold_in(_rk, 11), (2, 16, 512), jnp.float32)
        _ctx_1024c = jax.random.dirichlet(jax.random.fold_in(_rk, 511), 0.3 * jnp.ones((16,), jnp.float32), (2, 2048))
        _ctx_1024t = jnp.einsum('bsk,bkd->bsd', _ctx_1024c, _ctx_1024P)
        _ctx_1024t = _ctx_1024t * jax.lax.rsqrt(jnp.mean(jnp.square(_ctx_1024t)) + 1e-12) * 0.953939
        ctx_1024 = 4.13588e-05 + 0.999923 * (_ctx_1024t + 0.3 * jax.random.normal(jax.random.fold_in(_rk, 611), (2, 2048, 512), jnp.float32))
        _validS = jnp.arange(128)[None, :] < _lenS[:, None]
        _validS2 = jnp.arange(2048)[None, :] < _lenS2[:, None]
        _causal = jnp.tril(jnp.ones((128, 128), dtype=bool))
        mask_1x1xSxS2_ik0 = jnp.where(jnp.broadcast_to(_validS2[0:1, None, None, :], (1, 1, 128, 2048)), 0, 1).astype(jnp.int32)
        return (x, ctx_1024, mask_1x1xSxS2_ik0)
    x, ctx_1024, mask_1x1xSxS2_ik0 = _rec_inputs()

    def _L0_xattn_setup():
        import jax, jax.numpy as jnp
        import numpy as np
        D_MODEL = 512
        NUM_HEADS = 16
        D_K = D_MODEL // NUM_HEADS
        SCALE = float(np.sqrt(D_K))
        B, S = (4, 1024)
        key = jax.random.key(seed)
        ks = jax.random.split(key, 12)
        q = jax.random.normal(ks[0], (B, S, D_MODEL), dtype=jnp.float32)
        k = jax.random.normal(ks[1], (B, S, D_MODEL), dtype=jnp.float32)
        v = jax.random.normal(ks[2], (B, S, D_MODEL), dtype=jnp.float32)
        mask = jnp.tril(jnp.ones((S, S), dtype=jnp.int32))[None, None]
        std = 1.0 / np.sqrt(D_MODEL)
        Wq = jax.random.normal(ks[3], (D_MODEL, D_MODEL), dtype=jnp.float32) * std
        Wk = jax.random.normal(ks[4], (D_MODEL, D_MODEL), dtype=jnp.float32) * std
        Wv = jax.random.normal(ks[5], (D_MODEL, D_MODEL), dtype=jnp.float32) * std
        Wo = jax.random.normal(ks[6], (D_MODEL, D_MODEL), dtype=jnp.float32) * std
        bq = jax.random.normal(ks[7], (D_MODEL,), dtype=jnp.float32) * std
        bk = jax.random.normal(ks[8], (D_MODEL,), dtype=jnp.float32) * std
        bv = jax.random.normal(ks[9], (D_MODEL,), dtype=jnp.float32) * std
        bo = jax.random.normal(ks[10], (D_MODEL,), dtype=jnp.float32) * std
        return {'q': q, 'k': k, 'v': v, 'mask': mask, 'Wq': Wq, 'bq': bq, 'Wk': Wk, 'bk': bk, 'Wv': Wv, 'bv': bv, 'Wo': Wo, 'bo': bo}
    _L0_xattn_all = _L0_xattn_setup()
    _L0_xattn_in = {k: v for k, v in _L0_xattn_all.items() if k in ('Wq', 'bq', 'Wk', 'bk', 'Wv', 'bv', 'Wo', 'bo')}
    del _L0_xattn_all

    def _L0_attn_setup():
        import jax, jax.numpy as jnp
        import numpy as np
        L, H, D, DH, DF = (4, 16, 512, 64, 2048)
        B, S = (4, 512)

        def layer_norm(x, g, b):
            mu = jnp.mean(x, axis=-1, keepdims=True)
            var = jnp.mean((x - mu) ** 2, axis=-1, keepdims=True)
            return (x - mu) * jax.lax.rsqrt(var + 1e-05) * g + b

        def pos_encoding(seq_len, d):
            pos = jnp.arange(seq_len - 1, -1, -1, dtype=jnp.float32)
            freq = 1.0 / 10000.0 ** (jnp.arange(0, d, 2, dtype=jnp.float32) / d)
            ang = pos[:, None] * freq[None, :]
            return jnp.concatenate([jnp.sin(ang), jnp.cos(ang)], axis=-1)
        key = jax.random.key(seed)
        ks = jax.random.split(key, 16)
        s = 0.02
        return {'x': jax.random.normal(ks[0], (B, S, D), jnp.float32), 'W_qkv': jax.random.normal(ks[1], (L, D, 3 * H * DH), jnp.float32) * s, 'W_r': jax.random.normal(ks[2], (L, D, H * DH), jnp.float32) * s, 'W_o': jax.random.normal(ks[3], (L, H * DH, D), jnp.float32) * s, 'u': jax.random.normal(ks[4], (H, DH), jnp.float32) * s, 'v': jax.random.normal(ks[5], (H, DH), jnp.float32) * s, 'ln1_g': jnp.ones((L, D), jnp.float32), 'ln1_b': jnp.zeros((L, D), jnp.float32), 'W_ff1': jax.random.normal(ks[6], (L, D, DF), jnp.float32) * s, 'b_ff1': jnp.zeros((L, DF), jnp.float32), 'W_ff2': jax.random.normal(ks[7], (L, DF, D), jnp.float32) * s, 'b_ff2': jnp.zeros((L, D), jnp.float32), 'ln2_g': jnp.ones((L, D), jnp.float32), 'ln2_b': jnp.zeros((L, D), jnp.float32)}
    _L0_attn_all = _L0_attn_setup()
    _L0_attn_in = {k: v for k, v in _L0_attn_all.items() if k in ('W_qkv', 'W_r', 'W_o', 'u', 'v', 'ln1_g', 'ln1_b', 'W_ff1', 'b_ff1', 'W_ff2', 'b_ff2', 'ln2_g', 'ln2_b')}
    del _L0_attn_all

    def _L0_ffn_setup():
        import jax, jax.numpy as jnp
        import numpy as np
        E = 8
        TOPK = 2
        D = 512
        F = 2048
        B, S = (2, 256)

        def _gmm(x, W, expert_onehot):
            return jnp.einsum('te,td,edf->tf', expert_onehot, x, W)
        key = jax.random.key(seed)
        k1, k2, k3, k4, k5 = jax.random.split(key, 5)
        scale_d = 1.0 / np.sqrt(D)
        scale_f = 1.0 / np.sqrt(F)
        return {'inputs': jax.random.normal(k1, (B, S, D), jnp.float32), 'gate_kernel': jax.random.normal(k2, (D, E), jnp.float32) * scale_d, 'w0': jax.random.normal(k3, (E, D, F), jnp.float32) * scale_d, 'w1': jax.random.normal(k4, (E, D, F), jnp.float32) * scale_d, 'wo': jax.random.normal(k5, (E, F, D), jnp.float32) * scale_f}
    _L0_ffn_all = _L0_ffn_setup()
    _L0_ffn_in = {k: v for k, v in _L0_ffn_all.items() if k in ('gate_kernel', 'w0', 'w1', 'wo')}
    del _L0_ffn_all
    return {'x': x, 'ctx_1024': ctx_1024, 'mask_1x1xSxS2_ik0': mask_1x1xSxS2_ik0, 'L0_xattn_Wq': _L0_xattn_in['Wq'], 'L0_xattn_bq': _L0_xattn_in['bq'], 'L0_xattn_Wk': _L0_xattn_in['Wk'], 'L0_xattn_bk': _L0_xattn_in['bk'], 'L0_xattn_Wv': _L0_xattn_in['Wv'], 'L0_xattn_bv': _L0_xattn_in['bv'], 'L0_xattn_Wo': _L0_xattn_in['Wo'], 'L0_xattn_bo': _L0_xattn_in['bo'], 'L0_attn_W_qkv': _L0_attn_in['W_qkv'], 'L0_attn_W_r': _L0_attn_in['W_r'], 'L0_attn_W_o': _L0_attn_in['W_o'], 'L0_attn_u': _L0_attn_in['u'], 'L0_attn_v': _L0_attn_in['v'], 'L0_attn_ln1_g': _L0_attn_in['ln1_g'], 'L0_attn_ln1_b': _L0_attn_in['ln1_b'], 'L0_attn_W_ff1': _L0_attn_in['W_ff1'], 'L0_attn_b_ff1': _L0_attn_in['b_ff1'], 'L0_attn_W_ff2': _L0_attn_in['W_ff2'], 'L0_attn_b_ff2': _L0_attn_in['b_ff2'], 'L0_attn_ln2_g': _L0_attn_in['ln2_g'], 'L0_attn_ln2_b': _L0_attn_in['ln2_b'], 'L0_ffn_gate_kernel': _L0_ffn_in['gate_kernel'], 'L0_ffn_w0': _L0_ffn_in['w0'], 'L0_ffn_w1': _L0_ffn_in['w1'], 'L0_ffn_wo': _L0_ffn_in['wo']}

def reference(x, ctx_1024, mask_1x1xSxS2_ik0, L0_xattn_Wq, L0_xattn_bq, L0_xattn_Wk, L0_xattn_bk, L0_xattn_Wv, L0_xattn_bv, L0_xattn_Wo, L0_xattn_bo, L0_attn_W_qkv, L0_attn_W_r, L0_attn_W_o, L0_attn_u, L0_attn_v, L0_attn_ln1_g, L0_attn_ln1_b, L0_attn_W_ff1, L0_attn_b_ff1, L0_attn_W_ff2, L0_attn_b_ff2, L0_attn_ln2_g, L0_attn_ln2_b, L0_ffn_gate_kernel, L0_ffn_w0, L0_ffn_w1, L0_ffn_wo):
    import jax
    import jax.numpy as jnp

    def _L0_xattn_ref(q, k, v, mask, Wq, bq, Wk, bk, Wv, bv, Wo, bo):
        import jax, jax.numpy as jnp
        import numpy as np
        D_MODEL = 512
        NUM_HEADS = 16
        D_K = D_MODEL // NUM_HEADS
        SCALE = float(np.sqrt(D_K))
        B, S = (4, 1024)
        Bsz = q.shape[0]

        def proj(x, W, b):
            y = x @ W.T + b
            return y.reshape(Bsz, -1, NUM_HEADS, D_K).transpose(0, 2, 1, 3)
        qh = proj(q, Wq, bq)
        kh = proj(k, Wk, bk)
        vh = proj(v, Wv, bv)
        scores = jnp.einsum('bhqd,bhkd->bhqk', qh, kh) / SCALE
        scores = jnp.where(mask == 0, jnp.float32(-1000000000.0), scores)
        attn = jax.nn.softmax(scores, axis=-1)
        out = jnp.einsum('bhqk,bhkd->bhqd', attn, vh)
        out = out.transpose(0, 2, 1, 3).reshape(Bsz, -1, D_MODEL)
        return out @ Wo.T + bo

    def _L0_attn_ref(x, W_qkv, W_r, W_o, u, v, ln1_g, ln1_b, W_ff1, b_ff1, W_ff2, b_ff2, ln2_g, ln2_b):
        import jax, jax.numpy as jnp
        import numpy as np
        L, H, D, DH, DF = (4, 16, 512, 64, 2048)
        B, S = (4, 512)

        def layer_norm(x, g, b):
            mu = jnp.mean(x, axis=-1, keepdims=True)
            var = jnp.mean((x - mu) ** 2, axis=-1, keepdims=True)
            return (x - mu) * jax.lax.rsqrt(var + 1e-05) * g + b

        def pos_encoding(seq_len, d):
            pos = jnp.arange(seq_len - 1, -1, -1, dtype=jnp.float32)
            freq = 1.0 / 10000.0 ** (jnp.arange(0, d, 2, dtype=jnp.float32) / d)
            ang = pos[:, None] * freq[None, :]
            return jnp.concatenate([jnp.sin(ang), jnp.cos(ang)], axis=-1)
        b, s_len, _ = x.shape
        r = pos_encoding(s_len, D)
        h = x
        inv_sqrt_d = 1.0 / jnp.sqrt(jnp.float32(DH))
        for i in range(L):
            qkv = h @ W_qkv[i]
            q, k, val = jnp.split(qkv, 3, axis=-1)
            q = q.reshape(b, s_len, H, DH)
            k = k.reshape(b, s_len, H, DH)
            val = val.reshape(b, s_len, H, DH)
            kr = (r @ W_r[i]).reshape(s_len, H, DH)
            AC = jnp.einsum('bqhd,bkhd->bhqk', q + u, k)
            BD = jnp.einsum('bqhd,khd->bhqk', q + v, kr)
            prob = jax.nn.softmax((AC + BD) * inv_sqrt_d, axis=-1)
            vec = jnp.einsum('bhqk,bkhd->bqhd', prob, val).reshape(b, s_len, H * DH)
            h = layer_norm(h + vec @ W_o[i], ln1_g[i], ln1_b[i])
            ff = jax.nn.relu(h @ W_ff1[i] + b_ff1[i]) @ W_ff2[i] + b_ff2[i]
            h = layer_norm(ff, ln2_g[i], ln2_b[i])
        return h

    def _L0_ffn_ref(inputs, gate_kernel, w0, w1, wo):
        import jax, jax.numpy as jnp
        import numpy as np
        E = 8
        TOPK = 2
        D = 512
        F = 2048
        B, S = (2, 256)

        def _gmm(x, W, expert_onehot):
            return jnp.einsum('te,td,edf->tf', expert_onehot, x, W)
        dtype = inputs.dtype
        gate_logits = jnp.einsum('bsd,de->bse', inputs, gate_kernel)
        weights, selected_experts = jax.lax.top_k(gate_logits, TOPK)
        weights = jax.nn.softmax(weights.astype(jnp.float32), axis=-1).astype(dtype)
        inputs_2d = jnp.reshape(inputs, (-1, D))
        flat_sel = jnp.ravel(selected_experts)
        sort_idx = jnp.argsort(flat_sel)
        rep = jnp.repeat(inputs_2d, TOPK, axis=0)
        sorted_hidden = jnp.take(rep, sort_idx, axis=0)
        T = flat_sel.shape[0]
        group_sizes = jnp.zeros((E,), jnp.int32).at[flat_sel].add(1)
        expert_ids = jnp.repeat(jnp.arange(E), group_sizes, total_repeat_length=T)
        onehot = jax.nn.one_hot(expert_ids, E, dtype=dtype)
        layer_1 = _gmm(sorted_hidden, w0, onehot)
        layer_2 = _gmm(sorted_hidden, w1, onehot)
        intermediate = jax.nn.silu(layer_1) * layer_2
        layer_3 = _gmm(intermediate, wo, onehot)
        unsort = jnp.take(layer_3, jnp.argsort(sort_idx), axis=0)
        combined = unsort * jnp.ravel(weights)[:, None]
        out = jnp.sum(combined.reshape(-1, TOPK, D), axis=1)
        return out.reshape(inputs.shape).astype(dtype)
    x = x + _L0_xattn_ref(_layernorm(x, axis=-1), ctx_1024, ctx_1024, mask_1x1xSxS2_ik0, L0_xattn_Wq, L0_xattn_bq, L0_xattn_Wk, L0_xattn_bk, L0_xattn_Wv, L0_xattn_bv, L0_xattn_Wo, L0_xattn_bo)
    x = x + _L0_attn_ref(_layernorm(x, axis=-1), L0_attn_W_qkv, L0_attn_W_r, L0_attn_W_o, L0_attn_u, L0_attn_v, L0_attn_ln1_g, L0_attn_ln1_b, L0_attn_W_ff1, L0_attn_b_ff1, L0_attn_W_ff2, L0_attn_b_ff2, L0_attn_ln2_g, L0_attn_ln2_b)
    x = x + _L0_ffn_ref(_layernorm(x, axis=-1), L0_ffn_gate_kernel, L0_ffn_w0, L0_ffn_w1, L0_ffn_wo)
    return x

_drawn_inputs = setup_inputs


def setup_inputs(seed=0):
    import zlib

    import numpy as np

    out = dict(_drawn_inputs(seed))
    spreads = {'L0_attn_ln1_g': (1.0, 0.2),
     'L0_attn_ln1_b': (0.0, 0.1),
     'L0_attn_b_ff1': (0.0, 0.1),
     'L0_attn_b_ff2': (0.0, 0.1),
     'L0_attn_ln2_g': (1.0, 0.2),
     'L0_attn_ln2_b': (0.0, 0.1)}
    factors = {'L0_xattn_bk': 200.0,
     'L0_attn_W_r': 3.462,
     'L0_attn_u': 179.297,
     'L0_attn_v': 64.0,
     'L0_xattn_bq': 2.736}
    for name, (base, spread) in spreads.items():
        noise = np.random.default_rng([zlib.crc32(name.encode()), seed]).standard_normal(out[name].shape)
        drawn = base * np.exp(spread * noise) if base else spread * noise
        out[name] = jnp.asarray(drawn.astype(out[name].dtype))
    for name, factor in factors.items():
        out[name] = (out[name] * factor).astype(out[name].dtype)
    return out
```

```python
from contextlib import ExitStack

import concourse.bass as bass
import concourse.mybir as mybir
import numpy as np

F32 = mybir.dt.float32
F32R = mybir.dt.float32r
I32 = mybir.dt.int32
U32 = mybir.dt.uint32
ALU = mybir.AluOpType
ACT = mybir.ActivationFunctionType
X_AXIS = mybir.AxisListType.X

P = 128
B = 2
D = 512
KT = D // P
SK = 2048
CHUNK = 512
NCH = SK // CHUNK
XH, XDH = 16, 32
GROUPS = XH * XDH // P
HPG = P // XDH
L, H, DH, DF = 4, 16, 64, 2048
E, F = 8, 2048
EPS = 1e-5
MASKED = -float(2 ** 30)
X_SCALE = float(1.0 / np.float32(np.sqrt(XDH)))
L_SCALE = 1.0 / 8.0

RING = 3
S_WQ, S_WK, S_WV, S_CTX = 0, 1, 2, 3
S_WO = S_CTX + B * NCH
S_LAYER = S_WO + 1
LU = 18
U_WR, U_WQ, U_WK, U_WV, U_WO, U_FF1, U_FF2 = 0, 2, 4, 6, 8, 10, 14
S_MOE = S_LAYER + L * LU
EU = 12
E_ORDER = [("w0", 0), ("w1", 0), ("w0", 1), ("w1", 1), ("w0", 2), ("w1", 2), ("wo", 0), ("w0", 3),
           ("w1", 3), ("wo", 1), ("wo", 2), ("wo", 3)]
assert LU % RING == 0 and EU % RING == 0 and S_LAYER % RING == 0 and S_MOE % RING == 0


def nth(s):
    return s // RING + 1


def wait_unit(eng, sem, s, iteration=0, per=0, each=1):
    eng.wait_ge(sem[s % RING], (iteration * (per // RING) + nth(s)) * each)


class Memory:

    def __init__(self, nc, ctx, dram):
        self.nc, self.ctx, self.dram = nc, ctx, dram

    def sb(self, name, shape, dt=F32):
        return self.ctx.enter_context(self.nc.sbuf_tensor(name, shape, dt))

    def sems(self, names):
        return [self.ctx.enter_context(self.nc.semaphore(name)) for name in names.split()]

    def slot_sems(self, name):
        return [self.ctx.enter_context(self.nc.semaphore(f"{name}{i}")) for i in range(RING)]


def three_passes(pe, out, w_hi, w_lo, m_hi, m_lo, first, last):
    pe.matmul(out, w_hi, m_hi, start=first, stop=False)
    pe.matmul(out, w_hi, m_lo, start=False, stop=False)
    return pe.matmul(out, w_lo, m_hi, start=False, stop=last)


def split_hi(act, m, s, iteration=0, per=0, hi=None):
    wait_unit(act, m.loaded, s, iteration, per, 16)
    dst = m.w_hi[s % RING] if hi is None else hi
    act.activation(dst[:].rearrange("p k n -> p (k n)"), m.raw[:, s % RING, :], ACT.Copy).then_inc(
        m.hi_done[s % RING], 1)


def split_lo(eng, m, s, iteration=0, per=0, hi=None, lo=None):
    wait_unit(eng, m.hi_done, s, iteration, per)
    h = m.w_hi[s % RING] if hi is None else hi
    l_ = m.w_lo[s % RING] if lo is None else lo
    eng.tensor_tensor(l_[:].rearrange("p k n -> p (k n)"), m.raw[:, s % RING, :],
                      h[:].rearrange("p k n -> p (k n)").bitcast(F32), ALU.subtract).then_inc(
        m.lo_done[s % RING], 1)


class Step:

    def __init__(self, eng, sem, base=0, iteration=0, per=0):
        self.eng, self.sem, self.base, self.iteration, self.per, self.n = eng, sem, base, iteration, per, 0

    def done(self, ins):
        ins.then_inc(self.sem, 1)
        self.n += 1

    def wait(self):
        self.eng.wait_ge(self.sem, self.iteration * self.per + self.base + self.n)


def ln_scale(dve, m, step, src, t, n):
    step.done(dve.bn_stats(m.bn6[:, t, :], src))
    step.wait()
    dve.memset(m.newton[:, t:t + 1], 0.0)
    step.done(dve.bn_aggr(m.mean_var[:, t, :], m.bn6[:, t, :]))
    step.wait()
    var_eps, root0 = m.var_eps[:, t:t + 1], m.root0[:, t:t + 1]
    dve.tensor_scalar(var_eps, m.mean_var[:, t, 1:2], EPS, None, ALU.add).then_inc(m.ln_var, 1)
    dve.wait_ge(m.ln_rooted, (n - 1) * B + t + 1)
    step.done(dve.reciprocal(root0, m.ln_sqrt[:, t:t + 1]))
    step.wait()
    step.done(dve.scalar_tensor_tensor(m.newton[:, t:t + 1], root0, -0.5, root0, ALU.mult, ALU.mult))
    step.wait()
    step.done(dve.tensor_tensor(m.newton2[:, t:t + 1], m.newton[:, t:t + 1], var_eps, ALU.mult))
    step.wait()
    step.done(dve.scalar_tensor_tensor(m.rstd[:, t:t + 1], m.newton2[:, t:t + 1], 1.5, root0, ALU.add, ALU.mult))


def ln_root(act, m, n):
    for t in range(B):
        act.wait_ge(m.ln_var, (n - 1) * B + t + 1)
        act.activation(m.ln_sqrt[:, t:t + 1], m.var_eps[:, t:t + 1], ACT.Sqrt).then_inc(m.ln_rooted, 1)


def ln_apply(dve, m, out, src, t):
    return dve.tensor_scalar(out, src, m.mean_var[:, t, 0:1], m.rstd[:, t:t + 1], ALU.subtract, ALU.mult)


def build_program(nc, x, ctx_t, mask, w_cross, w_stream, cross_vecs, bo_row, consts, r_t, uv, ff1_bias,
                  layer_rows, gate, out):
    with ExitStack() as ctx:
        m = Memory(nc, ctx, dict(x=x, ctx_t=ctx_t, mask=mask, w_cross=w_cross, w_stream=w_stream,
                                 cross_vecs=cross_vecs, bo_row=bo_row, consts=consts, r_t=r_t, uv=uv,
                                 ff1_bias=ff1_bias, layer_rows=layer_rows, gate=gate, out=out))
        common_memory(m)
        for phase_memory in (cross_memory, layer_memory, moe_memory):
            with ExitStack() as m.ctx:
                phase_memory(m)
        block = ctx.enter_context(nc.Block())

        @block.sync
        def _(sp):
            sp_program(sp, m)

        @block.gpsimd
        def _(pool):
            pool_cross(pool, m)
            pool_layers(pool, m)
            pool_moe(pool, m)

        @block.scalar
        def _(act):
            act_cross(act, m)
            act_layers(act, m)
            act_moe(act, m)

        @block.vector
        def _(dve):
            step = Step(dve, m.dve_step)
            dve_cross(dve, m, step)
            dve_layers(dve, m, step)
            dve_moe(dve, m, step)

        @block.tensor
        def _(pe):
            pe_cross(pe, m)
            pe_layers(pe, m)
            pe_moe(pe, m)


def common_memory(m):
    m.raw = m.sb("raw", [P, RING, KT * CHUNK])
    m.w_hi = [m.sb(f"w_hi{i}", [P, KT, CHUNK], F32R) for i in range(RING)]
    m.w_lo = [m.sb(f"w_lo{i}", [P, KT, CHUNK], F32R) for i in range(RING)]
    m.loaded = m.slot_sems("loaded")
    m.hi_done = m.slot_sems("hi_done")
    m.lo_done = m.slot_sems("lo_done")
    m.ident = m.sb("ident", [P, P])
    m.earlier = m.sb("earlier", [P, P])
    m.iota = m.sb("iota", [P, P])
    m.ones = m.sb("ones", [P, P])
    m.gate_sb = m.sb("gate_sb", [P, KT, E])
    m.x_res = m.sb("x_res", [P, B, D])
    m.r_hi = m.sb("r_hi", [P, KT, P], F32R)
    m.r_lo = m.sb("r_lo", [P, KT, P], F32R)
    m.uv_sb = m.sb("uv_sb", [P, 2, H])
    m.ff1_bias_sb = m.sb("ff1_bias_sb", [P, L, DF // P])
    m.bn6 = m.sb("bn6", [P, B, 6])
    m.mean_var = m.sb("mean_var", [P, B, 2])
    m.var_eps = m.sb("var_eps", [P, B])
    m.ln_sqrt = m.sb("ln_sqrt", [P, B])
    m.root0 = m.sb("root0", [P, B])
    m.newton = m.sb("newton", [P, B])
    m.newton2 = m.sb("newton2", [P, B])
    m.rstd = m.sb("rstd", [P, B])
    (m.ident_in, m.x_in, m.vecs_in, m.vecs_in2, m.mask_in, m.r_in, m.uv_in, m.bias_in, m.gate_in,
     m.consts_in, m.ln_var, m.ln_rooted, m.dve_step, m.out_done) = m.sems(
        "ident_in x_in vecs_in vecs_in2 mask_in r_in uv_in bias_in gate_in consts_in ln_var "
        "ln_rooted dve_step out_done")
    m.bank = [m.ctx.enter_context(m.nc.psum_tensor(f"bank{i}", [P, CHUNK], F32)) for i in range(8)]


S_BANKS, T_BANKS, O_BANK, OT_BANK = (0, 1, 2, 3), (4, 5), 6, 7


def cross_memory(m):
    m.ident_r = m.sb("ident_r", [P, P], F32R)
    m.cross_vec = m.sb("cross_vec", [P, 3, KT])
    m.bo_bc = m.sb("bo_bc", [P, D])
    m.q_scale = m.sb("q_scale", [P, 1])
    m.mask_max = m.sb("mask_max", [P, 1])
    m.mask_add = m.sb("mask_add", [P, SK], F32R)
    m.q_feat = m.sb("q_feat", [P, KT, B * P])
    m.qz_hi = m.sb("qz_hi", [P, HPG, P], F32R)
    m.qz_lo = m.sb("qz_lo", [P, HPG, P], F32R)
    m.k_hi = m.sb("k_hi", [P, KT, CHUNK], F32R)
    m.k_lo = m.sb("k_lo", [P, KT, CHUNK], F32R)
    m.v_grp = m.sb("v_grp", [P, SK // P, P])
    m.probs = m.sb("probs", [P, NCH, CHUNK])
    m.probs_T = m.sb("probs_T", [P, 2, CHUNK])
    m.part_max = m.sb("part_max", [P, NCH])
    m.neg_max = m.sb("neg_max", [P, 1])
    m.shift = m.sb("shift", [P, HPG])
    m.part_sum = m.sb("part_sum", [P, HPG, NCH])
    m.row_sum = m.sb("row_sum", [P, HPG])
    m.row_inv = m.sb("row_inv", [P, HPG])
    m.o_feat = m.sb("o_feat", [P, P])
    m.o_tok = m.sb("o_tok", [P, B, D])
    outer = m.ctx
    with ExitStack() as m.ctx:
        m.k_all = m.sb("k_all", [P, KT, SK])
        m.v_all = m.sb("v_all", [P, SK // P, D])
    with ExitStack() as m.ctx:
        m.xn = m.sb("xn", [P, B, D])
        m.xT_hi = m.sb("xT_hi", [P, KT, B * P], F32R)
        m.xT_lo = m.sb("xT_lo", [P, KT, B * P], F32R)
    with ExitStack() as m.ctx:
        m.vecT_hi = m.sb("vecT_hi", [P, KT, B * P], F32R)
        m.vecT_lo = m.sb("vecT_lo", [P, KT, B * P], F32R)
    m.ctx = outer
    (m.ident_ready, m.xn_ready, m.xnT_mm, m.xT_hi_done, m.xT_lo_done, m.q_mm, m.q_done, m.mask_ready,
     m.r_hi_done, m.r_ready, m.qz_zeroed, m.bo_added, m.q_scale_done, m.k_mm, m.k_done, m.v_mm, m.v_done,
     m.k_hi_done, m.k_lo_done, m.qz_hi_done, m.qz_done, m.v_grp_done, m.s_mm, m.max_done, m.neg_done,
     m.shift_done, m.exp_done, m.pT_mm, m.pT_even, m.pT_odd, m.pv_mm, m.sum_done, m.inv_done, m.o_copied,
     m.oT_mm, m.oT_done, m.vec_mm, m.vec_hi, m.vec_lo, m.o_mm, m.x1_done) = m.sems(
        "ident_ready xn_ready xnT_mm xT_hi_done xT_lo_done q_mm q_done mask_ready r_hi_done r_ready "
        "qz_zeroed bo_added q_scale_done k_mm k_done v_mm v_done k_hi_done k_lo_done qz_hi_done qz_done "
        "v_grp_done s_mm max_done neg_done shift_done exp_done pT_mm pT_even pT_odd pv_mm sum_done "
        "inv_done o_copied oT_mm oT_done vec_mm vec_hi vec_lo o_mm x1_done")


def ctx_slot(m, n):
    return (m.w_hi[0], m.w_lo[0]) if n % 2 == 0 else (m.k_hi, m.k_lo)


def sp_program(sp, m):
    d = m.dram
    flat = m.raw

    def load(s, src):
        if s >= RING:
            wait_unit(sp, m.lo_done, s - RING)
        sp.dma_start(flat[:, s % RING, :], src).then_inc(m.loaded[s % RING], 16)

    sp.dma_start(m.x_res[:], d["x"].rearrange("b p d -> p b d")).then_inc(m.x_in, 16)
    load(S_WQ, d["w_cross"][0])
    sp.dma_start(m.ident[:], d["consts"][0]).then_inc(m.ident_in, 16)
    sp.dma_start(m.cross_vec[:], d["cross_vecs"]).then_inc(m.vecs_in, 16)
    sp.dma_start(m.bo_bc[:], d["bo_row"].partition_broadcast(P)).then_inc(m.vecs_in2, 16)
    load(S_WK, d["w_cross"][1])
    load(S_WV, d["w_cross"][2])
    sp.dma_start(m.k_all[:, KT - 1, :].bitcast(I32), d["mask"]).then_inc(m.mask_in, 16)
    sp.dma_start(m.v_all[:, 0, :], d["r_t"]).then_inc(m.r_in, 16)
    sp.dma_start(m.uv_sb[:], d["uv"]).then_inc(m.uv_in, 16)
    sp.dma_start(m.ff1_bias_sb[:], d["ff1_bias"]).then_inc(m.bias_in, 16)
    sp.dma_start(m.gate_sb[:], d["gate"]).then_inc(m.gate_in, 16)
    for n in range(B * NCH):
        load(S_CTX + n, d["ctx_t"][n])
        if n < 3:
            sp.wait_ge(m.consts_in, n * 16)
            sp.dma_start((m.earlier, m.iota, m.ones)[n][:], d["consts"][1 + n]).then_inc(m.consts_in, 16)
    load(S_WO, d["w_cross"][3])
    for k in range(RING):
        load(S_LAYER + k, d["w_stream"][k])
    sp_layers(sp, m)
    sp_moe(sp, m)


def pool_cross(pool, m):
    split_lo(pool, m, S_WQ)
    split_lo(pool, m, S_WK)
    split_lo(pool, m, S_WV)

    def context(n):
        split_lo(pool, m, S_CTX + n, hi=ctx_slot(m, n)[0], lo=ctx_slot(m, n)[1])

    for b in range(B):
        for n in range(b * NCH + b, (b + 1) * NCH):
            context(n)
        if b == 0:
            context(NCH)
        else:
            split_lo(pool, m, S_WO)
            split_lo(pool, m, S_LAYER)
            split_lo(pool, m, S_LAYER + 1)
        with pool.Fori(0, GROUPS) as g:
            for c in range(NCH):
                pool.wait_ge(m.k_hi_done, (g + b * GROUPS) * NCH + c + 1)
                pool.tensor_tensor(m.k_lo[:, c, :], m.k_all[:, g, c * CHUNK:(c + 1) * CHUNK],
                                   m.k_hi[:, c, :].bitcast(F32), ALU.subtract).then_inc(m.k_lo_done, 1)


def act_cross(act, m):
    act.wait_ge(m.x_in, 16)
    ln_root(act, m, 1)
    for s in (S_WQ, S_WK, S_WV):
        split_hi(act, m, s)
    for b in range(B):
        act.wait_ge(m.xnT_mm, b + 1)
        act.activation(m.xT_hi[:, :, b * P:(b + 1) * P], m.bank[b][:].rearrange("p (k t) -> p k t", k=KT),
                       ACT.Copy).then_inc(m.xT_hi_done, 1)
    act.wait_ge(m.vecs_in, 16)
    for f in range(KT):
        act.wait_ge(m.q_mm, f // 2 + 1)
        act.activation(m.q_feat[:, f, :], m.bank[2 + f // 2][:, (f % 2) * B * P:(f % 2 + 1) * B * P], ACT.Identity,
                       bias=m.cross_vec[:, 0, f:f + 1]).then_inc(m.q_done, 1)

    def context(n):
        if n >= 2:
            act.wait_ge(m.v_mm, (n - 1) * KT)
        if n == NCH + 1:
            act.wait_ge(m.s_mm, GROUPS * HPG * NCH)
        split_hi(act, m, S_CTX + n, hi=ctx_slot(m, n)[0])

    context(0)
    context(1)
    act.wait_ge(m.mask_ready, 1)
    for b in range(B):
        if b == 1:
            context(NCH + 1)
        for n in range(b * NCH, (b + 1) * NCH):
            c = n % NCH
            for f in range(KT):
                act.wait_ge(m.k_mm, n * KT + f + 1)
                act.activation(m.k_all[:, f, c * CHUNK:(c + 1) * CHUNK], m.bank[f][:], ACT.Identity,
                               bias=m.cross_vec[:, 1, f:f + 1]).then_inc(m.k_done, 1)
            if c + 2 < NCH or n + 2 == NCH:
                context(n + 2)
        if b == 1:
            act.wait_ge(m.v_mm, B * NCH * KT)
            for s in (S_WO, S_LAYER, S_LAYER + 1):
                split_hi(act, m, s)
        with act.Fori(0, GROUPS) as fb:
            g = fb + b * GROUPS
            n0 = g * HPG * NCH

            def transposed(j, c):
                act.wait_ge(m.pT_mm, n0 + j * NCH + c + 1)
                if j or c > 1:
                    act.wait_ge(m.pv_mm, n0 + j * NCH + c - 1)
                act.activation(m.probs_T[:, 1, :], m.bank[T_BANKS[1]][:], ACT.Copy).then_inc(m.pT_odd, 1)

            for j in range(HPG):
                if j:
                    transposed(j - 1, 1)
                    transposed(j - 1, 3)
                act.wait_ge(m.shift_done, g * HPG + j + 1)
                for c in range(NCH):
                    if j:
                        act.wait_ge(m.pT_mm, n0 + (j - 1) * NCH + c + 1)
                    act.activation(m.probs[:, c, :], m.bank[S_BANKS[c]][:], ACT.Exp, bias=m.shift[:, j:j + 1],
                                   scale=m.q_scale[:, 0:1], accum_out=m.part_sum[:, j, c:c + 1]).then_inc(m.exp_done, 1)
            transposed(HPG - 1, 1)
            transposed(HPG - 1, 3)
            act.wait_ge(m.pv_mm, n0 + HPG * NCH)
            act.activation(m.o_feat[:, :], m.bank[O_BANK][:, 0:P], ACT.Copy).then_inc(m.o_copied, 1)
    for b in range(B):
        act.wait_ge(m.vec_mm, b + 1)
        for k in range(KT):
            act.activation(m.vecT_hi[:, k, b * P:(b + 1) * P], m.bank[b][:, k * P:(k + 1) * P], ACT.Identity,
                           bias=m.cross_vec[:, 2, k:k + 1]).then_inc(m.vec_hi, 1)


def dve_cross(dve, m, step):
    dve.wait_ge(m.x_in, 16)
    for b in range(B):
        ln_scale(dve, m, step, m.x_res[:, b, :], b, 1)
        step.wait()
        ln_apply(dve, m, m.xn[:, b, :], m.x_res[:, b, :], b).then_inc(m.xn_ready, 1)
    dve.wait_ge(m.ident_in, 16)
    dve.tensor_copy(m.ident_r[:], m.ident[:]).then_inc(m.ident_ready, 1)
    for b in range(B):
        dve.wait_ge(m.xT_hi_done, b + 1)
        dve.tensor_tensor(m.xT_lo[:, :, b * P:(b + 1) * P], m.bank[b][:].rearrange("p (k t) -> p k t", k=KT),
                          m.xT_hi[:, :, b * P:(b + 1) * P].bitcast(F32), ALU.subtract).then_inc(m.xT_lo_done, 1)
    dve.wait_ge(m.mask_in, 16)
    dve.tensor_scalar(m.mask_add[:], m.k_all[:, KT - 1, :].bitcast(I32), 0.0, MASKED, ALU.is_equal,
                      ALU.mult).then_inc(m.mask_ready, 1)
    dve.wait_ge(m.mask_ready, 1)
    step.done(dve.tensor_reduce(m.mask_max[:], m.mask_add[:].bitcast(F32), X_AXIS, ALU.max))
    step.wait()
    dve.tensor_scalar(m.q_scale[:], m.mask_max[:], 0.0, X_SCALE, ALU.is_equal, ALU.mult).then_inc(m.q_scale_done, 1)
    dve.wait_ge(m.r_in, 16)
    dve.tensor_copy(m.r_hi[:].rearrange("p k t -> p (k t)"), m.v_all[:, 0, :]).then_inc(m.r_hi_done, 1)
    dve.wait_ge(m.r_hi_done, 1)
    dve.tensor_tensor(m.r_lo[:].rearrange("p k t -> p (k t)"), m.v_all[:, 0, :],
                      m.r_hi[:].rearrange("p k t -> p (k t)").bitcast(F32), ALU.subtract).then_inc(m.r_ready, 1)
    dve.memset(m.qz_hi[:].bitcast(U32), 0)
    dve.memset(m.qz_lo[:].bitcast(U32), 0).then_inc(m.qz_zeroed, 1)
    dve.wait_ge(m.vecs_in2, 16)
    for b in range(B):
        dve.tensor_tensor(m.x_res[:, b, :], m.x_res[:, b, :], m.bo_bc[:], ALU.add).then_inc(m.bo_added, 1)
    dve.wait_ge(m.qz_zeroed, 1)
    dve.wait_ge(m.q_done, KT)
    dve.wait_ge(m.q_scale_done, 1)
    dve.wait_ge(m.r_ready, 1)
    for b in range(B):
        for n in range(b * NCH, (b + 1) * NCH):
            for t in range(KT):
                dve.wait_ge(m.v_mm, n * KT + t + 1)
                dve.tensor_copy(m.v_all[:, (n % NCH) * KT + t, :], m.bank[4 + t][:]).then_inc(m.v_done, 1)
        dve.wait_ge(m.k_done, (b + 1) * NCH * KT)
        dve.wait_ge(m.v_done, (b + 1) * NCH * KT)
        with dve.Fori(0, GROUPS) as fb:
            g = fb + b * GROUPS
            n0 = g * HPG * NCH

            def k_part(c):
                dve.tensor_copy(m.k_hi[:, c, :], m.k_all[:, fb, c * CHUNK:(c + 1) * CHUNK]).then_inc(m.k_hi_done, 1)

            k_part(0)
            for j in range(HPG):
                rows = slice(j * XDH, (j + 1) * XDH)
                dve.tensor_copy(m.qz_hi[rows, j, :], m.q_feat[rows, fb, b * P:(b + 1) * P]).then_inc(m.qz_hi_done, 1)
            for j in range(HPG):
                rows = slice(j * XDH, (j + 1) * XDH)
                dve.wait_ge(m.qz_hi_done, g * HPG + j + 1)
                dve.tensor_tensor(m.qz_lo[rows, j, :], m.q_feat[rows, fb, b * P:(b + 1) * P],
                                  m.qz_hi[rows, j, :].bitcast(F32), ALU.subtract).then_inc(m.qz_done, 1)
            for c in range(1, NCH):
                k_part(c)
            dve.tensor_copy(m.v_grp[:], m.v_all[:, :, bass.ts(fb, P)]).then_inc(m.v_grp_done, 1)

            def transposed(j, c):
                dve.wait_ge(m.pT_mm, n0 + j * NCH + c + 1)
                if j or c:
                    dve.wait_ge(m.pv_mm, n0 + j * NCH + c - 1)
                dve.tensor_copy(m.probs_T[:, 0, :], m.bank[T_BANKS[0]][:]).then_inc(m.pT_even, 1)

            for j in range(HPG):
                for c in range(NCH):
                    dve.wait_ge(m.s_mm, n0 + j * NCH + c + 1)
                    dve.tensor_reduce(m.part_max[:, c:c + 1], m.bank[S_BANKS[c]][:], X_AXIS, ALU.max).then_inc(
                        m.max_done, 1)
                    if j and c % 2 == 0:
                        transposed(j - 1, c)
                dve.wait_ge(m.max_done, n0 + (j + 1) * NCH)
                dve.tensor_reduce(m.neg_max[:], m.part_max[:], X_AXIS, ALU.max, negate=True).then_inc(m.neg_done, 1)
                dve.wait_ge(m.neg_done, g * HPG + j + 1)
                dve.tensor_tensor(m.shift[:, j:j + 1], m.neg_max[:], m.q_scale[:], ALU.mult).then_inc(m.shift_done, 1)
            transposed(HPG - 1, 0)
            transposed(HPG - 1, 2)
            dve.wait_ge(m.exp_done, n0 + HPG * NCH)
            dve.tensor_reduce(m.row_sum[:], m.part_sum[:], X_AXIS, ALU.add).then_inc(m.sum_done, 1)
            dve.wait_ge(m.sum_done, g + 1)
            dve.reciprocal(m.row_inv[:], m.row_sum[:]).then_inc(m.inv_done, 1)
            dve.wait_ge(m.inv_done, g + 1)
            dve.wait_ge(m.oT_mm, g + 1)
            dve.tensor_tensor(m.o_tok[:, b, bass.ts(fb, P)].rearrange("p (h d) -> p h d", h=HPG),
                              m.bank[OT_BANK][:, 0:P].rearrange("p (h d) -> p h d", h=HPG),
                              m.row_inv[:].unsqueeze(2).to_broadcast([P, HPG, XDH]), ALU.mult).then_inc(m.oT_done, 1)
    for b in range(B):
        for k in range(KT):
            dve.wait_ge(m.vec_hi, (b + 1) * KT)
            dve.scalar_tensor_tensor(m.vecT_lo[:, k, b * P:(b + 1) * P], m.bank[b][:, k * P:(k + 1) * P],
                                     m.cross_vec[:, 2, k:k + 1], m.vecT_hi[:, k, b * P:(b + 1) * P].bitcast(F32),
                                     ALU.add, ALU.subtract).then_inc(m.vec_lo, 1)
    dve.wait_ge(m.bo_added, B)
    for b in range(B):
        dve.wait_ge(m.o_mm, b + 1)
        dve.tensor_tensor(m.x_res[:, b, :], m.bank[2 + b][:], m.x_res[:, b, :], ALU.add).then_inc(m.x1_done, 1)


def pe_transpose4(pe, m, bank, blocks, identity):
    for t, src in enumerate(blocks):
        last = pe.transpose(bank[:, t * P:(t + 1) * P], src, identity)
    return last


def pe_cross(pe, m):
    pe.wait_ge(m.ident_in, 16)
    for b in range(B):
        pe.wait_ge(m.xn_ready, b + 1)
        pe_transpose4(pe, m, m.bank[b], [m.xn[:, b, k * P:(k + 1) * P] for k in range(KT)], m.ident[:]).then_inc(
            m.xnT_mm, 1)
    wait_unit(pe, m.lo_done, S_WQ)
    pe.wait_ge(m.xT_lo_done, B)
    for f in range(KT):
        for k in range(KT):
            last = three_passes(pe, m.bank[2 + f // 2][:, (f % 2) * B * P:(f % 2 + 1) * B * P],
                                m.w_hi[0][:, k, f * P:(f + 1) * P], m.w_lo[0][:, k, f * P:(f + 1) * P],
                                m.xT_hi[:, k, :], m.xT_lo[:, k, :], k == 0, k == KT - 1)
        if f % 2:
            last.then_inc(m.q_mm, 1)
    for b in range(B):
        for n in range(b * NCH, (b + 1) * NCH):
            c_hi, c_lo = ctx_slot(m, n)
            wait_unit(pe, m.lo_done, S_CTX + n)
            if n == 0:
                wait_unit(pe, m.lo_done, S_WK)
                wait_unit(pe, m.lo_done, S_WV)
                pe.wait_ge(m.q_done, KT)
            for f in range(KT):
                if n % NCH:
                    pe.wait_ge(m.k_done, (n - 1) * KT + f + 1)
                for k in range(KT):
                    last = three_passes(pe, m.bank[f][:], m.w_hi[1][:, k, f * P:(f + 1) * P],
                                        m.w_lo[1][:, k, f * P:(f + 1) * P], c_hi[:, k, :], c_lo[:, k, :],
                                        k == 0, k == KT - 1)
                last.then_inc(m.k_mm, 1)
            if n == NCH:
                pe.wait_ge(m.oT_done, GROUPS)
            for t in range(KT):
                if n % NCH:
                    pe.wait_ge(m.v_done, (n - 1) * KT + t + 1)
                for k in range(KT):
                    last = three_passes(pe, m.bank[4 + t][:], c_hi[:, k, t * P:(t + 1) * P],
                                        c_lo[:, k, t * P:(t + 1) * P], m.w_hi[2][:, k, :], m.w_lo[2][:, k, :],
                                        k == 0, k == KT - 1)
                last.then_inc(m.v_mm, 1)
        pe.wait_ge(m.k_done, (b + 1) * NCH * KT)
        pe.wait_ge(m.v_done, (b + 1) * NCH * KT)
        pe.wait_ge(m.mask_ready, 1)
        pe.wait_ge(m.ident_ready, 1)
        with pe.Fori(0, GROUPS) as fb:
            g = fb + b * GROUPS
            n0 = g * HPG * NCH

            def scores(j, c):
                if j == 0:
                    pe.wait_ge(m.k_lo_done, g * NCH + c + 1)
                    if c == 0:
                        pe.wait_ge(m.qz_done, (g + 1) * HPG)
                else:
                    pe.wait_ge(m.exp_done, n0 + (j - 1) * NCH + c + 1)
                bank = m.bank[S_BANKS[c]][:]
                pe.matmul(bank, m.ident_r[:], m.mask_add[:, c * CHUNK:(c + 1) * CHUNK], start=True, stop=False)
                three_passes(pe, bank, m.qz_hi[:, j, :], m.qz_lo[:, j, :], m.k_hi[:, c, :], m.k_lo[:, c, :],
                             False, True).then_inc(m.s_mm, 1)

            def transposed(j, c):
                pe.wait_ge(m.exp_done, n0 + j * NCH + c + 1)
                if j or c >= 2:
                    pe.wait_ge((m.pT_even, m.pT_odd)[c % 2], (g * HPG + j) * 2 + c // 2)
                pe_transpose4(pe, m, m.bank[T_BANKS[c % 2]], [m.probs[:, c, t * P:(t + 1) * P] for t in range(KT)],
                              m.ident[:]).then_inc(m.pT_mm, 1)

            def values(j, c):
                if j == 0 and c == 0:
                    pe.wait_ge(m.v_grp_done, g + 1)
                pe.wait_ge((m.pT_even, m.pT_odd)[c % 2], (g * HPG + j) * 2 + c // 2 + 1)
                rows = slice(j * XDH, (j + 1) * XDH)
                for t in range(KT):
                    last = pe.matmul(m.bank[O_BANK][rows, 0:P], m.v_grp[:, c * KT + t, rows],
                                     m.probs_T[:, c % 2, t * P:(t + 1) * P], start=(c == 0 and t == 0),
                                     stop=(c == NCH - 1 and t == KT - 1), tile_position=(0, j * XDH))
                last.then_inc(m.pv_mm, 1)

            for j in range(HPG):
                for c in range(NCH):
                    scores(j, c)
                    if j:
                        transposed(j - 1, c)
                        if c:
                            values(j - 1, c - 1)
                if j:
                    values(j - 1, NCH - 1)
            for c in range(NCH):
                transposed(HPG - 1, c)
                if c:
                    values(HPG - 1, c - 1)
            values(HPG - 1, NCH - 1)
            pe.wait_ge(m.o_copied, g + 1)
            pe.transpose(m.bank[OT_BANK][:, 0:P], m.o_feat[:], m.ident[:]).then_inc(m.oT_mm, 1)
    pe.wait_ge(m.oT_done, B * GROUPS)
    for b in range(B):
        pe_transpose4(pe, m, m.bank[b], [m.o_tok[:, b, k * P:(k + 1) * P] for k in range(KT)], m.ident[:]).then_inc(
            m.vec_mm, 1)
    wait_unit(pe, m.lo_done, S_WO)
    slot = S_WO % RING
    for b in range(B):
        pe.wait_ge(m.vec_lo, (b + 1) * KT)
        for k in range(KT):
            last = three_passes(pe, m.bank[2 + b][:], m.vecT_hi[:, k, b * P:(b + 1) * P],
                                m.vecT_lo[:, k, b * P:(b + 1) * P], m.w_hi[slot][:, k, :], m.w_lo[slot][:, k, :],
                                k == 0, k == KT - 1)
        last.then_inc(m.o_mm, 1)


ROW_G1, ROW_B1, ROW_BF, ROW_G2, ROW_B2 = range(5)
SG = 8
KR_BANKS, HT_BANKS = (4, 5), (0, 1)
Q_BANKS, K_BANKS, V_BANKS = (6, 7, 2, 3), (0, 1, 4, 5), (6, 7, 2, 3)
SC_BANKS, PT_BANKS, PV_BANKS = (0, 1, 4, 5), (6, 7), (2, 3)
WO_BANKS, H1T_BANKS, FF1_BANKS, FF2_BANKS = (0, 1), (4, 5), (6, 7, 2, 3), (0, 1)
FF1_OUTS = DF // (2 * P)


def layer_memory(m):
    m.rows = m.sb("rows", [P, 5, D])
    m.h_tok = m.sb("h_tok", [P, B, D])
    m.s_tok = m.sb("s_tok", [P, B, D])
    m.hT_hi = m.sb("hT_hi", [P, KT, B * P], F32R)
    m.hT_lo = m.sb("hT_lo", [P, KT, B * P], F32R)
    m.v_tok = m.sb("v_tok", [P, B, H * DH])
    m.p_lay = m.sb("p_lay", [P, SG, CHUNK])
    m.pT_lay = m.sb("pT_lay", [P, 2, CHUNK])
    m.max_lay = m.sb("max_lay", [P, SG, 4])
    m.shift_lay = m.sb("shift_lay", [P, SG, 4])
    m.sum_lay = m.sb("sum_lay", [P, SG, 4])
    m.inv_lay = m.sb("inv_lay", [P, SG, 4])
    m.vT_hi = m.sb("vT_hi", [P, H // 2, B * P], F32R)
    m.vT_lo = m.sb("vT_lo", [P, H // 2, B * P], F32R)
    m.ff_t = m.sb("ff_t", [P, 2, CHUNK])
    outer = m.ctx
    with ExitStack() as m.ctx:
        m.q_stack = m.sb("q_stack", [P, H, B * P])
        m.k_stack = m.sb("k_stack", [P, H, B * P])
    with ExitStack() as m.ctx:
        m.ff_hi = m.sb("ff_hi", [P, DF // P, B * P], F32R)
        m.ff_lo = m.sb("ff_lo", [P, DF // P, B * P], F32R)
    m.ctx = outer
    (m.rows_in, m.wo_half, m.ff2_part, m.h_ready, m.hT_mm, m.hT_hi_done, m.hT_lo_done, m.kr_mm, m.kr_tok_done, m.krT_mm, m.kr_act,
     m.kr_dve, m.lq_mm, m.lq_act, m.lq_dve, m.lk_mm, m.lk_act, m.lk_dve, m.lv_mm, m.lv_act, m.lv_dve,
     m.sc_mm, m.lmax_done, m.lshift_done, m.lexp_done, m.linv_done, m.lnorm_done, m.lpT_mm, m.lpT_even,
     m.lpT_odd, m.lpv_mm, m.vT_hi_done, m.vT_lo_done, m.wo_mm, m.h1_ready, m.h1T_mm, m.h1T_hi, m.h1T_lo,
     m.ff1_mm, m.relu_done, m.ff_hi_done, m.ff_lo_done, m.ff2_mm, m.dve_step_l, m.x2_done) = m.sems(
        "rows_in wo_half ff2_part h_ready hT_mm hT_hi_done hT_lo_done kr_mm kr_tok_done krT_mm kr_act kr_dve lq_mm lq_act "
        "lq_dve lk_mm lk_act lk_dve lv_mm lv_act lv_dve sc_mm lmax_done lshift_done lexp_done linv_done "
        "lnorm_done lpT_mm lpT_even lpT_odd lpv_mm vT_hi_done vT_lo_done wo_mm h1_ready h1T_mm h1T_hi "
        "h1T_lo ff1_mm relu_done ff_hi_done ff_lo_done ff2_mm dve_step_l x2_done")


def sp_layers(sp, m):
    sp.wait_ge(m.uv_in, 16)
    with sp.Fori(0, L) as i:
        for k in range(RING, LU + RING):
            wait_unit(sp, m.lo_done, S_LAYER + k - RING, i, LU)
            sp.dma_start(m.raw[:, k % RING, :], m.dram["w_stream"][bass.ds(i * LU + k, 1)].rearrange(
                "a p n -> (a p) n")).then_inc(m.loaded[k % RING], 16)
            if k == U_WK:
                sp.wait_ge(m.h_ready, (i + 1) * B)
                sp.dma_start(m.rows[:], m.dram["layer_rows"][bass.ds(i, 1)].rearrange(
                    "a r d -> (a r) d").partition_broadcast(P)).then_inc(m.rows_in, 16)


def pool_layers(pool, m):
    split_lo(pool, m, S_LAYER + 2)
    with pool.Fori(0, L) as i:
        for k in range(RING, LU + RING):
            split_lo(pool, m, S_LAYER + k, i, LU)


def by_block(bank):
    return bank[:].rearrange("p (k t) -> p k t", t=P)


def pairs(bank):
    return bank[:].rearrange("p (k t) -> p k t", t=B * P)


def act_layers(act, m):
    act.wait_ge(m.o_mm, B)
    split_hi(act, m, S_LAYER + 2)
    ln_root(act, m, 2)
    act.wait_ge(m.uv_in, 16)
    act.wait_ge(m.bias_in, 16)
    with act.Fori(0, L) as i:

        def unit(k):
            act.wait_ge(*unit_used(m, k - RING, i))
            split_hi(act, m, S_LAYER + k, i, LU)

        for u in range(2):
            act.wait_ge(m.kr_mm, i * 2 + u + 1)
            act.activation(m.ff_t[:, u, :], m.bank[KR_BANKS[u]][:], ACT.Copy).then_inc(m.kr_tok_done, 1)
            unit(RING + u)
        for b in range(B):
            act.wait_ge(m.hT_mm, i * B + b + 1)
            act.activation(m.hT_hi[:, :, b * P:(b + 1) * P], by_block(m.bank[HT_BANKS[b]]), ACT.Copy).then_inc(
                m.hT_hi_done, 1)
        for u in range(2):
            act.wait_ge(m.krT_mm, i * 2 + u + 1)
            for b in range(B):
                last = act.activation(m.k_stack[DH:P, 8 * u + 1:8 * u + 8:2, b * P:(b + 1) * P],
                                      by_block(m.bank[KR_BANKS[u]])[DH:P], ACT.Copy)
            last.then_inc(m.kr_act, 1)
        for o in range(4):
            act.wait_ge(m.lq_mm, i * 4 + o + 1)
            for t in range(2):
                head = 4 * o + 2 * t + 1
                for w in range(2):
                    last = act.activation(m.q_stack[w * DH:(w + 1) * DH, head, :],
                                          pairs(m.bank[Q_BANKS[o]])[DH:P, t, :], ACT.Identity,
                                          bias=m.uv_sb[DH:P, w, head:head + 1])
            last.then_inc(m.lq_act, 1)
            if o % 2:
                unit(5 + o // 2)
        for o in range(4):
            act.wait_ge(m.lk_mm, i * 4 + o + 1)
            act.activation(m.k_stack[0:DH, 4 * o + 1:4 * o + 4:2, :], pairs(m.bank[K_BANKS[o]])[DH:P],
                           ACT.Copy).then_inc(m.lk_act, 1)
            if o % 2:
                unit(7 + o // 2)
        def values(u):
            act.wait_ge(m.lv_mm, i * 4 + 2 * u + 2)
            act.activation(m.v_tok[:, 1, u * CHUNK:(u + 1) * CHUNK], m.bank[V_BANKS[2 * u + 1]][:],
                           ACT.Copy).then_inc(m.lv_act, 1)
            unit(9 + u)

        def exps(g):
            act.wait_ge(m.lshift_done, i * SG + g + 1)
            for t in range(4):
                last = act.activation(m.p_lay[:, g, t * P:(t + 1) * P],
                                      m.bank[SC_BANKS[g % 4]][:, t * P:(t + 1) * P], ACT.Exp,
                                      bias=m.shift_lay[:, g, t:t + 1], scale=L_SCALE, accum_out=m.sum_lay[:, g, t:t + 1])
            last.then_inc(m.lexp_done, 1)

        def transposed(g):
            act.wait_ge(m.lpT_mm, i * SG + g + 1)
            if g >= 2:
                act.wait_ge(m.lpv_mm, i * SG + g - 1)
            act.activation(m.pT_lay[:, 1, :], m.bank[PT_BANKS[1]][:], ACT.Copy).then_inc(m.lpT_odd, 1)

        def vector_hi(q):
            b, half = q // 2, q % 2
            act.wait_ge(m.lpv_mm, i * SG + 2 * q + 2)
            act.activation(m.vT_hi[:, 4 * half:4 * half + 4, b * P:(b + 1) * P], by_block(m.bank[PV_BANKS[half]]),
                           ACT.Copy).then_inc(m.vT_hi_done, 1)

        exps(0)
        exps(1)
        values(0)
        for g in range(2, 6):
            exps(g)
        values(1)
        exps(6)
        transposed(1)
        exps(7)
        transposed(3)
        vector_hi(0)
        transposed(5)
        vector_hi(1)
        transposed(7)
        vector_hi(2)
        vector_hi(3)
        unit(11)
        ln_root(act, m, i * 2 + 3)
        unit(12)
        for b in range(B):
            act.wait_ge(m.h1T_mm, i * B + b + 1)
            act.activation(m.hT_hi[:, :, b * P:(b + 1) * P], by_block(m.bank[H1T_BANKS[b]]), ACT.Copy).then_inc(
                m.h1T_hi, 1)
        for f in range(FF1_OUTS):
            act.wait_ge(m.ff1_mm, i * FF1_OUTS + f + 1)
            if f >= 2:
                act.wait_ge(m.ff_lo_done, i * FF1_OUTS + f - 1)
            for t in range(2):
                last = act.activation(m.ff_t[:, f % 2, t * B * P:(t + 1) * B * P], pairs(m.bank[FF1_BANKS[f % 4]])[:, t, :],
                                      ACT.Relu, bias=m.ff1_bias_sb[:, bass.ds(i, 1), 2 * f + t])
            last.then_inc(m.relu_done, 1)
            if f % 2:
                unit(13 + f // 2)
        for k in range(17, 20):
            unit(k)
        ln_root(act, m, i * 2 + 4)
        unit(20)


def dve_layers(dve, m, step):
    dve.wait_ge(m.x1_done, B)
    for b in range(B):
        ln_scale(dve, m, step, m.x_res[:, b, :], b, 2)
        step.wait()
        ln_apply(dve, m, m.h_tok[:, b, :], m.x_res[:, b, :], b).then_inc(m.h_ready, 1)
    dve.wait_ge(m.uv_in, 16)
    with dve.Fori(0, L) as i:
        own = Step(dve, m.dve_step_l, 0, i, 32)
        for b in range(B):
            dve.wait_ge(m.hT_hi_done, i * B + b + 1)
            dve.tensor_tensor(m.hT_lo[:, :, b * P:(b + 1) * P], by_block(m.bank[HT_BANKS[b]]),
                              m.hT_hi[:, :, b * P:(b + 1) * P].bitcast(F32), ALU.subtract).then_inc(m.hT_lo_done, 1)
        for u in range(2):
            dve.wait_ge(m.krT_mm, i * 2 + u + 1)
            for b in range(B):
                last = dve.tensor_copy(m.k_stack[DH:P, 8 * u:8 * u + 8:2, b * P:(b + 1) * P],
                                       by_block(m.bank[KR_BANKS[u]])[0:DH])
            last.then_inc(m.kr_dve, 1)
        for o in range(4):
            dve.wait_ge(m.lq_mm, i * 4 + o + 1)
            heads = slice(4 * o, 4 * o + 4, 2)
            for w in range(2):
                last = dve.tensor_tensor(m.q_stack[w * DH:(w + 1) * DH, heads, :], pairs(m.bank[Q_BANKS[o]])[0:DH],
                                         m.uv_sb[0:DH, w, heads].unsqueeze(2).to_broadcast([DH, 2, B * P]), ALU.add)
            last.then_inc(m.lq_dve, 1)
        for o in range(4):
            dve.wait_ge(m.lk_mm, i * 4 + o + 1)
            dve.tensor_copy(m.k_stack[0:DH, 4 * o:4 * o + 4:2, :], pairs(m.bank[K_BANKS[o]])[0:DH]).then_inc(
                m.lk_dve, 1)
        def values(u):
            dve.wait_ge(m.lv_mm, i * 4 + 2 * u + 1)
            dve.tensor_copy(m.v_tok[:, 0, u * CHUNK:(u + 1) * CHUNK], m.bank[V_BANKS[2 * u]][:]).then_inc(m.lv_dve, 1)

        def maxima(g):
            dve.wait_ge(m.sc_mm, i * SG + g + 1)
            dve.tensor_reduce(m.max_lay[:, g, :], by_block(m.bank[SC_BANKS[g % 4]]), X_AXIS, ALU.max,
                              negate=True).then_inc(m.lmax_done, 1)
            dve.wait_ge(m.lmax_done, i * SG + g + 1)
            dve.tensor_scalar(m.shift_lay[:, g, :], m.max_lay[:, g, :], L_SCALE, None, ALU.mult).then_inc(
                m.lshift_done, 1)

        def normed(g):
            dve.wait_ge(m.lexp_done, i * SG + g + 1)
            dve.reciprocal(m.inv_lay[:, g, :], m.sum_lay[:, g, :]).then_inc(m.linv_done, 1)
            dve.wait_ge(m.linv_done, i * SG + g + 1)
            p = m.p_lay[:, g, :].rearrange("p (h t) -> p h t", h=4)
            dve.tensor_tensor(p, p, m.inv_lay[:, g, :].unsqueeze(2).to_broadcast([P, 4, P]), ALU.mult).then_inc(
                m.lnorm_done, 1)

        def transposed(g):
            dve.wait_ge(m.lpT_mm, i * SG + g + 1)
            if g >= 2:
                dve.wait_ge(m.lpv_mm, i * SG + g - 1)
            dve.tensor_copy(m.pT_lay[:, 0, :], m.bank[PT_BANKS[0]][:]).then_inc(m.lpT_even, 1)

        def vector_lo(q):
            b, half = q // 2, q % 2
            dve.wait_ge(m.vT_hi_done, i * 4 + q + 1)
            hi = m.vT_hi[:, 4 * half:4 * half + 4, b * P:(b + 1) * P]
            dve.tensor_tensor(m.vT_lo[:, 4 * half:4 * half + 4, b * P:(b + 1) * P], by_block(m.bank[PV_BANKS[half]]),
                              hi.bitcast(F32), ALU.subtract).then_inc(m.vT_lo_done, 1)

        values(0)
        for g in range(0, SG, 2):
            if g == 4:
                values(1)
            maxima(g)
            maxima(g + 1)
            if g == 6:
                transposed(0)
                transposed(2)
            normed(g)
            normed(g + 1)
        vector_lo(0)
        transposed(4)
        vector_lo(1)
        transposed(6)
        vector_lo(2)
        vector_lo(3)

        def layer_norm(dst, t, n, g, b, sem):
            src = m.s_tok[:, t, :]
            own.wait()
            ln_scale(dve, m, own, src, t, n)
            own.done(dve.scalar_tensor_tensor(src, src, m.mean_var[:, t, 0:1], m.rows[:, g, :], ALU.subtract, ALU.mult))
            own.wait()
            dve.scalar_tensor_tensor(dst[:, t, :], src, m.rstd[:, t:t + 1], m.rows[:, b, :], ALU.mult, ALU.add).then_inc(
                sem, 1)

        dve.wait_ge(m.rows_in, i * 16 + 16)
        dve.wait_ge(m.h_ready, (i + 1) * B)
        for b in range(B):
            dve.wait_ge(m.wo_mm, i * B + b + 1)
            own.done(dve.tensor_tensor(m.s_tok[:, b, :], m.bank[WO_BANKS[b]][:], m.h_tok[:, b, :], ALU.add))
            layer_norm(m.s_tok, b, i * 2 + 3, ROW_G1, ROW_B1, m.h1_ready)
        for b in range(B):
            dve.wait_ge(m.h1T_hi, i * B + b + 1)
            dve.tensor_tensor(m.hT_lo[:, :, b * P:(b + 1) * P], by_block(m.bank[H1T_BANKS[b]]),
                              m.hT_hi[:, :, b * P:(b + 1) * P].bitcast(F32), ALU.subtract).then_inc(m.h1T_lo, 1)
        for f in range(FF1_OUTS):
            dve.wait_ge(m.relu_done, i * FF1_OUTS + f + 1)
            hi = m.ff_hi[:, 2 * f:2 * f + 2, :].rearrange("p k t -> p (k t)")
            dve.tensor_copy(hi, m.ff_t[:, f % 2, :]).then_inc(m.ff_hi_done, 1)
            dve.wait_ge(m.ff_hi_done, i * FF1_OUTS + f + 1)
            dve.tensor_tensor(m.ff_lo[:, 2 * f:2 * f + 2, :].rearrange("p k t -> p (k t)"), m.ff_t[:, f % 2, :],
                              hi.bitcast(F32), ALU.subtract).then_inc(m.ff_lo_done, 1)
        for b in range(B):
            dve.wait_ge(m.ff2_mm, i * B + b + 1)
            own.done(dve.tensor_tensor(m.s_tok[:, b, :], m.bank[FF2_BANKS[b]][:], m.rows[:, ROW_BF, :], ALU.add))
            layer_norm(m.h_tok, b, i * 2 + 4, ROW_G2, ROW_B2, m.h_ready)
        assert own.n == own.per, own.n
    dve.wait_ge(m.h_ready, (L + 1) * B)
    for b in range(B):
        dve.tensor_tensor(m.x_res[:, b, :], m.x_res[:, b, :], m.h_tok[:, b, :], ALU.add).then_inc(m.x2_done, 1)


def unit_used(m, u, i):
    if u < U_WQ:
        return m.kr_mm, i * 2 + u + 1
    if u < U_WO:
        return (m.lq_mm, m.lk_mm, m.lv_mm)[(u - U_WQ) // 2], i * 4 + 2 * (u % 2) + 2
    if u < U_FF1:
        return (m.wo_half, i + 1) if u == U_WO else (m.wo_mm, i * B + B)
    if u < U_FF2:
        return m.ff1_mm, i * FF1_OUTS + 2 * (u - U_FF1) + 2
    return (m.ff2_part, i * 3 + u - U_FF2 + 1) if u < LU - 1 else (m.ff2_mm, i * B + B)


def pe_layers(pe, m):
    wait_unit(pe, m.lo_done, S_WO)
    pe.wait_ge(m.x1_done, B)
    pe.wait_ge(m.r_ready, 1)
    with pe.Fori(0, L) as i:

        def unit(k):
            wait_unit(pe, m.lo_done, S_LAYER + k, i, LU)
            return m.w_hi[k % RING], m.w_lo[k % RING]

        for u in range(2):
            w_hi, w_lo = unit(U_WR + u)
            for k in range(KT):
                last = three_passes(pe, m.bank[KR_BANKS[u]][:], m.r_hi[:, k, :], m.r_lo[:, k, :], w_hi[:, k, :],
                                    w_lo[:, k, :], k == 0, k == KT - 1)
            last.then_inc(m.kr_mm, 1)

        def position_keys(u):
            pe.wait_ge(m.kr_tok_done, i * 2 + u + 1)
            pe_transpose4(pe, m, m.bank[KR_BANKS[u]], [m.ff_t[:, u, t * P:(t + 1) * P] for t in range(4)],
                          m.ident[:]).then_inc(m.krT_mm, 1)

        position_keys(0)
        for b in range(B):
            pe.wait_ge(m.h_ready, i * B + b + 1)
            pe_transpose4(pe, m, m.bank[HT_BANKS[b]], [m.h_tok[:, b, k * P:(k + 1) * P] for k in range(KT)],
                          m.ident[:]).then_inc(m.hT_mm, 1)
        position_keys(1)
        pe.wait_ge(m.hT_lo_done, (i + 1) * B)

        def by_feature(unit0, banks, sem, free):
            for o in range(4):
                if o % 2 == 0:
                    w_hi, w_lo = unit(unit0 + o // 2)
                free(o)
                for q in range(2):
                    cols = slice((2 * (o % 2) + q) * P, (2 * (o % 2) + q + 1) * P)
                    for k in range(KT):
                        last = three_passes(pe, m.bank[banks[o]][:, q * B * P:(q + 1) * B * P], w_hi[:, k, cols],
                                            w_lo[:, k, cols], m.hT_hi[:, k, :], m.hT_lo[:, k, :],
                                            k == 0, k == KT - 1)
                last.then_inc(sem, 1)

        def k_bank_free(o):
            if o >= 2:
                pe.wait_ge(m.kr_dve, i * 2 + o - 1)
                pe.wait_ge(m.kr_act, i * 2 + o - 1)

        by_feature(U_WQ, Q_BANKS, m.lq_mm, lambda o: None)
        by_feature(U_WK, K_BANKS, m.lk_mm, k_bank_free)

        def value_rows(u, b):
            w_hi, w_lo = unit(U_WV + u)
            pe.wait_ge(m.lq_act, i * 4 + 2 * u + b + 1)
            pe.wait_ge(m.lq_dve, i * 4 + 2 * u + b + 1)
            for k in range(KT):
                last = three_passes(pe, m.bank[V_BANKS[2 * u + b]][:], m.hT_hi[:, k, b * P:(b + 1) * P],
                                    m.hT_lo[:, k, b * P:(b + 1) * P], w_hi[:, k, :], w_lo[:, k, :],
                                    k == 0, k == KT - 1)
            last.then_inc(m.lv_mm, 1)

        def scores(g):
            if g == 0:
                pe.wait_ge(m.lk_act, i * 4 + 4)
                pe.wait_ge(m.lk_dve, i * 4 + 4)
            if g >= 4:
                pe.wait_ge(m.lexp_done, i * SG + g - 3)
            b = g // 4
            for t in range(4):
                head = 4 * (g % 4) + t
                last = pe.matmul(m.bank[SC_BANKS[g % 4]][:, t * P:(t + 1) * P], m.q_stack[:, head, b * P:(b + 1) * P],
                                 m.k_stack[:, head, b * P:(b + 1) * P], start=True, stop=True)
            last.then_inc(m.sc_mm, 1)

        def transposed(g):
            pe.wait_ge(m.lnorm_done, i * SG + g + 1)
            if g < 2:
                pe.wait_ge((m.lv_dve, m.lv_act)[g], i * 2 + 1)
            else:
                pe.wait_ge((m.lpT_even, m.lpT_odd)[g % 2], i * 4 + g // 2)
            pe_transpose4(pe, m, m.bank[PT_BANKS[g % 2]], [m.p_lay[:, g, t * P:(t + 1) * P] for t in range(4)],
                          m.ident[:]).then_inc(m.lpT_mm, 1)

        def values(g):
            pe.wait_ge((m.lpT_even, m.lpT_odd)[g % 2], i * 4 + g // 2 + 1)
            half, b = (g % 4) // 2, g // 4
            if g == 0:
                pe.wait_ge(m.lv_dve, i * 2 + 2)
                pe.wait_ge(m.lv_act, i * 2 + 2)
            if g >= 4:
                pe.wait_ge(m.vT_lo_done, i * 4 + half + 1)
            for t in range(4):
                head = 4 * (g % 4) + t
                side, block = head % 2, (head // 2) % 4
                last = pe.matmul(m.bank[PV_BANKS[half]][side * DH:(side + 1) * DH, block * P:(block + 1) * P],
                                 m.v_tok[:, b, head * DH:(head + 1) * DH], m.pT_lay[:, g % 2, t * P:(t + 1) * P],
                                 start=True, stop=True, tile_position=(0, side * DH))
            last.then_inc(m.lpv_mm, 1)

        for pair in range(4):
            value_rows(pair // 2, pair % 2)
            scores(2 * pair)
            scores(2 * pair + 1)
        transposed(0)
        for g in range(SG):
            if g + 1 < SG:
                transposed(g + 1)
            values(g)
        for u in range(2):
            w_hi, w_lo = unit(U_WO + u)
            for b in range(B):
                pe.wait_ge(m.vT_lo_done, i * 4 + 2 * b + 2)
                for k in range(KT):
                    last = three_passes(pe, m.bank[WO_BANKS[b]][:], m.vT_hi[:, KT * u + k, b * P:(b + 1) * P],
                                        m.vT_lo[:, KT * u + k, b * P:(b + 1) * P], w_hi[:, k, :], w_lo[:, k, :],
                                        u == 0 and k == 0, u == 1 and k == KT - 1)
                if u == 1:
                    last.then_inc(m.wo_mm, 1)
            if u == 0:
                last.then_inc(m.wo_half, 1)
        for b in range(B):
            pe.wait_ge(m.h1_ready, i * B + b + 1)
            pe_transpose4(pe, m, m.bank[H1T_BANKS[b]], [m.s_tok[:, b, k * P:(k + 1) * P] for k in range(KT)],
                          m.ident[:]).then_inc(m.h1T_mm, 1)
        pe.wait_ge(m.h1T_lo, (i + 1) * B)
        for f in range(FF1_OUTS):
            if f % 2 == 0:
                w_hi, w_lo = unit(U_FF1 + f // 2)
            if f >= 4:
                pe.wait_ge(m.relu_done, i * FF1_OUTS + f - 3)
            for q in range(2):
                cols = slice((2 * (f % 2) + q) * P, (2 * (f % 2) + q + 1) * P)
                for k in range(KT):
                    last = three_passes(pe, m.bank[FF1_BANKS[f % 4]][:, q * B * P:(q + 1) * B * P], w_hi[:, k, cols],
                                        w_lo[:, k, cols], m.hT_hi[:, k, :], m.hT_lo[:, k, :], k == 0, k == KT - 1)
            last.then_inc(m.ff1_mm, 1)
        for u in range(4):
            w_hi, w_lo = unit(U_FF2 + u)
            pe.wait_ge(m.ff_lo_done, i * FF1_OUTS + 2 * u + 2)
            for b in range(B):
                for k in range(KT):
                    last = three_passes(pe, m.bank[FF2_BANKS[b]][:], m.ff_hi[:, KT * u + k, b * P:(b + 1) * P],
                                        m.ff_lo[:, KT * u + k, b * P:(b + 1) * P], w_hi[:, k, :], w_lo[:, k, :],
                                        u == 0 and k == 0, u == 3 and k == KT - 1)
                if u == 3:
                    last.then_inc(m.ff2_mm, 1)
            if u < 3:
                last.then_inc(m.ff2_part, 1)


EXTRA = (B * P * 2 - 1) // (P + 1)
TURNS = E + EXTRA + 1
QUARTERS = F // CHUNK
E_RING = 2 * RING
UP_UNITS = [k for k, (name, _) in enumerate(E_ORDER) if name != "wo"]
DOWN_UNITS = [k for k, (name, _) in enumerate(E_ORDER) if name == "wo"]
UP_BANKS, HIDDEN_BANK, Y_BANK, XG_BANKS = (0, 2), 4, 5, (6, 7)
BELOW_ALL = -3e38


def moe_memory(m):
    m.xn_tok = m.sb("xn_tok", [P, B, D])
    m.xn_hi = m.sb("xn_hi", [P, B, D], F32R)
    m.xn_lo = m.sb("xn_lo", [P, B, D], F32R)
    m.xn_T = m.sb("xn_T", [P, KT, B * P])
    m.logits = m.sb("logits", [P, B, E])
    m.is_max = m.sb("is_max", [P, B, E])
    m.candidate = m.sb("candidate", [P, B, E])
    m.chosen1 = m.sb("chosen1", [P, B, E])
    m.chosen2 = m.sb("chosen2", [P, B, E])
    m.rest = m.sb("rest", [P, B, E])
    m.routed = m.sb("routed", [P, B, E])
    m.weighted1 = m.sb("weighted1", [P, B, E])
    m.position = m.sb("position", [P, B, E])
    m.product = m.sb("product", [P, B, E])
    m.best1 = m.sb("best1", [P, B])
    m.best2 = m.sb("best2", [P, B])
    m.first1 = m.sb("first1", [P, B])
    m.first2 = m.sb("first2", [P, B])
    m.gap = m.sb("gap", [P, B])
    m.gap_exp = m.sb("gap_exp", [P, B])
    m.gap_sum = m.sb("gap_sum", [P, B])
    m.weight1 = m.sb("weight1", [P, B])
    m.weight2 = m.sb("weight2", [P, B])
    m.slot_of = m.sb("slot_of", [P, B, TURNS])
    m.gate_of = m.sb("gate_of", [P, B, TURNS])
    m.crowded = m.sb("crowded", [P, EXTRA + 1, E])
    m.order = m.sb("order", [P, E])
    m.first_one = m.sb("first_one", [P, 1])
    m.extra = m.sb("extra", [P, EXTRA, E])
    m.extra_index = m.sb("extra_index", [P, EXTRA, E])
    m.n_crowded = m.sb("n_crowded", [P, 1])
    m.n_turns = m.sb("n_turns", [P, 1], I32)
    m.expert_f = m.sb("expert_f", [P, TURNS])
    m.expert_of = m.sb("expert_of", [P, TURNS], I32)
    more = range(RING, E_RING)
    m.raw_more = m.sb("raw_more", [P, RING, KT * CHUNK])
    m.e_raw = [m.raw[:, s, :] for s in range(RING)] + [m.raw_more[:, s, :] for s in range(RING)]
    m.e_hi = m.w_hi + [m.sb(f"w_hi{s}", [P, KT, CHUNK], F32R) for s in more]
    m.e_lo = m.w_lo + [m.sb(f"w_lo{s}", [P, KT, CHUNK], F32R) for s in more]
    m.e_loaded = m.loaded + m.slot_sems("loaded_more")
    m.e_hi_done = m.hi_done + m.slot_sems("hi_done_more")
    m.e_lo_done = m.lo_done + m.slot_sems("lo_done_more")
    m.pick = m.sb("pick", [P, B, P], F32R)
    m.pick_gate = m.sb("pick_gate", [P, B, P])
    m.pick_gate_T = m.sb("pick_gate_T", [P, B, P])
    m.xg_hi = m.sb("xg_hi", [P, KT, P], F32R)
    m.xg_lo = m.sb("xg_lo", [P, KT, P], F32R)
    m.silu = m.sb("silu", [P, 2, CHUNK])
    m.hidden = m.sb("hidden", [P, 2, CHUNK])
    m.hidden_hi = m.sb("hidden_hi", [P, 2, CHUNK], F32R)
    m.hidden_lo = m.sb("hidden_lo", [P, 2, CHUNK], F32R)
    m.y = m.sb("y", [P, D])
    (m.xn2_ready, m.xn2_hi, m.xn2_lo, m.xn2_mm, m.xn2_T, m.logit_mm, m.gap_done, m.gap_exp_done,
     m.routed_done, m.rank_mm, m.n_ready, m.pick_done, m.gather_mm, m.xg_hi_done, m.xg_lo_done,
     m.gateT_mm, m.gateT_done, m.up_mm, m.silu_done, m.hidden_done, m.hiddenT_mm, m.hidden_hi_done,
     m.hidden_lo_done, m.down_mm, m.y_done, m.scatter_mm, m.acc_done, m.table_ready) = m.sems(
        "xn2_ready xn2_hi xn2_lo xn2_mm xn2_T logit_mm gap_done gap_exp_done routed_done rank_mm n_ready "
        "pick_done gather_mm xg_hi_done xg_lo_done gateT_mm gateT_done up_mm silu_done hidden_done "
        "hiddenT_mm hidden_hi_done hidden_lo_done down_mm y_done scatter_mm acc_done table_ready")


def e_slot(k):
    return k % E_RING


def e_wait(eng, sem, k, i, each=1):
    before = S_MOE // RING if e_slot(k) < RING else 0
    eng.wait_ge(sem[e_slot(k)], (i * (EU // E_RING) + before + k // E_RING + 1) * each)


def e_split_hi(act, m, k, i):
    s = e_slot(k)
    e_wait(act, m.e_loaded, k, i, 16)
    act.activation(m.e_hi[s][:].rearrange("p k n -> p (k n)"), m.e_raw[s], ACT.Copy).then_inc(m.e_hi_done[s], 1)


def e_split_lo(eng, m, k, i):
    s = e_slot(k)
    e_wait(eng, m.e_hi_done, k, i)
    eng.tensor_tensor(m.e_lo[s][:].rearrange("p k n -> p (k n)"), m.e_raw[s],
                      m.e_hi[s][:].rearrange("p k n -> p (k n)").bitcast(F32), ALU.subtract).then_inc(m.e_lo_done[s], 1)


def e_unit_used(m, k, i):
    if k in UP_UNITS:
        return m.up_mm, i * len(UP_UNITS) + UP_UNITS.index(k) + 1
    return m.down_mm, i * QUARTERS + DOWN_UNITS.index(k) + 1


def turns(eng, m):
    eng.wait_ge(m.n_ready, 1)
    return eng.value_load(m.n_turns[0:1, 0:1], min_val=E, max_val=E + EXTRA)


def sp_moe(sp, m):
    sp.wait_ge(m.x2_done, B)
    for s in range(RING, E_RING):
        sp.dma_start(m.e_raw[s], m.dram["w_stream"][L * LU + s]).then_inc(m.e_loaded[s], 16)
    n = turns(sp, m)
    sp.wait_ge(m.table_ready, 1)
    with sp.Fori(0, n) as i:
        expert = sp.value_load(m.expert_of[0:1, bass.ds(i, 1)], min_val=0, max_val=E - 1)
        after = sp.value_load(m.expert_of[0:1, bass.ds(i + 1, 1)], min_val=0, max_val=E - 1)
        for k in range(E_RING, EU + E_RING):
            at = expert * EU + (L * LU + k) if k < EU else after * EU + (L * LU + k - EU)
            e_wait(sp, m.e_lo_done, k - E_RING, i)
            sp.dma_start(m.e_raw[e_slot(k)], m.dram["w_stream"][bass.ds(at, 1)].rearrange("a p n -> (a p) n")
                         ).then_inc(m.e_loaded[e_slot(k)], 16)
    sp.wait_ge(m.acc_done, n * B)
    sp.dma_start(m.dram["out"].rearrange("b p d -> p b d"), m.x_res[:]).then_inc(m.out_done, 16)
    sp.wait_ge(m.out_done, 16)


def pool_moe(pool, m):
    e_split_lo(pool, m, RING, 0)
    with pool.Fori(0, turns(pool, m)) as i:
        for k in range(E_RING, EU + E_RING, RING):
            e_split_lo(pool, m, k, i)


def act_moe(act, m):
    ln_root(act, m, 2 * L + 3)
    for b in range(B):
        act.wait_ge(m.xn2_ready, b + 1)
        act.activation(m.xn_hi[:, b, :], m.xn_tok[:, b, :], ACT.Copy).then_inc(m.xn2_hi, 1)
    for k in range(RING, E_RING):
        e_split_hi(act, m, k, 0)
    act.wait_ge(m.gap_done, 1)
    act.activation(m.gap_exp[:], m.gap[:], ACT.Exp).then_inc(m.gap_exp_done, 1)

    def gathered(e):
        act.wait_ge(m.gather_mm, e * 2 + 1)
        act.activation(m.xg_hi[:], by_block(m.bank[XG_BANKS[0]]), ACT.Copy).then_inc(m.xg_hi_done, 1)

    gathered(0)
    with act.Fori(0, turns(act, m)) as i:

        def unit(k):
            act.wait_ge(*e_unit_used(m, k - E_RING, i))
            e_split_hi(act, m, k, i)

        def silu(j):
            act.wait_ge(m.up_mm, i * len(UP_UNITS) + 2 * j + 1)
            act.activation(m.silu[:, j % 2, :], m.bank[UP_BANKS[j % 2]][:], ACT.Silu).then_inc(m.silu_done, 1)

        def hidden(j):
            act.wait_ge(m.hiddenT_mm, i * QUARTERS + j + 1)
            act.activation(m.hidden_hi[:, j % 2, :], m.bank[HIDDEN_BANK][:], ACT.Copy).then_inc(m.hidden_hi_done, 1)

        unit(6)
        silu(0)
        unit(7)
        act.wait_ge(m.gateT_mm, i + 1)
        act.activation(m.pick_gate_T[:].rearrange("p b t -> p (b t)"), m.bank[HIDDEN_BANK][:, 0:B * P], ACT.Copy).then_inc(
            m.gateT_done, 1)
        unit(8)
        silu(1)
        unit(9)
        hidden(0)
        unit(10)
        unit(11)
        silu(2)
        hidden(1)
        unit(12)
        unit(13)
        unit(14)
        silu(3)
        hidden(2)
        unit(15)
        gathered(i + 1)
        hidden(3)
        unit(16)
        act.wait_ge(m.down_mm, i * QUARTERS + QUARTERS)
        act.activation(m.y[:], m.bank[Y_BANK][:], ACT.Copy).then_inc(m.y_done, 1)
        unit(17)


def dve_moe(dve, m, step):
    dve.wait_ge(m.x2_done, B)
    for b in range(B):
        ln_scale(dve, m, step, m.x_res[:, b, :], b, 2 * L + 3)
        step.wait()
        ln_apply(dve, m, m.xn_tok[:, b, :], m.x_res[:, b, :], b).then_inc(m.xn2_ready, 1)
    for b in range(B):
        dve.wait_ge(m.xn2_mm, b + 1)
        dve.tensor_copy(m.xn_T[:, :, b * P:(b + 1) * P], by_block(m.bank[b])).then_inc(m.xn2_T, 1)
    for b in range(B):
        dve.wait_ge(m.xn2_hi, b + 1)
        dve.tensor_tensor(m.xn_lo[:, b, :], m.xn_tok[:, b, :], m.xn_hi[:, b, :].bitcast(F32), ALU.subtract).then_inc(
            m.xn2_lo, 1)
    for k in range(RING + 1, E_RING):
        e_split_lo(dve, m, k, 0)
    dve.wait_ge(m.logit_mm, 1)
    dve.wait_ge(m.consts_in, 48)

    def do(ins):
        step.done(ins)
        step.wait()

    def over_experts(t):
        return t[:].unsqueeze(2).to_broadcast([P, B, E])

    iota = m.iota[:, 0:E].unsqueeze(1).to_broadcast([P, B, E])
    do(dve.tensor_copy(m.logits[:].rearrange("p b e -> p (b e)"), m.bank[2][:, 0:B * E]))
    for scores, best, first, chosen in ((m.logits, m.best1, m.first1, m.chosen1), (m.rest, m.best2, m.first2, m.chosen2)):
        do(dve.tensor_reduce(best[:], scores[:], X_AXIS, ALU.max))
        do(dve.tensor_tensor(m.is_max[:], scores[:], over_experts(best), ALU.is_equal))
        do(dve.scalar_tensor_tensor(m.candidate[:], m.is_max[:], -float(E), iota, ALU.mult, ALU.add))
        do(dve.tensor_reduce(first[:], m.candidate[:], X_AXIS, ALU.min))
        do(dve.tensor_tensor(chosen[:], m.candidate[:], over_experts(first), ALU.is_equal))
        if chosen is m.chosen1:
            do(dve.scalar_tensor_tensor(m.rest[:], chosen[:], BELOW_ALL, m.logits[:], ALU.mult, ALU.add))
    dve.tensor_tensor(m.routed[:], m.chosen1[:], m.chosen2[:], ALU.add).then_inc(m.routed_done, 1)
    dve.tensor_tensor(m.gap[:], m.best2[:], m.best1[:], ALU.subtract).then_inc(m.gap_done, 1)
    dve.wait_ge(m.gap_exp_done, 1)
    do(dve.tensor_scalar(m.gap_sum[:], m.gap_exp[:], 1.0, None, ALU.add))
    do(dve.reciprocal(m.weight1[:], m.gap_sum[:]))
    do(dve.tensor_tensor(m.weight2[:], m.gap_exp[:], m.weight1[:], ALU.mult))
    do(dve.tensor_tensor(m.weighted1[:], m.chosen1[:], over_experts(m.weight1), ALU.mult))
    do(dve.tensor_tensor(m.candidate[:], m.chosen2[:], over_experts(m.weight2), ALU.mult))
    do(dve.tensor_tensor(m.gate_of[:, :, 0:E], m.weighted1[:], m.candidate[:], ALU.add))
    do(dve.memset(m.gate_of[:, :, TURNS - 1:], 0.0))
    do(dve.memset(m.slot_of[:, :, TURNS - 1:], -1.0))
    dve.wait_ge(m.rank_mm, 1)
    rank = m.bank[3][:, 0:B * E].rearrange("p (b e) -> p b e", b=B)
    do(dve.scalar_tensor_tensor(m.position[:], rank, 1.0, m.routed[:], ALU.add, ALU.mult))
    do(dve.tensor_scalar(m.slot_of[:, :, 0:E], m.position[:], -1.0, None, ALU.add))

    def build(e):
        for b in range(B):
            dve.tensor_scalar(m.pick[:, b, :], m.iota[:], m.slot_of[:, b, bass.ds(e, 1)], None, ALU.is_equal)
        for b in range(B):
            last = dve.tensor_scalar(m.pick_gate[:, b, :], m.iota[:], m.slot_of[:, b, bass.ds(e, 1)],
                                     m.gate_of[:, b, bass.ds(e, 1)], ALU.is_equal, ALU.mult)
        last.then_inc(m.pick_done, 1)

    def gathered(e):
        dve.wait_ge(m.gather_mm, e * 2 + 2)
        dve.tensor_copy(m.xg_lo[:], by_block(m.bank[XG_BANKS[1]])).then_inc(m.xg_lo_done, 1)

    build(0)
    do(dve.tensor_scalar(m.crowded[:, 0, :], m.bank[3][:, B * E:B * E + E], float(P), None, ALU.is_gt))
    do(dve.tensor_reduce(m.n_crowded[:], m.crowded[:, 0, :], X_AXIS, ALU.add))
    dve.tensor_scalar(m.n_turns[:], m.n_crowded[:], float(E), None, ALU.add).then_inc(m.n_ready, 1)
    gathered(0)
    do(dve.memset(m.expert_f[:, TURNS - 1:], 0.0))
    do(dve.tensor_copy(m.expert_f[:, 0:E], m.iota[:, 0:E]))
    for r in range(EXTRA):
        turn = slice(E + r, E + r + 1)
        do(dve.scalar_tensor_tensor(m.order[:], m.crowded[:, r, :], -float(E), m.iota[:, 0:E], ALU.mult, ALU.add))
        do(dve.tensor_reduce(m.first_one[:], m.order[:], X_AXIS, ALU.min))
        do(dve.scalar_tensor_tensor(m.extra[:, r, :], m.order[:], m.first_one[:], m.crowded[:, r, :], ALU.is_equal, ALU.mult))
        do(dve.tensor_tensor(m.crowded[:, r + 1, :], m.crowded[:, r, :], m.extra[:, r, :], ALU.subtract))
        do(dve.tensor_tensor(m.extra_index[:, r, :], m.extra[:, r, :], m.iota[:, 0:E], ALU.mult))
        do(dve.tensor_reduce(m.expert_f[:, turn], m.extra_index[:, r, :], X_AXIS, ALU.add))
        chosen = m.extra[:, r, :].unsqueeze(1).to_broadcast([P, B, E])
        do(dve.tensor_tensor(m.product[:], m.gate_of[:, :, 0:E], chosen, ALU.mult))
        do(dve.tensor_reduce(m.gate_of[:, :, turn], m.product[:], X_AXIS, ALU.add))
        do(dve.tensor_tensor(m.product[:], m.position[:], chosen, ALU.mult))
        do(dve.tensor_reduce(m.best1[:], m.product[:], X_AXIS, ALU.add))
        do(dve.tensor_scalar(m.slot_of[:, :, E + r], m.best1[:], -1.0 - P, None, ALU.add))
    dve.tensor_copy(m.expert_of[:], m.expert_f[:]).then_inc(m.table_ready, 1)
    with dve.Fori(0, turns(dve, m)) as i:
        def unit(k):
            e_split_lo(dve, m, k, i)

        def hidden(j):
            bank = UP_BANKS[j % 2]
            dve.wait_ge(m.silu_done, i * QUARTERS + j + 1)
            dve.wait_ge(m.up_mm, i * len(UP_UNITS) + 2 * j + 2)
            dve.tensor_tensor(m.hidden[:, j % 2, :], m.bank[bank + 1][:], m.silu[:, j % 2, :], ALU.mult).then_inc(
                m.hidden_done, 1)

        def hidden_lo(j):
            dve.wait_ge(m.hidden_hi_done, i * QUARTERS + j + 1)
            dve.tensor_tensor(m.hidden_lo[:, j % 2, :], m.bank[HIDDEN_BANK][:], m.hidden_hi[:, j % 2, :].bitcast(F32),
                              ALU.subtract).then_inc(m.hidden_lo_done, 1)

        hidden(0)
        unit(7)
        unit(8)
        hidden(1)
        hidden_lo(0)
        build(i + 1)
        unit(10)
        unit(11)
        hidden(2)
        hidden_lo(1)
        unit(13)
        unit(14)
        hidden(3)
        hidden_lo(2)
        gathered(i + 1)
        hidden_lo(3)
        unit(16)
        for b in range(B):
            dve.wait_ge(m.scatter_mm, i * B + b + 1)
            dve.tensor_tensor(m.x_res[:, b, :], m.bank[XG_BANKS[b]][:], m.x_res[:, b, :], ALU.add).then_inc(m.acc_done, 1)
        unit(17)


def pe_moe(pe, m):
    for b in range(B):
        pe.wait_ge(m.xn2_ready, b + 1)
        pe_transpose4(pe, m, m.bank[b], [m.xn_tok[:, b, k * P:(k + 1) * P] for k in range(KT)], m.ident[:]).then_inc(
            m.xn2_mm, 1)
    pe.wait_ge(m.gate_in, 16)
    pe.wait_ge(m.xn2_T, B)
    for b in range(B):
        for k in range(KT):
            last = pe.matmul(m.bank[2][:, b * E:(b + 1) * E], m.xn_T[:, k, b * P:(b + 1) * P], m.gate_sb[:, k, :],
                             start=k == 0, stop=k == KT - 1)
    last.then_inc(m.logit_mm, 1)
    pe.wait_ge(m.consts_in, 48)
    pe.wait_ge(m.routed_done, 1)
    pe.matmul(m.bank[3][:, 0:E], m.earlier[:], m.routed[:, 0, :], start=True, stop=True)
    pe.matmul(m.bank[3][:, E:2 * E], m.earlier[:], m.routed[:, 1, :], start=True, stop=False)
    pe.matmul(m.bank[3][:, E:2 * E], m.ones[:], m.routed[:, 0, :], start=False, stop=True)
    for b in range(B):
        last = pe.matmul(m.bank[3][:, 2 * E:3 * E], m.ones[:], m.routed[:, b, :], start=b == 0, stop=b == B - 1)
    last.then_inc(m.rank_mm, 1)

    def gather(e):
        pe.wait_ge(m.pick_done, e + 1)
        for part, bank in ((m.xn_hi, m.bank[XG_BANKS[0]]), (m.xn_lo, m.bank[XG_BANKS[1]])):
            for k in range(KT):
                for b in range(B):
                    last = pe.matmul(bank[:, k * P:(k + 1) * P], part[:, b, k * P:(k + 1) * P], m.pick[:, b, :],
                                     start=b == 0, stop=b == B - 1)
            last.then_inc(m.gather_mm, 1)

    pe.wait_ge(m.xn2_lo, B)
    gather(0)
    with pe.Fori(0, turns(pe, m)) as i:

        def unit(k):
            e_wait(pe, m.e_lo_done, k, i)
            return m.e_hi[e_slot(k)], m.e_lo[e_slot(k)]

        def up(j):
            if j == 0:
                pe.wait_ge(m.xg_hi_done, i + 1)
                pe.wait_ge(m.xg_lo_done, i + 1)
            for q in range(2):
                w_hi, w_lo = unit(UP_UNITS[2 * j + q])
                if q == 0 and j >= 2:
                    pe.wait_ge(m.hidden_done, i * QUARTERS + j - 1)
                for k in range(KT):
                    last = three_passes(pe, m.bank[UP_BANKS[j % 2] + q][:], m.xg_hi[:, k, :], m.xg_lo[:, k, :],
                                        w_hi[:, k, :], w_lo[:, k, :], k == 0, k == KT - 1)
                last.then_inc(m.up_mm, 1)

        def hidden(j):
            pe.wait_ge(m.hidden_done, i * QUARTERS + j + 1)
            if j:
                pe.wait_ge(m.hidden_lo_done, i * QUARTERS + j)
            else:
                pe.wait_ge(m.gateT_done, i + 1)
            pe_transpose4(pe, m, m.bank[HIDDEN_BANK], [m.hidden[:, j % 2, t * P:(t + 1) * P] for t in range(KT)],
                          m.ident[:]).then_inc(m.hiddenT_mm, 1)

        def down(j):
            w_hi, w_lo = unit(DOWN_UNITS[j])
            pe.wait_ge(m.hidden_lo_done, i * QUARTERS + j + 1)
            for k in range(KT):
                cols = slice(k * P, (k + 1) * P)
                last = three_passes(pe, m.bank[Y_BANK][:], m.hidden_hi[:, j % 2, cols], m.hidden_lo[:, j % 2, cols],
                                    w_hi[:, k, :], w_lo[:, k, :], j == 0 and k == 0, j == QUARTERS - 1 and k == KT - 1)
            last.then_inc(m.down_mm, 1)

        up(0)
        for b in range(B):
            last = pe.transpose(m.bank[HIDDEN_BANK][:, b * P:(b + 1) * P], m.pick_gate[:, b, :], m.ident[:])
        last.then_inc(m.gateT_mm, 1)
        up(1)
        hidden(0)
        up(2)
        down(0)
        hidden(1)
        up(3)
        down(1)
        hidden(2)
        gather(i + 1)
        hidden(3)
        down(2)
        down(3)
        pe.wait_ge(m.xg_hi_done, i + 2)
        pe.wait_ge(m.xg_lo_done, i + 2)
        pe.wait_ge(m.y_done, i + 1)
        for b in range(B):
            pe.matmul(m.bank[XG_BANKS[b]][:], m.pick_gate_T[:, b, :], m.y[:], start=True, stop=True).then_inc(
                m.scatter_mm, 1)


def _blocks(w, rows):
    return w.reshape(rows // P, P, -1).transpose(1, 0, 2)


def _positions():
    pos = np.arange(P - 1, -1, -1, dtype=np.float32)
    freq = (np.float32(1.0) / np.float32(10000.0) ** (np.arange(0, D, 2, dtype=np.float32) / np.float32(D))).astype(
        np.float32)
    ang = pos[:, None] * freq[None, :]
    return np.concatenate([np.sin(ang), np.cos(ang)], axis=-1).astype(np.float32)


def kernel(**inputs):
    from concourse import bacc
    from concourse.bass_utils import run_bass_kernel_spmd

    a = {k: np.asarray(v) for k, v in inputs.items()}
    c = np.ascontiguousarray
    unit = (P, KT * CHUNK)
    w_cross = c(np.stack([_blocks(a[f"L0_xattn_{n}"].T, D).reshape(unit) for n in ("Wq", "Wk", "Wv", "Wo")]))
    ctx_t = c(a["ctx_1024"].reshape(B, NCH, CHUNK, KT, P).transpose(0, 1, 4, 3, 2).reshape(B * NCH, *unit))

    def units(w, rows):
        r, n = w.shape
        return [_blocks(w[i:i + D, j:j + CHUNK], D).reshape(unit) for i in range(0, r, D) for j in range(0, n, CHUNK)]

    stream = []
    for i in range(L):
        qkv = a["L0_attn_W_qkv"][i]
        hd = H * DH
        for w in (a["L0_attn_W_r"][i], qkv[:, :hd], qkv[:, hd:2 * hd], qkv[:, 2 * hd:], a["L0_attn_W_o"][i],
                  a["L0_attn_W_ff1"][i], a["L0_attn_W_ff2"][i]):
            stream += units(w, D)
    for e in range(E):
        quarters = {n: units(a[f"L0_ffn_{n}"][e], D) for n in ("w0", "w1", "wo")}
        stream += [quarters[n][q] for n, q in E_ORDER]
    w_stream = c(np.stack(stream))
    arrays = {
        "x": c(a["x"]),
        "ctx_t": ctx_t,
        "mask": c(a["mask_1x1xSxS2_ik0"].reshape(P, SK)),
        "w_cross": w_cross,
        "w_stream": w_stream,
        "cross_vecs": c(np.stack([a[f"L0_xattn_{n}"].reshape(KT, P).T for n in ("bq", "bk", "bv")], axis=1)),
        "bo_row": c(a["L0_xattn_bo"]),
        "consts": np.stack([np.eye(P), np.triu(np.ones((P, P)), 1), np.tile(np.arange(P), (P, 1)),
                            np.ones((P, P))]).astype(np.float32),
        "r_t": c(_blocks(_positions().T, D).reshape(unit[0], KT * P)),
        "uv": c(np.stack([np.tile(a[f"L0_attn_{n}"].T, (2, 1)) for n in "uv"], axis=1)),
        "ff1_bias": c(a["L0_attn_b_ff1"].reshape(L, DF // P, P).transpose(2, 0, 1)),
        "layer_rows": c(np.stack([a[f"L0_attn_{n}"] for n in ("ln1_g", "ln1_b", "b_ff2", "ln2_g", "ln2_b")], axis=1)),
        "gate": c(_blocks(a["L0_ffn_gate_kernel"], D)),
    }
    nc = bacc.Bacc("TRN2", target_bir_lowering=False, num_devices=1)
    aps = {n: nc.dram_tensor(n, v.shape, mybir.dt.from_np(v.dtype), kind="ExternalInput").ap() for n, v in arrays.items()}
    out = nc.dram_tensor("out", (B, P, D), F32, kind="ExternalOutput").ap()
    build_program(nc, **aps, out=out)
    r = run_bass_kernel_spmd(nc, [arrays], core_ids=[0])
    return r.results[0]["out"]
```

```python
from contextlib import ExitStack

import concourse.bass as bass
import concourse.mybir as mybir
import numpy as np

F32 = mybir.dt.float32
F32R = mybir.dt.float32r
I32 = mybir.dt.int32
U32 = mybir.dt.uint32
ALU = mybir.AluOpType
ACT = mybir.ActivationFunctionType
X_AXIS = mybir.AxisListType.X

P = 128
B = 2
D = 512
KT = D // P
SK = 2048
CHUNK = 512
NCH = SK // CHUNK
XH, XDH = 16, 32
GROUPS = XH * XDH // P
HPG = P // XDH
L, H, DH, DF = 4, 16, 64, 2048
E, F = 8, 2048
EPS = 1e-5
MASKED = -float(2 ** 30)
X_SCALE = float(1.0 / np.float32(np.sqrt(XDH)))
L_SCALE = 1.0 / 8.0

RING = 3
S_WQ, S_WK, S_WV, S_CTX = 0, 1, 2, 3
S_WO = S_CTX + B * NCH
S_LAYER = S_WO + 1
LU = 18
U_WR, U_WQ, U_WK, U_WV, U_WO, U_FF1, U_FF2 = 0, 2, 4, 6, 8, 10, 14
S_MOE = S_LAYER + L * LU
EU = 12
E_ORDER = [("w0", 0), ("w1", 0), ("w0", 1), ("w1", 1), ("w0", 2), ("w1", 2), ("wo", 0), ("w0", 3),
           ("w1", 3), ("wo", 1), ("wo", 2), ("wo", 3)]
assert LU % RING == 0 and EU % RING == 0 and S_LAYER % RING == 0 and S_MOE % RING == 0


def nth(s):
    return s // RING + 1


def wait_unit(eng, sem, s, iteration=0, per=0, each=1):
    eng.wait_ge(sem[s % RING], (iteration * (per // RING) + nth(s)) * each)


class Memory:

    def __init__(self, nc, ctx, dram):
        self.nc, self.ctx, self.dram = nc, ctx, dram

    def sb(self, name, shape, dt=F32):
        return self.ctx.enter_context(self.nc.sbuf_tensor(name, shape, dt))

    def sems(self, names):
        return [self.ctx.enter_context(self.nc.semaphore(name)) for name in names.split()]

    def slot_sems(self, name):
        return [self.ctx.enter_context(self.nc.semaphore(f"{name}{i}")) for i in range(RING)]


def three_passes(pe, out, w_hi, w_lo, m_hi, m_lo, first, last):
    pe.matmul(out, w_hi, m_hi, start=first, stop=False)
    pe.matmul(out, w_hi, m_lo, start=False, stop=False)
    return pe.matmul(out, w_lo, m_hi, start=False, stop=last)


def split_hi(act, m, s, iteration=0, per=0, hi=None):
    wait_unit(act, m.loaded, s, iteration, per, 16)
    dst = m.w_hi[s % RING] if hi is None else hi
    act.activation(dst[:].rearrange("p k n -> p (k n)"), m.raw[:, s % RING, :], ACT.Copy).then_inc(
        m.hi_done[s % RING], 1)


def split_lo(eng, m, s, iteration=0, per=0, hi=None, lo=None):
    wait_unit(eng, m.hi_done, s, iteration, per)
    h = m.w_hi[s % RING] if hi is None else hi
    l_ = m.w_lo[s % RING] if lo is None else lo
    eng.tensor_tensor(l_[:].rearrange("p k n -> p (k n)"), m.raw[:, s % RING, :],
                      h[:].rearrange("p k n -> p (k n)").bitcast(F32), ALU.subtract).then_inc(
        m.lo_done[s % RING], 1)


class Step:

    def __init__(self, eng, sem, base=0, iteration=0, per=0):
        self.eng, self.sem, self.base, self.iteration, self.per, self.n = eng, sem, base, iteration, per, 0

    def done(self, ins):
        ins.then_inc(self.sem, 1)
        self.n += 1

    def wait(self):
        self.eng.wait_ge(self.sem, self.iteration * self.per + self.base + self.n)


def ln_scale(dve, m, step, src, t, n):
    step.done(dve.bn_stats(m.bn6[:, t, :], src))
    step.wait()
    dve.memset(m.newton[:, t:t + 1], 0.0)
    step.done(dve.bn_aggr(m.mean_var[:, t, :], m.bn6[:, t, :]))
    step.wait()
    var_eps, root0 = m.var_eps[:, t:t + 1], m.root0[:, t:t + 1]
    dve.tensor_scalar(var_eps, m.mean_var[:, t, 1:2], EPS, None, ALU.add).then_inc(m.ln_var, 1)
    dve.wait_ge(m.ln_rooted, (n - 1) * B + t + 1)
    step.done(dve.reciprocal(root0, m.ln_sqrt[:, t:t + 1]))
    step.wait()
    step.done(dve.scalar_tensor_tensor(m.newton[:, t:t + 1], root0, -0.5, root0, ALU.mult, ALU.mult))
    step.wait()
    step.done(dve.tensor_tensor(m.newton2[:, t:t + 1], m.newton[:, t:t + 1], var_eps, ALU.mult))
    step.wait()
    step.done(dve.scalar_tensor_tensor(m.rstd[:, t:t + 1], m.newton2[:, t:t + 1], 1.5, root0, ALU.add, ALU.mult))


def ln_root(act, m, n, t):
    act.wait_ge(m.ln_var, (n - 1) * B + t + 1)
    act.activation(m.ln_sqrt[:, t:t + 1], m.var_eps[:, t:t + 1], ACT.Sqrt).then_inc(m.ln_rooted, 1)


def ln_apply(dve, m, out, src, t):
    return dve.tensor_scalar(out, src, m.mean_var[:, t, 0:1], m.rstd[:, t:t + 1], ALU.subtract, ALU.mult)


def build_program(nc, x, ctx_t, mask, w_cross, w_stream, cross_vecs, bo_row, consts, r_t, uv, ff1_bias,
                  layer_rows, gate, out):
    with ExitStack() as ctx:
        m = Memory(nc, ctx, dict(x=x, ctx_t=ctx_t, mask=mask, w_cross=w_cross, w_stream=w_stream,
                                 cross_vecs=cross_vecs, bo_row=bo_row, consts=consts, r_t=r_t, uv=uv,
                                 ff1_bias=ff1_bias, layer_rows=layer_rows, gate=gate, out=out))
        common_memory(m)
        for phase_memory in (cross_memory, layer_memory, moe_memory):
            with ExitStack() as m.ctx:
                phase_memory(m)
        block = ctx.enter_context(nc.Block())

        @block.sync
        def _(sp):
            sp_program(sp, m)

        @block.gpsimd
        def _(pool):
            pool_cross(pool, m)
            pool_layers(pool, m)
            pool_moe(pool, m)

        @block.scalar
        def _(act):
            act_cross(act, m)
            act_layers(act, m)
            act_moe(act, m)

        @block.vector
        def _(dve):
            step = Step(dve, m.dve_step)
            dve_cross(dve, m, step)
            dve_layers(dve, m, step)
            dve_moe(dve, m, step)

        @block.tensor
        def _(pe):
            pe_cross(pe, m)
            pe_layers(pe, m)
            pe_moe(pe, m)


def common_memory(m):
    m.raw = m.sb("raw", [P, RING, KT * CHUNK])
    m.w_hi = [m.sb(f"w_hi{i}", [P, KT, CHUNK], F32R) for i in range(RING)]
    m.w_lo = [m.sb(f"w_lo{i}", [P, KT, CHUNK], F32R) for i in range(RING)]
    m.loaded = m.slot_sems("loaded")
    m.hi_done = m.slot_sems("hi_done")
    m.lo_done = m.slot_sems("lo_done")
    m.ident = m.sb("ident", [P, P])
    m.earlier = m.sb("earlier", [P, P])
    m.iota = m.sb("iota", [P, P])
    m.ones = m.sb("ones", [P, P])
    m.gate_sb = m.sb("gate_sb", [P, KT, E])
    m.x_res = m.sb("x_res", [P, B, D])
    m.r_hi = m.sb("r_hi", [P, KT, P], F32R)
    m.r_lo = m.sb("r_lo", [P, KT, P], F32R)
    m.uv_sb = m.sb("uv_sb", [P, 2, H])
    m.ff1_bias_sb = m.sb("ff1_bias_sb", [P, L, DF // P])
    m.bn6 = m.sb("bn6", [P, B, 6])
    m.mean_var = m.sb("mean_var", [P, B, 2])
    m.var_eps = m.sb("var_eps", [P, B])
    m.ln_sqrt = m.sb("ln_sqrt", [P, B])
    m.root0 = m.sb("root0", [P, B])
    m.newton = m.sb("newton", [P, B])
    m.newton2 = m.sb("newton2", [P, B])
    m.rstd = m.sb("rstd", [P, B])
    (m.ident_in, m.x_in, m.vecs_in, m.vecs_in2, m.mask_in, m.r_in, m.uv_in, m.bias_in, m.gate_in,
     m.consts_in, m.ln_var, m.ln_rooted, m.dve_step, m.out_done) = m.sems(
        "ident_in x_in vecs_in vecs_in2 mask_in r_in uv_in bias_in gate_in consts_in ln_var "
        "ln_rooted dve_step out_done")
    m.bank = [m.ctx.enter_context(m.nc.psum_tensor(f"bank{i}", [P, CHUNK], F32)) for i in range(8)]


S_BANKS, T_BANKS, O_BANK = (0, 1, 2, 3), (4, 5, 7), 6
T_SLOT = (0, 1, 2, 1)
NG = B * GROUPS


def cross_memory(m):
    m.ident_r = m.sb("ident_r", [P, P], F32R)
    m.cross_vec = m.sb("cross_vec", [P, 3, KT])
    m.bo_bc = m.sb("bo_bc", [P, D])
    m.q_scale = m.sb("q_scale", [P, 1])
    m.mask_max = m.sb("mask_max", [P, 1])
    m.mask_add = m.sb("mask_add", [P, SK], F32R)
    m.q_feat = m.sb("q_feat", [P, KT, B * P])
    m.qz_hi = m.sb("qz_hi", [P, HPG, P], F32R)
    m.qz_lo = m.sb("qz_lo", [P, HPG, P], F32R)
    m.k_hi = m.sb("k_hi", [P, KT, CHUNK], F32R)
    m.k_lo = m.sb("k_lo", [P, KT, CHUNK], F32R)
    m.probs = m.sb("probs", [P, NCH, CHUNK])
    m.probs_T = m.sb("probs_T", [P, len(T_BANKS), CHUNK])
    m.part_max = m.sb("part_max", [P, NCH])
    m.neg_max = m.sb("neg_max", [P, 1])
    m.shift = m.sb("shift", [P, HPG])
    m.part_sum = m.sb("part_sum", [P, HPG, NCH])
    m.row_sum = m.sb("row_sum", [P, HPG])
    m.row_inv = m.sb("row_inv", [P, NG, HPG])
    m.o_feat = m.sb("o_feat", [P, NG, P])
    m.v_grp = m.sb("v_grp", [P, SK // P, P])
    outer = m.ctx
    with ExitStack() as m.ctx:
        m.k_all = m.sb("k_all", [P, KT, SK])
        m.v_all = m.sb("v_all", [P, SK // P, D])
    with ExitStack() as m.ctx:
        m.xn = m.sb("xn", [P, B, D])
        m.xT_hi = m.sb("xT_hi", [P, KT, B * P], F32R)
        m.xT_lo = m.sb("xT_lo", [P, KT, B * P], F32R)
    with ExitStack() as m.ctx:
        m.vecT_hi = m.sb("vecT_hi", [P, KT, B * P], F32R)
        m.vecT_lo = m.sb("vecT_lo", [P, KT, B * P], F32R)
        m.o_tok = m.sb("o_tok", [P, B, D])
    m.ctx = outer
    (m.ident_ready, m.xn_ready, m.xnT_mm, m.xT_hi_done, m.xT_lo_done, m.q_mm, m.q_done, m.mask_ready,
     m.r_hi_done, m.r_ready, m.qz_zeroed, m.bo_added, m.q_scale_done, m.k_mm, m.k_done, m.v_mm, m.v_done,
     m.k_hi_done, m.k_lo_done, m.qz_hi_done, m.qz_done, m.s_mm, m.max_done, m.neg_done,
     m.shift_done, m.exp_done, m.pT_mm, m.pT_dve, m.pT_act, m.pv_mm, m.sum_done, m.inv_done,
     m.o_copied, m.v_part_done, m.oT_mm, m.oT_done, m.vec_mm, m.vec_hi, m.vec_lo, m.o_mm, m.x1_done) = m.sems(
        "ident_ready xn_ready xnT_mm xT_hi_done xT_lo_done q_mm q_done mask_ready r_hi_done r_ready "
        "qz_zeroed bo_added q_scale_done k_mm k_done v_mm v_done k_hi_done k_lo_done qz_hi_done qz_done "
        "s_mm max_done neg_done shift_done exp_done pT_mm pT_dve pT_act pv_mm sum_done "
        "inv_done o_copied v_part_done oT_mm oT_done vec_mm vec_hi vec_lo o_mm x1_done")


MASK_ROWS = SK // D


def ctx_slot(m, n):
    return (m.w_hi[0], m.w_lo[0]) if n % 2 == 0 else (m.k_hi, m.k_lo)


def sp_program(sp, m):
    d = m.dram
    flat = m.raw

    def load(s, src):
        if s >= RING:
            wait_unit(sp, m.lo_done, s - RING)
        sp.dma_start(flat[:, s % RING, :], src).then_inc(m.loaded[s % RING], 16)

    sp.dma_start(m.x_res[:], d["x"].rearrange("b p d -> p b d")).then_inc(m.x_in, 16)
    load(S_WQ, d["w_cross"][0])
    sp.dma_start(m.ident[:], d["consts"][0]).then_inc(m.ident_in, 16)
    sp.dma_start(m.cross_vec[:], d["cross_vecs"]).then_inc(m.vecs_in, 16)
    load(S_WK, d["w_cross"][1])
    load(S_WV, d["w_cross"][2])
    load(S_CTX, d["ctx_t"][0])
    sp.dma_start(m.v_all[:, SK // P - MASK_ROWS:, :].rearrange("p t d -> p (t d)").bitcast(I32), d["mask"]).then_inc(
        m.mask_in, 16)
    load(S_CTX + 1, d["ctx_t"][1])
    sp.dma_start(m.v_all[:, SK // P - MASK_ROWS - 1, :], d["r_t"]).then_inc(m.r_in, 16)
    sp.dma_start(m.bo_bc[:], d["bo_row"].partition_broadcast(P)).then_inc(m.vecs_in2, 16)
    sp.dma_start(m.uv_sb[:], d["uv"]).then_inc(m.uv_in, 16)
    sp.dma_start(m.ff1_bias_sb[:], d["ff1_bias"]).then_inc(m.bias_in, 16)
    sp.dma_start(m.gate_sb[:], d["gate"]).then_inc(m.gate_in, 16)
    for n in range(2, B * NCH):
        load(S_CTX + n, d["ctx_t"][n])
        if n < 5:
            if n > 2:
                sp.wait_ge(m.consts_in, (n - 2) * 16)
            sp.dma_start((m.earlier, m.iota, m.ones)[n - 2][:], d["consts"][n - 1]).then_inc(m.consts_in, 16)
    load(S_WO, d["w_cross"][3])
    for k in range(RING):
        load(S_LAYER + k, d["w_stream"][k])
    sp_layers(sp, m)
    sp_moe(sp, m)


def pool_cross(pool, m):
    split_lo(pool, m, S_WK)

    def context(n):
        split_lo(pool, m, S_CTX + n, hi=ctx_slot(m, n)[0], lo=ctx_slot(m, n)[1])

    def keys(g):
        for c in range(NCH):
            pool.wait_ge(m.k_hi_done, g * NCH + c + 1)
            pool.tensor_tensor(m.k_lo[:, c, :], m.k_all[:, g - b * GROUPS, c * CHUNK:(c + 1) * CHUNK],
                               m.k_hi[:, c, :].bitcast(F32), ALU.subtract).then_inc(m.k_lo_done, 1)

    for b in range(B):
        for n in range(b * NCH + 1, (b + 1) * NCH):
            context(n)
        if b == 0:
            keys(0)
            context(NCH)
        else:
            split_lo(pool, m, S_LAYER)
            split_lo(pool, m, S_LAYER + 1)
            keys(GROUPS)
            split_lo(pool, m, S_WO)
        with pool.Fori(0, GROUPS - 1) as fb:
            keys(fb + b * GROUPS + 1)


def act_cross(act, m):
    act.wait_ge(m.x_in, 16)
    for t in range(B):
        ln_root(act, m, 1, t)
    split_hi(act, m, S_WQ, hi=m.k_hi)
    split_hi(act, m, S_WK)
    split_hi(act, m, S_WV)
    for b in range(B):
        act.wait_ge(m.xnT_mm, b + 1)
        act.activation(m.xT_hi[:, :, b * P:(b + 1) * P], m.bank[b][:].rearrange("p (k t) -> p k t", k=KT),
                       ACT.Copy).then_inc(m.xT_hi_done, 1)
    def context(n):
        if n >= 2:
            act.wait_ge(m.v_mm, (n - 1) * KT)
        if n == NCH + 1:
            act.wait_ge(m.s_mm, GROUPS * HPG * NCH)
        split_hi(act, m, S_CTX + n, hi=ctx_slot(m, n)[0])

    context(0)
    act.wait_ge(m.vecs_in, 16)
    for f in range(KT):
        act.wait_ge(m.q_mm, f // 2 + 1)
        act.activation(m.q_feat[:, f, :], m.bank[2 + f // 2][:, (f % 2) * B * P:(f % 2 + 1) * B * P], ACT.Identity,
                       bias=m.cross_vec[:, 0, f:f + 1]).then_inc(m.q_done, 1)
    context(1)
    for b in range(B):
        if b == 1:
            context(NCH + 1)
        for n in range(b * NCH, (b + 1) * NCH):
            c = n % NCH
            for f in range(KT):
                act.wait_ge(m.k_mm, n * KT + f + 1)
                act.activation(m.k_all[:, f, c * CHUNK:(c + 1) * CHUNK], m.bank[f][:], ACT.Identity,
                               bias=m.cross_vec[:, 1, f:f + 1]).then_inc(m.k_done, 1)
            if c + 2 < NCH or n + 2 == NCH:
                context(n + 2)
        if b == 1:
            act.wait_ge(m.v_mm, (B * NCH - 1) * KT)
            split_hi(act, m, S_LAYER)
            split_hi(act, m, S_LAYER + 1)

        def transposed(g, j, c):
            act.wait_ge(m.pT_mm, (g * HPG + j) * NCH + c + 1)
            act.activation(m.probs_T[:, T_SLOT[c], :], m.bank[T_BANKS[T_SLOT[c]]][:], ACT.Copy).then_inc(m.pT_act, 1)

        def exps(g, j, first=False):
            act.wait_ge(m.shift_done, g * HPG + j + 1)
            for c in range(NCH):
                if not first:
                    act.wait_ge(m.pT_mm, (g * HPG + j - 1) * NCH + c + 1)
                act.activation(m.probs[:, c, :], m.bank[S_BANKS[c]][:], ACT.Exp, bias=m.shift[:, j:j + 1],
                               scale=m.q_scale[:, 0:1], accum_out=m.part_sum[:, j, c:c + 1]).then_inc(m.exp_done, 1)

        def group(g, more):
            for j in range(1, HPG):
                for c in range(1, NCH):
                    transposed(g, j - 1, c)
                exps(g, j)
            for c in range(1, NCH):
                transposed(g, HPG - 1, c)
            if more:
                exps(g + 1, 0)

        exps(b * GROUPS, 0, first=True)
        if b == 1:
            act.wait_ge(m.v_mm, B * NCH * KT)
            split_hi(act, m, S_WO)
        with act.Fori(0, GROUPS - 1) as fb:
            group(fb + b * GROUPS, True)
        group((b + 1) * GROUPS - 1, False)
    for b in range(B):
        act.wait_ge(m.vec_mm, b + 1)
        for k in range(KT):
            act.activation(m.vecT_hi[:, k, b * P:(b + 1) * P], m.bank[4 + b][:, k * P:(k + 1) * P], ACT.Identity,
                           bias=m.cross_vec[:, 2, k:k + 1]).then_inc(m.vec_hi, 1)


def dve_cross(dve, m, step):
    dve.wait_ge(m.x_in, 16)
    for b in range(B):
        ln_scale(dve, m, step, m.x_res[:, b, :], b, 1)
        step.wait()
        ln_apply(dve, m, m.xn[:, b, :], m.x_res[:, b, :], b).then_inc(m.xn_ready, 1)
    dve.wait_ge(m.ident_in, 16)
    dve.tensor_copy(m.ident_r[:], m.ident[:]).then_inc(m.ident_ready, 1)
    split_lo(dve, m, S_WQ, hi=m.k_hi, lo=m.k_lo)
    for b in range(B):
        dve.wait_ge(m.xT_hi_done, b + 1)
        dve.tensor_tensor(m.xT_lo[:, :, b * P:(b + 1) * P], m.bank[b][:].rearrange("p (k t) -> p k t", k=KT),
                          m.xT_hi[:, :, b * P:(b + 1) * P].bitcast(F32), ALU.subtract).then_inc(m.xT_lo_done, 1)
    split_lo(dve, m, S_WV)
    split_lo(dve, m, S_CTX)

    def mask_and_positions():
        dve.wait_ge(m.mask_in, 16)
        dve.tensor_scalar(m.mask_add[:], m.v_all[:, SK // P - MASK_ROWS:, :].rearrange("p t d -> p (t d)").bitcast(I32),
                          0.0, MASKED, ALU.is_equal, ALU.mult).then_inc(m.mask_ready, 1)
        dve.wait_ge(m.mask_ready, 1)
        step.done(dve.tensor_reduce(m.mask_max[:], m.mask_add[:].bitcast(F32), X_AXIS, ALU.max))
        step.wait()
        dve.tensor_scalar(m.q_scale[:], m.mask_max[:], 0.0, X_SCALE, ALU.is_equal, ALU.mult).then_inc(m.q_scale_done, 1)
        positions = m.v_all[:, SK // P - MASK_ROWS - 1, :]
        dve.wait_ge(m.r_in, 16)
        dve.tensor_copy(m.r_hi[:].rearrange("p k t -> p (k t)"), positions).then_inc(m.r_hi_done, 1)
        dve.wait_ge(m.r_hi_done, 1)
        dve.tensor_tensor(m.r_lo[:].rearrange("p k t -> p (k t)"), positions,
                          m.r_hi[:].rearrange("p k t -> p (k t)").bitcast(F32), ALU.subtract).then_inc(m.r_ready, 1)
        dve.memset(m.qz_hi[:].bitcast(U32), 0)
        dve.memset(m.qz_lo[:].bitcast(U32), 0).then_inc(m.qz_zeroed, 1)
        dve.wait_ge(m.vecs_in2, 16)
        for b in range(B):
            dve.tensor_tensor(m.x_res[:, b, :], m.x_res[:, b, :], m.bo_bc[:], ALU.add).then_inc(m.bo_added, 1)
        dve.wait_ge(m.qz_zeroed, 1)
        dve.wait_ge(m.q_done, KT)
        dve.wait_ge(m.q_scale_done, 1)
        dve.wait_ge(m.r_ready, 1)

    for b in range(B):

        def queries(g, j):
            rows = slice(j * XDH, (j + 1) * XDH)
            q = m.q_feat[rows, g - b * GROUPS, b * P:(b + 1) * P]
            dve.tensor_copy(m.qz_hi[rows, j, :], q).then_inc(m.qz_hi_done, 1)
            dve.wait_ge(m.qz_hi_done, g * HPG + j + 1)
            dve.tensor_tensor(m.qz_lo[rows, j, :], q, m.qz_hi[rows, j, :].bitcast(F32), ALU.subtract).then_inc(
                m.qz_done, 1)

        def keys(g, c):
            dve.tensor_copy(m.k_hi[:, c, :], m.k_all[:, g - b * GROUPS, c * CHUNK:(c + 1) * CHUNK]).then_inc(
                m.k_hi_done, 1)

        def values(g, j):
            cols = bass.ds((g - b * GROUPS) * P + j * XDH, XDH)
            dve.tensor_copy(m.v_grp[:, :, j * XDH:(j + 1) * XDH], m.v_all[:, :, cols]).then_inc(m.v_part_done, 1)

        def maximum(g, j, c):
            dve.wait_ge(m.s_mm, (g * HPG + j) * NCH + c + 1)
            dve.tensor_reduce(m.part_max[:, c:c + 1], m.bank[S_BANKS[c]][:], X_AXIS, ALU.max).then_inc(m.max_done, 1)

        def shift(g, j):
            dve.wait_ge(m.max_done, (g * HPG + j + 1) * NCH)
            dve.tensor_reduce(m.neg_max[:], m.part_max[:], X_AXIS, ALU.max, negate=True).then_inc(m.neg_done, 1)
            dve.wait_ge(m.neg_done, g * HPG + j + 1)
            dve.tensor_tensor(m.shift[:, j:j + 1], m.neg_max[:], m.q_scale[:], ALU.mult).then_inc(m.shift_done, 1)

        def transposed(g, j):
            dve.wait_ge(m.pT_mm, (g * HPG + j) * NCH + 1)
            dve.tensor_copy(m.probs_T[:, T_SLOT[0], :], m.bank[T_BANKS[T_SLOT[0]]][:]).then_inc(m.pT_dve, 1)

        def total(g, j):
            dve.wait_ge(m.exp_done, (g * HPG + j + 1) * NCH)
            dve.tensor_reduce(m.row_sum[:, j:j + 1], m.part_sum[:, j, :], X_AXIS, ALU.add).then_inc(m.sum_done, 1)

        def group(g, more):
            for j in range(1, HPG + 1):
                ahead = (g, j) if j < HPG else (g + 1, 0) if more else None
                for c in range(NCH):
                    if ahead:
                        maximum(*ahead, c)
                        if j == HPG - 1 and more:
                            keys(g + 1, c)
                    if c == 1:
                        transposed(g, j - 1)
                if ahead:
                    shift(*ahead)
                total(g, j - 1)
                if more:
                    queries(g + 1, j - 1)
                    if j > 1:
                        dve.wait_ge(m.pv_mm, (g * HPG + j - 1) * NCH)
                        values(g + 1, j - 2)
            dve.wait_ge(m.sum_done, (g + 1) * HPG)
            dve.reciprocal(m.row_inv[:, bass.ds(g, 1), :].rearrange("p g h -> p (g h)"), m.row_sum[:]).then_inc(
                m.inv_done, 1)
            dve.wait_ge(m.pv_mm, (g + 1) * HPG * NCH)
            dve.tensor_copy(m.o_feat[:, bass.ds(g, 1), :].rearrange("p g t -> p (g t)"), m.bank[O_BANK][:, 0:P]).then_inc(
                m.o_copied, 1)
            if more:
                values(g + 1, HPG - 1)

        for n in range(b * NCH, (b + 1) * NCH):
            for t in range(KT):
                dve.wait_ge(m.v_mm, n * KT + t + 1)
                dve.tensor_copy(m.v_all[:, (n % NCH) * KT + t, :], m.bank[4 + t][:]).then_inc(m.v_done, 1)
            if n == 0:
                mask_and_positions()
            if n % NCH == NCH - 2:
                for j in range(HPG):
                    queries(b * GROUPS, j)
        dve.wait_ge(m.k_done, (b + 1) * NCH * KT)
        for c in range(NCH):
            keys(b * GROUPS, c)
        dve.wait_ge(m.v_done, (b + 1) * NCH * KT)
        for j in range(HPG):
            values(b * GROUPS, j)
        for c in range(NCH):
            maximum(b * GROUPS, 0, c)
        shift(b * GROUPS, 0)
        with dve.Fori(0, GROUPS - 1) as fb:
            group(fb + b * GROUPS, True)
        group((b + 1) * GROUPS - 1, False)
    dve.wait_ge(m.inv_done, NG)
    for b in range(B):
        dve.wait_ge(m.oT_mm, b + 1)
        dve.tensor_tensor(m.o_tok[:, b, :].rearrange("p (h d) -> p h d", h=XH),
                          m.bank[b][:].rearrange("p (h d) -> p h d", h=XH),
                          m.row_inv[:, b * GROUPS:(b + 1) * GROUPS, :].rearrange("p g h -> p (g h)").unsqueeze(
                              2).to_broadcast([P, XH, XDH]), ALU.mult).then_inc(m.oT_done, 1)
    for b in range(B):
        for k in range(KT):
            dve.wait_ge(m.vec_hi, (b + 1) * KT)
            dve.scalar_tensor_tensor(m.vecT_lo[:, k, b * P:(b + 1) * P], m.bank[4 + b][:, k * P:(k + 1) * P],
                                     m.cross_vec[:, 2, k:k + 1], m.vecT_hi[:, k, b * P:(b + 1) * P].bitcast(F32),
                                     ALU.add, ALU.subtract).then_inc(m.vec_lo, 1)
    dve.wait_ge(m.bo_added, B)
    for b in range(B):
        dve.wait_ge(m.o_mm, b + 1)
        dve.tensor_tensor(m.x_res[:, b, :], m.bank[2 + b][:], m.x_res[:, b, :], ALU.add).then_inc(m.x1_done, 1)


def pe_transpose4(pe, m, bank, blocks, identity):
    for t, src in enumerate(blocks):
        last = pe.transpose(bank[:, t * P:(t + 1) * P], src, identity)
    return last


def pe_cross(pe, m):
    pe.wait_ge(m.ident_in, 16)
    for b in range(B):
        pe.wait_ge(m.xn_ready, b + 1)
        pe_transpose4(pe, m, m.bank[b], [m.xn[:, b, k * P:(k + 1) * P] for k in range(KT)], m.ident[:]).then_inc(
            m.xnT_mm, 1)
    wait_unit(pe, m.lo_done, S_WQ)
    pe.wait_ge(m.xT_lo_done, B)
    for f in range(KT):
        for k in range(KT):
            last = three_passes(pe, m.bank[2 + f // 2][:, (f % 2) * B * P:(f % 2 + 1) * B * P],
                                m.k_hi[:, k, f * P:(f + 1) * P], m.k_lo[:, k, f * P:(f + 1) * P],
                                m.xT_hi[:, k, :], m.xT_lo[:, k, :], k == 0, k == KT - 1)
        if f % 2:
            last.then_inc(m.q_mm, 1)
    for b in range(B):
        for n in range(b * NCH, (b + 1) * NCH):
            c_hi, c_lo = ctx_slot(m, n)
            wait_unit(pe, m.lo_done, S_CTX + n)
            if n == 0:
                wait_unit(pe, m.lo_done, S_WK)
                wait_unit(pe, m.lo_done, S_WV)
                pe.wait_ge(m.q_done, KT)
            for f in range(KT):
                if n % NCH:
                    pe.wait_ge(m.k_done, (n - 1) * KT + f + 1)
                for k in range(KT):
                    last = three_passes(pe, m.bank[f][:], m.w_hi[1][:, k, f * P:(f + 1) * P],
                                        m.w_lo[1][:, k, f * P:(f + 1) * P], c_hi[:, k, :], c_lo[:, k, :],
                                        k == 0, k == KT - 1)
                last.then_inc(m.k_mm, 1)
            if n == NCH:
                pe.wait_ge(m.o_copied, GROUPS)
            for t in range(KT):
                if n % NCH:
                    pe.wait_ge(m.v_done, (n - 1) * KT + t + 1)
                for k in range(KT):
                    last = three_passes(pe, m.bank[4 + t][:], c_hi[:, k, t * P:(t + 1) * P],
                                        c_lo[:, k, t * P:(t + 1) * P], m.w_hi[2][:, k, :], m.w_lo[2][:, k, :],
                                        k == 0, k == KT - 1)
                last.then_inc(m.v_mm, 1)
        pe.wait_ge(m.k_done, (b + 1) * NCH * KT)
        pe.wait_ge(m.v_done, (b + 1) * NCH * KT)
        pe.wait_ge(m.mask_ready, 1)
        pe.wait_ge(m.ident_ready, 1)

        def scores(g, j, c, first=False):
            if not first:
                pe.wait_ge(m.exp_done, (g * HPG + j - 1) * NCH + c + 1)
            if j == 0:
                pe.wait_ge(m.k_lo_done, g * NCH + c + 1)
            if c == 0:
                pe.wait_ge(m.qz_done, g * HPG + j + 1)
            bank = m.bank[S_BANKS[c]][:]
            pe.matmul(bank, m.ident_r[:], m.mask_add[:, c * CHUNK:(c + 1) * CHUNK], start=True, stop=False)
            three_passes(pe, bank, m.qz_hi[:, j, :], m.qz_lo[:, j, :], m.k_hi[:, c, :], m.k_lo[:, c, :],
                         False, True).then_inc(m.s_mm, 1)

        def transposed(g, j, c):
            pe.wait_ge(m.exp_done, (g * HPG + j) * NCH + c + 1)
            pe_transpose4(pe, m, m.bank[T_BANKS[T_SLOT[c]]], [m.probs[:, c, t * P:(t + 1) * P] for t in range(KT)],
                          m.ident[:]).then_inc(m.pT_mm, 1)

        def values(g, j, c):
            if c == 0:
                pe.wait_ge(m.v_part_done, g * HPG + j + 1)
            if c == 0:
                pe.wait_ge(m.pT_dve, g * HPG + j + 1)
            else:
                pe.wait_ge(m.pT_act, (g * HPG + j) * (NCH - 1) + c)
            rows = slice(j * XDH, (j + 1) * XDH)
            for t in range(KT):
                last = pe.matmul(m.bank[O_BANK][rows, 0:P], m.v_grp[:, c * KT + t, rows],
                                 m.probs_T[:, T_SLOT[c], t * P:(t + 1) * P], start=(c == 0 and t == 0),
                                 stop=(c == NCH - 1 and t == KT - 1), tile_position=(0, j * XDH))
            last.then_inc(m.pv_mm, 1)

        def group(g, more):
            for j in range(1, HPG + 1):
                ahead = (g, j) if j < HPG else (g + 1, 0) if more else None

                def ahead_scores(c):
                    if ahead:
                        scores(*ahead, c)

                ahead_scores(0)
                ahead_scores(1)
                transposed(g, j - 1, 0)
                ahead_scores(2)
                transposed(g, j - 1, 1)
                values(g, j - 1, 0)
                ahead_scores(3)
                transposed(g, j - 1, 2)
                values(g, j - 1, 1)
                transposed(g, j - 1, 3)
                values(g, j - 1, 2)
                values(g, j - 1, 3)

        for c in range(NCH):
            scores(b * GROUPS, 0, c, first=True)
        with pe.Fori(0, GROUPS - 1) as fb:
            group(fb + b * GROUPS, True)
        group((b + 1) * GROUPS - 1, False)
    pe.wait_ge(m.o_copied, NG)
    for b in range(B):
        pe_transpose4(pe, m, m.bank[b], [m.o_feat[:, b * GROUPS + k, :] for k in range(GROUPS)], m.ident[:]).then_inc(
            m.oT_mm, 1)
    for b in range(B):
        pe.wait_ge(m.oT_done, b + 1)
        pe_transpose4(pe, m, m.bank[4 + b], [m.o_tok[:, b, k * P:(k + 1) * P] for k in range(KT)], m.ident[:]).then_inc(
            m.vec_mm, 1)
    wait_unit(pe, m.lo_done, S_WO)
    slot = S_WO % RING
    for b in range(B):
        pe.wait_ge(m.vec_lo, (b + 1) * KT)
        for k in range(KT):
            last = three_passes(pe, m.bank[2 + b][:], m.vecT_hi[:, k, b * P:(b + 1) * P],
                                m.vecT_lo[:, k, b * P:(b + 1) * P], m.w_hi[slot][:, k, :], m.w_lo[slot][:, k, :],
                                k == 0, k == KT - 1)
        last.then_inc(m.o_mm, 1)


ROW_G1, ROW_B1, ROW_BF, ROW_G2, ROW_B2 = range(5)
SG = 8
KR_BANKS, HT_BANKS = (4, 5), (0, 1)
Q_BANKS, K_BANKS, V_BANKS = (6, 7, 2, 3), (0, 1, 4, 5), (6, 7, 2, 3)
SC_BANKS, PT_BANKS, PV_BANKS = (0, 1, 4, 5), (6, 7), (2, 3)
WO_BANKS, H1T_BANKS, FF1_BANKS, FF2_BANKS = (0, 1), (4, 5), (6, 7, 2, 3), (0, 1)
FF1_OUTS = DF // (2 * P)


def layer_memory(m):
    m.rows = m.sb("rows", [P, 5, D])
    m.h_tok = m.sb("h_tok", [P, B, D])
    m.s_tok = m.sb("s_tok", [P, B, D])
    m.hT_hi = m.sb("hT_hi", [P, KT, B * P], F32R)
    m.hT_lo = m.sb("hT_lo", [P, KT, B * P], F32R)
    m.v_tok = m.sb("v_tok", [P, B, H * DH])
    m.p_lay = m.sb("p_lay", [P, SG, CHUNK])
    m.pT_lay = m.sb("pT_lay", [P, 2, CHUNK])
    m.max_lay = m.sb("max_lay", [P, SG, 4])
    m.shift_lay = m.sb("shift_lay", [P, SG, 4])
    m.sum_lay = m.sb("sum_lay", [P, SG, 4])
    m.inv_lay = m.sb("inv_lay", [P, SG, 4])
    m.vT_hi = m.sb("vT_hi", [P, H // 2, B * P], F32R)
    m.vT_lo = m.sb("vT_lo", [P, H // 2, B * P], F32R)
    m.ff_t = m.sb("ff_t", [P, 2, CHUNK])
    outer = m.ctx
    with ExitStack() as m.ctx:
        m.q_stack = m.sb("q_stack", [P, H, B * P])
        m.k_stack = m.sb("k_stack", [P, H, B * P])
    with ExitStack() as m.ctx:
        m.ff_hi = m.sb("ff_hi", [P, DF // P, B * P], F32R)
        m.ff_lo = m.sb("ff_lo", [P, DF // P, B * P], F32R)
    m.ctx = outer
    (m.rows_in, m.wo_half, m.ff2_part, m.h_ready, m.hT_mm, m.hT_hi_done, m.hT_lo_done, m.kr_mm, m.kr_tok_done, m.krT_mm, m.kr_act,
     m.kr_dve, m.lq_mm, m.lq_act, m.lq_dve, m.lk_mm, m.lk_act, m.lk_dve, m.lv_mm, m.lv_act, m.lv_dve,
     m.sc_mm, m.lmax_done, m.lshift_done, m.lexp_done, m.linv_done, m.lnorm_done, m.lpT_mm, m.lpT_even,
     m.lpT_odd, m.lpv_mm, m.vT_hi_done, m.vT_lo_done, m.wo_mm, m.h1_ready, m.h1T_mm, m.h1T_hi, m.h1T_lo,
     m.ff1_mm, m.relu_done, m.ff_hi_done, m.ff_lo_done, m.ff2_mm, m.dve_step_l, m.x2_done) = m.sems(
        "rows_in wo_half ff2_part h_ready hT_mm hT_hi_done hT_lo_done kr_mm kr_tok_done krT_mm kr_act kr_dve lq_mm lq_act "
        "lq_dve lk_mm lk_act lk_dve lv_mm lv_act lv_dve sc_mm lmax_done lshift_done lexp_done linv_done "
        "lnorm_done lpT_mm lpT_even lpT_odd lpv_mm vT_hi_done vT_lo_done wo_mm h1_ready h1T_mm h1T_hi "
        "h1T_lo ff1_mm relu_done ff_hi_done ff_lo_done ff2_mm dve_step_l x2_done")


def sp_layers(sp, m):
    sp.wait_ge(m.uv_in, 16)
    with sp.Fori(0, L) as i:
        for k in range(RING, LU + RING):
            wait_unit(sp, m.lo_done, S_LAYER + k - RING, i, LU)
            sp.dma_start(m.raw[:, k % RING, :], m.dram["w_stream"][bass.ds(i * LU + k, 1)].rearrange(
                "a p n -> (a p) n")).then_inc(m.loaded[k % RING], 16)
            if k == U_WK:
                sp.wait_ge(m.h_ready, (i + 1) * B)
                sp.dma_start(m.rows[:], m.dram["layer_rows"][bass.ds(i, 1)].rearrange(
                    "a r d -> (a r) d").partition_broadcast(P)).then_inc(m.rows_in, 16)


def pool_layers(pool, m):
    split_lo(pool, m, S_LAYER + 2)
    with pool.Fori(0, L) as i:
        for k in range(RING, LU + RING):
            split_lo(pool, m, S_LAYER + k, i, LU)


def by_block(bank):
    return bank[:].rearrange("p (k t) -> p k t", t=P)


def pairs(bank):
    return bank[:].rearrange("p (k t) -> p k t", t=B * P)


def act_layers(act, m):
    act.wait_ge(m.o_mm, B)
    split_hi(act, m, S_LAYER + 2)
    for t in range(B):
        ln_root(act, m, 2, t)
    act.wait_ge(m.uv_in, 16)
    act.wait_ge(m.bias_in, 16)
    with act.Fori(0, L) as i:

        def unit(k):
            act.wait_ge(*unit_used(m, k - RING, i))
            split_hi(act, m, S_LAYER + k, i, LU)

        for u in range(2):
            act.wait_ge(m.kr_mm, i * 2 + u + 1)
            act.activation(m.ff_t[:, u, :], m.bank[KR_BANKS[u]][:], ACT.Copy).then_inc(m.kr_tok_done, 1)
            if u == 0:
                unit(RING)
        for b in range(B):
            act.wait_ge(m.hT_mm, i * B + b + 1)
            act.activation(m.hT_hi[:, :, b * P:(b + 1) * P], by_block(m.bank[HT_BANKS[b]]), ACT.Copy).then_inc(
                m.hT_hi_done, 1)
        unit(RING + 1)
        for u in range(2):
            act.wait_ge(m.krT_mm, i * 2 + u + 1)
            for b in range(B):
                last = act.activation(m.k_stack[DH:P, 8 * u + 1:8 * u + 8:2, b * P:(b + 1) * P],
                                      by_block(m.bank[KR_BANKS[u]])[DH:P], ACT.Copy)
            last.then_inc(m.kr_act, 1)
        for o in range(4):
            act.wait_ge(m.lq_mm, i * 4 + o + 1)
            for t in range(2):
                head = 4 * o + 2 * t + 1
                for w in range(2):
                    last = act.activation(m.q_stack[w * DH:(w + 1) * DH, head, :],
                                          pairs(m.bank[Q_BANKS[o]])[DH:P, t, :], ACT.Identity,
                                          bias=m.uv_sb[DH:P, w, head:head + 1])
            last.then_inc(m.lq_act, 1)
            if o % 2:
                unit(5 + o // 2)
        for o in range(4):
            act.wait_ge(m.lk_mm, i * 4 + o + 1)
            act.activation(m.k_stack[0:DH, 4 * o + 1:4 * o + 4:2, :], pairs(m.bank[K_BANKS[o]])[DH:P],
                           ACT.Copy).then_inc(m.lk_act, 1)
            if o % 2:
                unit(7 + o // 2)
        def values(u):
            act.wait_ge(m.lv_mm, i * 4 + 2 * u + 2)
            act.activation(m.v_tok[:, 1, u * CHUNK:(u + 1) * CHUNK], m.bank[V_BANKS[2 * u + 1]][:],
                           ACT.Copy).then_inc(m.lv_act, 1)
            unit(9 + u)

        def exps(g):
            act.wait_ge(m.lshift_done, i * SG + g + 1)
            for t in range(4):
                last = act.activation(m.p_lay[:, g, t * P:(t + 1) * P],
                                      m.bank[SC_BANKS[g % 4]][:, t * P:(t + 1) * P], ACT.Exp,
                                      bias=m.shift_lay[:, g, t:t + 1], scale=L_SCALE, accum_out=m.sum_lay[:, g, t:t + 1])
            last.then_inc(m.lexp_done, 1)

        def transposed(g):
            act.wait_ge(m.lpT_mm, i * SG + g + 1)
            if g >= 2:
                act.wait_ge(m.lpv_mm, i * SG + g - 1)
            act.activation(m.pT_lay[:, 1, :], m.bank[PT_BANKS[1]][:], ACT.Copy).then_inc(m.lpT_odd, 1)

        def vector_hi(q):
            b, half = q // 2, q % 2
            act.wait_ge(m.lpv_mm, i * SG + 2 * q + 2)
            act.activation(m.vT_hi[:, 4 * half:4 * half + 4, b * P:(b + 1) * P], by_block(m.bank[PV_BANKS[half]]),
                           ACT.Copy).then_inc(m.vT_hi_done, 1)

        exps(0)
        exps(1)
        values(0)
        for g in range(2, 6):
            exps(g)
        values(1)
        exps(6)
        transposed(1)
        exps(7)
        transposed(3)
        vector_hi(0)
        transposed(5)
        vector_hi(1)
        transposed(7)
        vector_hi(2)
        vector_hi(3)
        ln_root(act, m, i * 2 + 3, 0)
        unit(11)
        ln_root(act, m, i * 2 + 3, 1)
        unit(12)
        for b in range(B):
            act.wait_ge(m.h1T_mm, i * B + b + 1)
            act.activation(m.hT_hi[:, :, b * P:(b + 1) * P], by_block(m.bank[H1T_BANKS[b]]), ACT.Copy).then_inc(
                m.h1T_hi, 1)
        for f in range(FF1_OUTS):
            act.wait_ge(m.ff1_mm, i * FF1_OUTS + f + 1)
            if f >= 2:
                act.wait_ge(m.ff_lo_done, i * FF1_OUTS + f - 1)
            for t in range(2):
                last = act.activation(m.ff_t[:, f % 2, t * B * P:(t + 1) * B * P], pairs(m.bank[FF1_BANKS[f % 4]])[:, t, :],
                                      ACT.Relu, bias=m.ff1_bias_sb[:, bass.ds(i, 1), 2 * f + t])
            last.then_inc(m.relu_done, 1)
            if f % 2:
                unit(13 + f // 2)
        unit(17)
        unit(18)
        ln_root(act, m, i * 2 + 4, 0)
        unit(19)
        ln_root(act, m, i * 2 + 4, 1)
        unit(20)


def dve_layers(dve, m, step):
    dve.wait_ge(m.x1_done, B)
    for b in range(B):
        ln_scale(dve, m, step, m.x_res[:, b, :], b, 2)
        step.wait()
        ln_apply(dve, m, m.h_tok[:, b, :], m.x_res[:, b, :], b).then_inc(m.h_ready, 1)
    dve.wait_ge(m.uv_in, 16)
    with dve.Fori(0, L) as i:
        own = Step(dve, m.dve_step_l, 0, i, 32)
        for b in range(B):
            dve.wait_ge(m.hT_hi_done, i * B + b + 1)
            dve.tensor_tensor(m.hT_lo[:, :, b * P:(b + 1) * P], by_block(m.bank[HT_BANKS[b]]),
                              m.hT_hi[:, :, b * P:(b + 1) * P].bitcast(F32), ALU.subtract).then_inc(m.hT_lo_done, 1)
        for u in range(2):
            dve.wait_ge(m.krT_mm, i * 2 + u + 1)
            for b in range(B):
                last = dve.tensor_copy(m.k_stack[DH:P, 8 * u:8 * u + 8:2, b * P:(b + 1) * P],
                                       by_block(m.bank[KR_BANKS[u]])[0:DH])
            last.then_inc(m.kr_dve, 1)
        for o in range(4):
            dve.wait_ge(m.lq_mm, i * 4 + o + 1)
            heads = slice(4 * o, 4 * o + 4, 2)
            for w in range(2):
                last = dve.tensor_tensor(m.q_stack[w * DH:(w + 1) * DH, heads, :], pairs(m.bank[Q_BANKS[o]])[0:DH],
                                         m.uv_sb[0:DH, w, heads].unsqueeze(2).to_broadcast([DH, 2, B * P]), ALU.add)
            last.then_inc(m.lq_dve, 1)
        for o in range(4):
            dve.wait_ge(m.lk_mm, i * 4 + o + 1)
            dve.tensor_copy(m.k_stack[0:DH, 4 * o:4 * o + 4:2, :], pairs(m.bank[K_BANKS[o]])[0:DH]).then_inc(
                m.lk_dve, 1)
        def values(u):
            dve.wait_ge(m.lv_mm, i * 4 + 2 * u + 1)
            dve.tensor_copy(m.v_tok[:, 0, u * CHUNK:(u + 1) * CHUNK], m.bank[V_BANKS[2 * u]][:]).then_inc(m.lv_dve, 1)

        def maxima(g):
            dve.wait_ge(m.sc_mm, i * SG + g + 1)
            dve.tensor_reduce(m.max_lay[:, g, :], by_block(m.bank[SC_BANKS[g % 4]]), X_AXIS, ALU.max,
                              negate=True).then_inc(m.lmax_done, 1)
            dve.wait_ge(m.lmax_done, i * SG + g + 1)
            dve.tensor_scalar(m.shift_lay[:, g, :], m.max_lay[:, g, :], L_SCALE, None, ALU.mult).then_inc(
                m.lshift_done, 1)

        def normed(g):
            dve.wait_ge(m.lexp_done, i * SG + g + 1)
            dve.reciprocal(m.inv_lay[:, g, :], m.sum_lay[:, g, :]).then_inc(m.linv_done, 1)
            dve.wait_ge(m.linv_done, i * SG + g + 1)
            p = m.p_lay[:, g, :].rearrange("p (h t) -> p h t", h=4)
            dve.tensor_tensor(p, p, m.inv_lay[:, g, :].unsqueeze(2).to_broadcast([P, 4, P]), ALU.mult).then_inc(
                m.lnorm_done, 1)

        def transposed(g):
            dve.wait_ge(m.lpT_mm, i * SG + g + 1)
            if g >= 2:
                dve.wait_ge(m.lpv_mm, i * SG + g - 1)
            dve.tensor_copy(m.pT_lay[:, 0, :], m.bank[PT_BANKS[0]][:]).then_inc(m.lpT_even, 1)

        def vector_lo(q):
            b, half = q // 2, q % 2
            dve.wait_ge(m.vT_hi_done, i * 4 + q + 1)
            hi = m.vT_hi[:, 4 * half:4 * half + 4, b * P:(b + 1) * P]
            dve.tensor_tensor(m.vT_lo[:, 4 * half:4 * half + 4, b * P:(b + 1) * P], by_block(m.bank[PV_BANKS[half]]),
                              hi.bitcast(F32), ALU.subtract).then_inc(m.vT_lo_done, 1)

        values(0)
        for g in range(0, SG, 2):
            if g == 4:
                values(1)
            maxima(g)
            if g == 6:
                transposed(0)
            maxima(g + 1)
            if g == 6:
                transposed(2)
            normed(g)
            normed(g + 1)
        vector_lo(0)
        transposed(4)
        vector_lo(1)
        transposed(6)
        vector_lo(2)
        vector_lo(3)

        def layer_norm(dst, t, n, g, b, sem):
            src = m.s_tok[:, t, :]
            own.wait()
            ln_scale(dve, m, own, src, t, n)
            own.done(dve.scalar_tensor_tensor(src, src, m.mean_var[:, t, 0:1], m.rows[:, g, :], ALU.subtract, ALU.mult))
            own.wait()
            dve.scalar_tensor_tensor(dst[:, t, :], src, m.rstd[:, t:t + 1], m.rows[:, b, :], ALU.mult, ALU.add).then_inc(
                sem, 1)

        dve.wait_ge(m.rows_in, i * 16 + 16)
        dve.wait_ge(m.h_ready, (i + 1) * B)
        for b in range(B):
            dve.wait_ge(m.wo_mm, i * B + b + 1)
            own.done(dve.tensor_tensor(m.s_tok[:, b, :], m.bank[WO_BANKS[b]][:], m.h_tok[:, b, :], ALU.add))
            layer_norm(m.s_tok, b, i * 2 + 3, ROW_G1, ROW_B1, m.h1_ready)
        for b in range(B):
            dve.wait_ge(m.h1T_hi, i * B + b + 1)
            dve.tensor_tensor(m.hT_lo[:, :, b * P:(b + 1) * P], by_block(m.bank[H1T_BANKS[b]]),
                              m.hT_hi[:, :, b * P:(b + 1) * P].bitcast(F32), ALU.subtract).then_inc(m.h1T_lo, 1)
        for f in range(FF1_OUTS):
            dve.wait_ge(m.relu_done, i * FF1_OUTS + f + 1)
            hi = m.ff_hi[:, 2 * f:2 * f + 2, :].rearrange("p k t -> p (k t)")
            dve.tensor_copy(hi, m.ff_t[:, f % 2, :]).then_inc(m.ff_hi_done, 1)
            dve.wait_ge(m.ff_hi_done, i * FF1_OUTS + f + 1)
            dve.tensor_tensor(m.ff_lo[:, 2 * f:2 * f + 2, :].rearrange("p k t -> p (k t)"), m.ff_t[:, f % 2, :],
                              hi.bitcast(F32), ALU.subtract).then_inc(m.ff_lo_done, 1)
        for b in range(B):
            dve.wait_ge(m.ff2_mm, i * B + b + 1)
            own.done(dve.tensor_tensor(m.s_tok[:, b, :], m.bank[FF2_BANKS[b]][:], m.rows[:, ROW_BF, :], ALU.add))
            layer_norm(m.h_tok, b, i * 2 + 4, ROW_G2, ROW_B2, m.h_ready)
        assert own.n == own.per, own.n
    dve.wait_ge(m.h_ready, (L + 1) * B)
    for b in range(B):
        dve.tensor_tensor(m.x_res[:, b, :], m.x_res[:, b, :], m.h_tok[:, b, :], ALU.add).then_inc(m.x2_done, 1)


def unit_used(m, u, i):
    if u < U_WQ:
        return m.kr_mm, i * 2 + u + 1
    if u < U_WO:
        return (m.lq_mm, m.lk_mm, m.lv_mm)[(u - U_WQ) // 2], i * 4 + 2 * (u % 2) + 2
    if u < U_FF1:
        return (m.wo_half, i + 1) if u == U_WO else (m.wo_mm, i * B + B)
    if u < U_FF2:
        return m.ff1_mm, i * FF1_OUTS + 2 * (u - U_FF1) + 2
    return (m.ff2_part, i * 3 + u - U_FF2 + 1) if u < LU - 1 else (m.ff2_mm, i * B + B)


def pe_layers(pe, m):
    wait_unit(pe, m.lo_done, S_WO)
    pe.wait_ge(m.x1_done, B)
    pe.wait_ge(m.r_ready, 1)
    with pe.Fori(0, L) as i:

        def unit(k):
            wait_unit(pe, m.lo_done, S_LAYER + k, i, LU)
            return m.w_hi[k % RING], m.w_lo[k % RING]

        for u in range(2):
            w_hi, w_lo = unit(U_WR + u)
            for k in range(KT):
                last = three_passes(pe, m.bank[KR_BANKS[u]][:], m.r_hi[:, k, :], m.r_lo[:, k, :], w_hi[:, k, :],
                                    w_lo[:, k, :], k == 0, k == KT - 1)
            last.then_inc(m.kr_mm, 1)

        def position_keys(u):
            pe.wait_ge(m.kr_tok_done, i * 2 + u + 1)
            pe_transpose4(pe, m, m.bank[KR_BANKS[u]], [m.ff_t[:, u, t * P:(t + 1) * P] for t in range(4)],
                          m.ident[:]).then_inc(m.krT_mm, 1)

        position_keys(0)
        for b in range(B):
            pe.wait_ge(m.h_ready, i * B + b + 1)
            pe_transpose4(pe, m, m.bank[HT_BANKS[b]], [m.h_tok[:, b, k * P:(k + 1) * P] for k in range(KT)],
                          m.ident[:]).then_inc(m.hT_mm, 1)
        position_keys(1)
        pe.wait_ge(m.hT_lo_done, (i + 1) * B)

        def by_feature(unit0, banks, sem, free):
            for o in range(4):
                if o % 2 == 0:
                    w_hi, w_lo = unit(unit0 + o // 2)
                free(o)
                for q in range(2):
                    cols = slice((2 * (o % 2) + q) * P, (2 * (o % 2) + q + 1) * P)
                    for k in range(KT):
                        last = three_passes(pe, m.bank[banks[o]][:, q * B * P:(q + 1) * B * P], w_hi[:, k, cols],
                                            w_lo[:, k, cols], m.hT_hi[:, k, :], m.hT_lo[:, k, :],
                                            k == 0, k == KT - 1)
                last.then_inc(sem, 1)

        def k_bank_free(o):
            if o >= 2:
                pe.wait_ge(m.kr_dve, i * 2 + o - 1)
                pe.wait_ge(m.kr_act, i * 2 + o - 1)

        by_feature(U_WQ, Q_BANKS, m.lq_mm, lambda o: None)
        by_feature(U_WK, K_BANKS, m.lk_mm, k_bank_free)

        def value_rows(u, b):
            w_hi, w_lo = unit(U_WV + u)
            pe.wait_ge(m.lq_act, i * 4 + 2 * u + b + 1)
            pe.wait_ge(m.lq_dve, i * 4 + 2 * u + b + 1)
            for k in range(KT):
                last = three_passes(pe, m.bank[V_BANKS[2 * u + b]][:], m.hT_hi[:, k, b * P:(b + 1) * P],
                                    m.hT_lo[:, k, b * P:(b + 1) * P], w_hi[:, k, :], w_lo[:, k, :],
                                    k == 0, k == KT - 1)
            last.then_inc(m.lv_mm, 1)

        def scores(g):
            if g == 0:
                pe.wait_ge(m.lk_act, i * 4 + 4)
                pe.wait_ge(m.lk_dve, i * 4 + 4)
            if g >= 4:
                pe.wait_ge(m.lexp_done, i * SG + g - 3)
            b = g // 4
            for t in range(4):
                head = 4 * (g % 4) + t
                last = pe.matmul(m.bank[SC_BANKS[g % 4]][:, t * P:(t + 1) * P], m.q_stack[:, head, b * P:(b + 1) * P],
                                 m.k_stack[:, head, b * P:(b + 1) * P], start=True, stop=True)
            last.then_inc(m.sc_mm, 1)

        def transposed(g):
            pe.wait_ge(m.lnorm_done, i * SG + g + 1)
            if g < 2:
                pe.wait_ge((m.lv_dve, m.lv_act)[g], i * 2 + 1)
            else:
                pe.wait_ge((m.lpT_even, m.lpT_odd)[g % 2], i * 4 + g // 2)
            pe_transpose4(pe, m, m.bank[PT_BANKS[g % 2]], [m.p_lay[:, g, t * P:(t + 1) * P] for t in range(4)],
                          m.ident[:]).then_inc(m.lpT_mm, 1)

        def values(g):
            pe.wait_ge((m.lpT_even, m.lpT_odd)[g % 2], i * 4 + g // 2 + 1)
            half, b = (g % 4) // 2, g // 4
            if g == 0:
                pe.wait_ge(m.lv_dve, i * 2 + 2)
                pe.wait_ge(m.lv_act, i * 2 + 2)
            if g >= 4:
                pe.wait_ge(m.vT_lo_done, i * 4 + half + 1)
            for t in range(4):
                head = 4 * (g % 4) + t
                side, block = head % 2, (head // 2) % 4
                last = pe.matmul(m.bank[PV_BANKS[half]][side * DH:(side + 1) * DH, block * P:(block + 1) * P],
                                 m.v_tok[:, b, head * DH:(head + 1) * DH], m.pT_lay[:, g % 2, t * P:(t + 1) * P],
                                 start=True, stop=True, tile_position=(0, side * DH))
            last.then_inc(m.lpv_mm, 1)

        for pair in range(4):
            value_rows(pair // 2, pair % 2)
            scores(2 * pair)
            if pair == 3:
                transposed(0)
            scores(2 * pair + 1)
        for g in range(SG):
            if g + 1 < SG:
                transposed(g + 1)
            values(g)
        for b in range(B):
            for u in range(2):
                w_hi, w_lo = unit(U_WO + u)
                if u == 0:
                    pe.wait_ge(m.vT_lo_done, i * 4 + 2 * b + 2)
                for k in range(KT):
                    last = three_passes(pe, m.bank[WO_BANKS[b]][:], m.vT_hi[:, KT * u + k, b * P:(b + 1) * P],
                                        m.vT_lo[:, KT * u + k, b * P:(b + 1) * P], w_hi[:, k, :], w_lo[:, k, :],
                                        u == 0 and k == 0, u == 1 and k == KT - 1)
                if u == 1:
                    last.then_inc(m.wo_mm, 1)
                elif b == B - 1:
                    last.then_inc(m.wo_half, 1)
        for b in range(B):
            pe.wait_ge(m.h1_ready, i * B + b + 1)
            pe_transpose4(pe, m, m.bank[H1T_BANKS[b]], [m.s_tok[:, b, k * P:(k + 1) * P] for k in range(KT)],
                          m.ident[:]).then_inc(m.h1T_mm, 1)
        pe.wait_ge(m.h1T_lo, (i + 1) * B)
        for f in range(FF1_OUTS):
            if f % 2 == 0:
                w_hi, w_lo = unit(U_FF1 + f // 2)
            if f >= 4:
                pe.wait_ge(m.relu_done, i * FF1_OUTS + f - 3)
            for q in range(2):
                cols = slice((2 * (f % 2) + q) * P, (2 * (f % 2) + q + 1) * P)
                for k in range(KT):
                    last = three_passes(pe, m.bank[FF1_BANKS[f % 4]][:, q * B * P:(q + 1) * B * P], w_hi[:, k, cols],
                                        w_lo[:, k, cols], m.hT_hi[:, k, :], m.hT_lo[:, k, :], k == 0, k == KT - 1)
            last.then_inc(m.ff1_mm, 1)
        for u, b in ((0, 0), (0, 1), (1, 0), (1, 1), (2, 0), (3, 0), (2, 1), (3, 1)):
            w_hi, w_lo = unit(U_FF2 + u)
            pe.wait_ge(m.ff_lo_done, i * FF1_OUTS + 2 * u + 2)
            for k in range(KT):
                last = three_passes(pe, m.bank[FF2_BANKS[b]][:], m.ff_hi[:, KT * u + k, b * P:(b + 1) * P],
                                    m.ff_lo[:, KT * u + k, b * P:(b + 1) * P], w_hi[:, k, :], w_lo[:, k, :],
                                    u == 0 and k == 0, u == 3 and k == KT - 1)
            if u == 3:
                last.then_inc(m.ff2_mm, 1)
            elif b == B - 1:
                last.then_inc(m.ff2_part, 1)


EXTRA = (B * P * 2 - 1) // (P + 1)
TURNS = E + EXTRA + 1
QUARTERS = F // CHUNK
E_RING = 2 * RING
UP_UNITS = [k for k, (name, _) in enumerate(E_ORDER) if name != "wo"]
DOWN_UNITS = [k for k, (name, _) in enumerate(E_ORDER) if name == "wo"]
UP_BANKS, HIDDEN_BANK, Y_BANK, XG_BANKS = (0, 2), 4, 5, (6, 7)
BELOW_ALL = -3e38


def moe_memory(m):
    m.xn_tok = m.sb("xn_tok", [P, B, D])
    m.xn_hi = m.sb("xn_hi", [P, B, D], F32R)
    m.xn_lo = m.sb("xn_lo", [P, B, D], F32R)
    m.xn_T = m.sb("xn_T", [P, KT, B * P])
    m.logits = m.sb("logits", [P, B, E])
    m.is_max = m.sb("is_max", [P, B, E])
    m.candidate = m.sb("candidate", [P, B, E])
    m.chosen1 = m.sb("chosen1", [P, B, E])
    m.chosen2 = m.sb("chosen2", [P, B, E])
    m.rest = m.sb("rest", [P, B, E])
    m.routed = m.sb("routed", [P, B, E])
    m.weighted1 = m.sb("weighted1", [P, B, E])
    m.position = m.sb("position", [P, B, E])
    m.best1 = m.sb("best1", [P, B])
    m.best2 = m.sb("best2", [P, B])
    m.first1 = m.sb("first1", [P, B])
    m.first2 = m.sb("first2", [P, B])
    m.gap = m.sb("gap", [P, B])
    m.gap_exp = m.sb("gap_exp", [P, B])
    m.gap_sum = m.sb("gap_sum", [P, B])
    m.weight1 = m.sb("weight1", [P, B])
    m.weight2 = m.sb("weight2", [P, B])
    m.slot_of = m.sb("slot_of", [P, B, TURNS])
    m.gate_of = m.sb("gate_of", [P, B, TURNS])
    m.crowded = m.sb("crowded", [P, EXTRA + 1, E])
    m.order = m.sb("order", [P, E])
    m.first_one = m.sb("first_one", [P, 1])
    m.extra = m.sb("extra", [P, EXTRA, E])
    m.extra_index = m.sb("extra_index", [P, EXTRA, E])
    m.extra_gate = m.sb("extra_gate", [P, B, EXTRA, E])
    m.extra_position = m.sb("extra_position", [P, B, EXTRA, E])
    m.extra_slot = m.sb("extra_slot", [P, B, EXTRA])
    m.n_crowded = m.sb("n_crowded", [P, 1])
    m.n_turns = m.sb("n_turns", [P, 1], I32)
    m.expert_f = m.sb("expert_f", [P, TURNS])
    m.expert_of = m.sb("expert_of", [P, TURNS], I32)
    more = range(RING, E_RING)
    m.raw_more = m.sb("raw_more", [P, RING, KT * CHUNK])
    m.e_raw = [m.raw[:, s, :] for s in range(RING)] + [m.raw_more[:, s, :] for s in range(RING)]
    m.e_hi = m.w_hi + [m.sb(f"w_hi{s}", [P, KT, CHUNK], F32R) for s in more]
    m.e_lo = m.w_lo + [m.sb(f"w_lo{s}", [P, KT, CHUNK], F32R) for s in more]
    m.e_loaded = m.loaded + m.slot_sems("loaded_more")
    m.e_hi_done = m.hi_done + m.slot_sems("hi_done_more")
    m.e_lo_done = m.lo_done + m.slot_sems("lo_done_more")
    m.pick = m.sb("pick", [P, B, P], F32R)
    m.pick_gate = m.sb("pick_gate", [P, B, P])
    m.pick_gate_T = m.sb("pick_gate_T", [P, B, P])
    m.xg_hi = m.sb("xg_hi", [P, KT, P], F32R)
    m.xg_lo = m.sb("xg_lo", [P, KT, P], F32R)
    m.silu = m.sb("silu", [P, 2, CHUNK])
    m.hidden = m.sb("hidden", [P, 2, CHUNK])
    m.hidden_hi = m.sb("hidden_hi", [P, 2, CHUNK], F32R)
    m.hidden_lo = m.sb("hidden_lo", [P, 2, CHUNK], F32R)
    m.y = m.sb("y", [P, D])
    (m.xn2_ready, m.xn2_hi, m.xn2_lo, m.xn2_mm, m.xn2_T, m.logit_mm, m.gap_done, m.gap_exp_done,
     m.routed_done, m.rank_mm, m.n_ready, m.pick_done, m.gather_mm, m.xg_hi_done, m.xg_lo_done,
     m.gateT_mm, m.gateT_done, m.up_mm, m.silu_done, m.hidden_done, m.hiddenT_mm, m.hidden_hi_done,
     m.hidden_lo_done, m.down_mm, m.y_done, m.scatter_mm, m.acc_done, m.table_ready) = m.sems(
        "xn2_ready xn2_hi xn2_lo xn2_mm xn2_T logit_mm gap_done gap_exp_done routed_done rank_mm n_ready "
        "pick_done gather_mm xg_hi_done xg_lo_done gateT_mm gateT_done up_mm silu_done hidden_done "
        "hiddenT_mm hidden_hi_done hidden_lo_done down_mm y_done scatter_mm acc_done table_ready")


def e_slot(k):
    return k % E_RING


def e_wait(eng, sem, k, i, each=1):
    before = S_MOE // RING if e_slot(k) < RING else 0
    eng.wait_ge(sem[e_slot(k)], (i * (EU // E_RING) + before + k // E_RING + 1) * each)


def e_split_hi(act, m, k, i):
    s = e_slot(k)
    e_wait(act, m.e_loaded, k, i, 16)
    act.activation(m.e_hi[s][:].rearrange("p k n -> p (k n)"), m.e_raw[s], ACT.Copy).then_inc(m.e_hi_done[s], 1)


def e_split_lo(eng, m, k, i):
    s = e_slot(k)
    e_wait(eng, m.e_hi_done, k, i)
    eng.tensor_tensor(m.e_lo[s][:].rearrange("p k n -> p (k n)"), m.e_raw[s],
                      m.e_hi[s][:].rearrange("p k n -> p (k n)").bitcast(F32), ALU.subtract).then_inc(m.e_lo_done[s], 1)


def e_unit_used(m, k, i):
    if k in UP_UNITS:
        return m.up_mm, i * len(UP_UNITS) + UP_UNITS.index(k) + 1
    return m.down_mm, i * QUARTERS + DOWN_UNITS.index(k) + 1


def turns(eng, m):
    eng.wait_ge(m.n_ready, 1)
    return eng.value_load(m.n_turns[0:1, 0:1], min_val=E, max_val=E + EXTRA)


def sp_moe(sp, m):
    sp.wait_ge(m.x2_done, B)
    for s in range(RING, E_RING):
        sp.dma_start(m.e_raw[s], m.dram["w_stream"][L * LU + s]).then_inc(m.e_loaded[s], 16)
    n = turns(sp, m)
    sp.wait_ge(m.table_ready, 1)
    with sp.Fori(0, n) as i:
        expert = sp.value_load(m.expert_of[0:1, bass.ds(i, 1)], min_val=0, max_val=E - 1)
        after = sp.value_load(m.expert_of[0:1, bass.ds(i + 1, 1)], min_val=0, max_val=E - 1)
        for k in range(E_RING, EU + E_RING):
            at = expert * EU + (L * LU + k) if k < EU else after * EU + (L * LU + k - EU)
            e_wait(sp, m.e_lo_done, k - E_RING, i)
            sp.dma_start(m.e_raw[e_slot(k)], m.dram["w_stream"][bass.ds(at, 1)].rearrange("a p n -> (a p) n")
                         ).then_inc(m.e_loaded[e_slot(k)], 16)
    sp.wait_ge(m.acc_done, n * B)
    sp.dma_start(m.dram["out"].rearrange("b p d -> p b d"), m.x_res[:]).then_inc(m.out_done, 16)
    sp.wait_ge(m.out_done, 16)


def pool_moe(pool, m):
    for k in range(RING, E_RING):
        e_split_lo(pool, m, k, 0)
    with pool.Fori(0, turns(pool, m)) as i:
        for k in range(E_RING, EU + E_RING, RING):
            e_split_lo(pool, m, k, i)


def act_moe(act, m):
    for t in range(B):
        ln_root(act, m, 2 * L + 3, t)
    for b in range(B):
        act.wait_ge(m.xn2_ready, b + 1)
        act.activation(m.xn_hi[:, b, :], m.xn_tok[:, b, :], ACT.Copy).then_inc(m.xn2_hi, 1)
    for k in range(RING, E_RING):
        e_split_hi(act, m, k, 0)
    act.wait_ge(m.gap_done, 1)
    act.activation(m.gap_exp[:], m.gap[:], ACT.Exp).then_inc(m.gap_exp_done, 1)

    def gathered(e):
        act.wait_ge(m.gather_mm, e * 2 + 1)
        act.activation(m.xg_hi[:], by_block(m.bank[XG_BANKS[0]]), ACT.Copy).then_inc(m.xg_hi_done, 1)

    gathered(0)
    with act.Fori(0, turns(act, m)) as i:

        def unit(k):
            act.wait_ge(*e_unit_used(m, k - E_RING, i))
            e_split_hi(act, m, k, i)

        def silu(j):
            act.wait_ge(m.up_mm, i * len(UP_UNITS) + 2 * j + 1)
            act.activation(m.silu[:, j % 2, :], m.bank[UP_BANKS[j % 2]][:], ACT.Silu).then_inc(m.silu_done, 1)

        def hidden(j):
            act.wait_ge(m.hiddenT_mm, i * QUARTERS + j + 1)
            act.activation(m.hidden_hi[:, j % 2, :], m.bank[HIDDEN_BANK][:], ACT.Copy).then_inc(m.hidden_hi_done, 1)

        unit(6)
        silu(0)
        unit(7)
        act.wait_ge(m.gateT_mm, i + 1)
        act.activation(m.pick_gate_T[:].rearrange("p b t -> p (b t)"), m.bank[HIDDEN_BANK][:, 0:B * P], ACT.Copy).then_inc(
            m.gateT_done, 1)
        unit(8)
        silu(1)
        unit(9)
        hidden(0)
        unit(10)
        unit(11)
        silu(2)
        hidden(1)
        unit(12)
        unit(13)
        unit(14)
        silu(3)
        hidden(2)
        unit(15)
        gathered(i + 1)
        hidden(3)
        unit(16)
        act.wait_ge(m.down_mm, i * QUARTERS + QUARTERS)
        act.activation(m.y[:], m.bank[Y_BANK][:], ACT.Copy).then_inc(m.y_done, 1)
        unit(17)


def dve_moe(dve, m, step):
    dve.wait_ge(m.x2_done, B)
    for b in range(B):
        ln_scale(dve, m, step, m.x_res[:, b, :], b, 2 * L + 3)
        step.wait()
        ln_apply(dve, m, m.xn_tok[:, b, :], m.x_res[:, b, :], b).then_inc(m.xn2_ready, 1)
    for b in range(B):
        dve.wait_ge(m.xn2_mm, b + 1)
        dve.tensor_copy(m.xn_T[:, :, b * P:(b + 1) * P], by_block(m.bank[b])).then_inc(m.xn2_T, 1)
    for b in range(B):
        dve.wait_ge(m.xn2_hi, b + 1)
        dve.tensor_tensor(m.xn_lo[:, b, :], m.xn_tok[:, b, :], m.xn_hi[:, b, :].bitcast(F32), ALU.subtract).then_inc(
            m.xn2_lo, 1)
    dve.wait_ge(m.logit_mm, 1)
    dve.wait_ge(m.consts_in, 48)

    def do(ins):
        step.done(ins)
        step.wait()

    def over_experts(t):
        return t[:].unsqueeze(2).to_broadcast([P, B, E])

    iota = m.iota[:, 0:E].unsqueeze(1).to_broadcast([P, B, E])
    do(dve.tensor_copy(m.logits[:].rearrange("p b e -> p (b e)"), m.bank[2][:, 0:B * E]))
    for scores, best, first, chosen in ((m.logits, m.best1, m.first1, m.chosen1), (m.rest, m.best2, m.first2, m.chosen2)):
        do(dve.tensor_reduce(best[:], scores[:], X_AXIS, ALU.max))
        do(dve.tensor_tensor(m.is_max[:], scores[:], over_experts(best), ALU.is_equal))
        do(dve.scalar_tensor_tensor(m.candidate[:], m.is_max[:], -float(E), iota, ALU.mult, ALU.add))
        do(dve.tensor_reduce(first[:], m.candidate[:], X_AXIS, ALU.min))
        do(dve.tensor_tensor(chosen[:], m.candidate[:], over_experts(first), ALU.is_equal))
        if chosen is m.chosen1:
            do(dve.scalar_tensor_tensor(m.rest[:], chosen[:], BELOW_ALL, m.logits[:], ALU.mult, ALU.add))
    dve.tensor_tensor(m.routed[:], m.chosen1[:], m.chosen2[:], ALU.add).then_inc(m.routed_done, 1)
    dve.tensor_tensor(m.gap[:], m.best2[:], m.best1[:], ALU.subtract).then_inc(m.gap_done, 1)
    dve.wait_ge(m.gap_exp_done, 1)
    do(dve.tensor_scalar(m.gap_sum[:], m.gap_exp[:], 1.0, None, ALU.add))
    do(dve.reciprocal(m.weight1[:], m.gap_sum[:]))
    do(dve.tensor_tensor(m.weight2[:], m.gap_exp[:], m.weight1[:], ALU.mult))
    do(dve.tensor_tensor(m.weighted1[:], m.chosen1[:], over_experts(m.weight1), ALU.mult))
    do(dve.tensor_tensor(m.candidate[:], m.chosen2[:], over_experts(m.weight2), ALU.mult))
    do(dve.tensor_tensor(m.gate_of[:, :, 0:E], m.weighted1[:], m.candidate[:], ALU.add))
    do(dve.memset(m.gate_of[:, :, TURNS - 1:], 0.0))
    do(dve.memset(m.slot_of[:, :, TURNS - 1:], -1.0))
    dve.wait_ge(m.rank_mm, 1)
    rank = m.bank[3][:, 0:B * E].rearrange("p (b e) -> p b e", b=B)
    do(dve.scalar_tensor_tensor(m.position[:], rank, 1.0, m.routed[:], ALU.add, ALU.mult))
    do(dve.tensor_scalar(m.slot_of[:, :, 0:E], m.position[:], -1.0, None, ALU.add))

    def build(e):
        for b in range(B):
            dve.tensor_scalar(m.pick[:, b, :], m.iota[:], m.slot_of[:, b, bass.ds(e, 1)], None, ALU.is_equal)
        for b in range(B):
            last = dve.tensor_scalar(m.pick_gate[:, b, :], m.iota[:], m.slot_of[:, b, bass.ds(e, 1)],
                                     m.gate_of[:, b, bass.ds(e, 1)], ALU.is_equal, ALU.mult)
        last.then_inc(m.pick_done, 1)

    def gathered(e):
        dve.wait_ge(m.gather_mm, e * 2 + 2)
        dve.tensor_copy(m.xg_lo[:], by_block(m.bank[XG_BANKS[1]])).then_inc(m.xg_lo_done, 1)

    build(0)
    do(dve.tensor_scalar(m.crowded[:, 0, :], m.bank[3][:, B * E:B * E + E], float(P), None, ALU.is_gt))
    do(dve.tensor_reduce(m.n_crowded[:], m.crowded[:, 0, :], X_AXIS, ALU.add))
    dve.tensor_scalar(m.n_turns[:], m.n_crowded[:], float(E), None, ALU.add).then_inc(m.n_ready, 1)
    gathered(0)
    do(dve.memset(m.expert_f[:, TURNS - 1:], 0.0))
    do(dve.tensor_copy(m.expert_f[:, 0:E], m.iota[:, 0:E]))
    for r in range(EXTRA):
        do(dve.scalar_tensor_tensor(m.order[:], m.crowded[:, r, :], -float(E), m.iota[:, 0:E], ALU.mult, ALU.add))
        do(dve.tensor_reduce(m.first_one[:], m.order[:], X_AXIS, ALU.min))
        do(dve.scalar_tensor_tensor(m.extra[:, r, :], m.order[:], m.first_one[:], m.crowded[:, r, :], ALU.is_equal, ALU.mult))
        do(dve.tensor_tensor(m.crowded[:, r + 1, :], m.crowded[:, r, :], m.extra[:, r, :], ALU.subtract))
    extra_turns = slice(E, E + EXTRA)
    extra = m.extra[:].unsqueeze(1).to_broadcast([P, B, EXTRA, E])
    step.done(dve.tensor_tensor(m.extra_index[:], m.extra[:], m.iota[:, 0:E].unsqueeze(1).to_broadcast([P, EXTRA, E]),
                                ALU.mult))
    step.done(dve.tensor_tensor(m.extra_gate[:], m.gate_of[:, :, 0:E].unsqueeze(2).to_broadcast([P, B, EXTRA, E]), extra,
                                ALU.mult))
    do(dve.tensor_tensor(m.extra_position[:], m.position[:].unsqueeze(2).to_broadcast([P, B, EXTRA, E]), extra, ALU.mult))
    step.done(dve.tensor_reduce(m.expert_f[:, extra_turns], m.extra_index[:], X_AXIS, ALU.add))
    step.done(dve.tensor_reduce(m.gate_of[:, :, extra_turns], m.extra_gate[:], X_AXIS, ALU.add))
    do(dve.tensor_reduce(m.extra_slot[:], m.extra_position[:], X_AXIS, ALU.add))
    do(dve.tensor_scalar(m.slot_of[:, :, extra_turns], m.extra_slot[:], -1.0 - P, None, ALU.add))
    dve.tensor_copy(m.expert_of[:], m.expert_f[:]).then_inc(m.table_ready, 1)
    with dve.Fori(0, turns(dve, m)) as i:
        def unit(k):
            e_split_lo(dve, m, k, i)

        def hidden(j):
            bank = UP_BANKS[j % 2]
            dve.wait_ge(m.silu_done, i * QUARTERS + j + 1)
            dve.wait_ge(m.up_mm, i * len(UP_UNITS) + 2 * j + 2)
            dve.tensor_tensor(m.hidden[:, j % 2, :], m.bank[bank + 1][:], m.silu[:, j % 2, :], ALU.mult).then_inc(
                m.hidden_done, 1)

        def hidden_lo(j):
            dve.wait_ge(m.hidden_hi_done, i * QUARTERS + j + 1)
            dve.tensor_tensor(m.hidden_lo[:, j % 2, :], m.bank[HIDDEN_BANK][:], m.hidden_hi[:, j % 2, :].bitcast(F32),
                              ALU.subtract).then_inc(m.hidden_lo_done, 1)

        hidden(0)
        unit(7)
        unit(8)
        hidden(1)
        hidden_lo(0)
        build(i + 1)
        unit(10)
        unit(11)
        hidden(2)
        hidden_lo(1)
        unit(13)
        unit(14)
        hidden(3)
        hidden_lo(2)
        gathered(i + 1)
        hidden_lo(3)
        unit(16)
        for b in range(B):
            dve.wait_ge(m.scatter_mm, i * B + b + 1)
            dve.tensor_tensor(m.x_res[:, b, :], m.bank[XG_BANKS[b]][:], m.x_res[:, b, :], ALU.add).then_inc(m.acc_done, 1)
        unit(17)


def pe_moe(pe, m):
    for b in range(B):
        pe.wait_ge(m.xn2_ready, b + 1)
        pe_transpose4(pe, m, m.bank[b], [m.xn_tok[:, b, k * P:(k + 1) * P] for k in range(KT)], m.ident[:]).then_inc(
            m.xn2_mm, 1)
    pe.wait_ge(m.gate_in, 16)
    pe.wait_ge(m.xn2_T, B)
    for b in range(B):
        for k in range(KT):
            last = pe.matmul(m.bank[2][:, b * E:(b + 1) * E], m.xn_T[:, k, b * P:(b + 1) * P], m.gate_sb[:, k, :],
                             start=k == 0, stop=k == KT - 1)
    last.then_inc(m.logit_mm, 1)
    pe.wait_ge(m.consts_in, 48)
    pe.wait_ge(m.routed_done, 1)
    pe.matmul(m.bank[3][:, 0:E], m.earlier[:], m.routed[:, 0, :], start=True, stop=True)
    pe.matmul(m.bank[3][:, E:2 * E], m.earlier[:], m.routed[:, 1, :], start=True, stop=False)
    pe.matmul(m.bank[3][:, E:2 * E], m.ones[:], m.routed[:, 0, :], start=False, stop=True)
    for b in range(B):
        last = pe.matmul(m.bank[3][:, 2 * E:3 * E], m.ones[:], m.routed[:, b, :], start=b == 0, stop=b == B - 1)
    last.then_inc(m.rank_mm, 1)

    def gather(e):
        pe.wait_ge(m.pick_done, e + 1)
        for part, bank in ((m.xn_hi, m.bank[XG_BANKS[0]]), (m.xn_lo, m.bank[XG_BANKS[1]])):
            for k in range(KT):
                for b in range(B):
                    last = pe.matmul(bank[:, k * P:(k + 1) * P], part[:, b, k * P:(k + 1) * P], m.pick[:, b, :],
                                     start=b == 0, stop=b == B - 1)
            last.then_inc(m.gather_mm, 1)

    pe.wait_ge(m.xn2_lo, B)
    gather(0)
    with pe.Fori(0, turns(pe, m)) as i:

        def unit(k):
            e_wait(pe, m.e_lo_done, k, i)
            return m.e_hi[e_slot(k)], m.e_lo[e_slot(k)]

        def up(j):
            if j == 0:
                pe.wait_ge(m.xg_hi_done, i + 1)
                pe.wait_ge(m.xg_lo_done, i + 1)
            for q in range(2):
                w_hi, w_lo = unit(UP_UNITS[2 * j + q])
                if q == 0 and j >= 2:
                    pe.wait_ge(m.hidden_done, i * QUARTERS + j - 1)
                for k in range(KT):
                    last = three_passes(pe, m.bank[UP_BANKS[j % 2] + q][:], m.xg_hi[:, k, :], m.xg_lo[:, k, :],
                                        w_hi[:, k, :], w_lo[:, k, :], k == 0, k == KT - 1)
                last.then_inc(m.up_mm, 1)

        def hidden(j):
            pe.wait_ge(m.hidden_done, i * QUARTERS + j + 1)
            if j:
                pe.wait_ge(m.hidden_lo_done, i * QUARTERS + j)
            else:
                pe.wait_ge(m.gateT_done, i + 1)
            pe_transpose4(pe, m, m.bank[HIDDEN_BANK], [m.hidden[:, j % 2, t * P:(t + 1) * P] for t in range(KT)],
                          m.ident[:]).then_inc(m.hiddenT_mm, 1)

        def down(j):
            w_hi, w_lo = unit(DOWN_UNITS[j])
            pe.wait_ge(m.hidden_lo_done, i * QUARTERS + j + 1)
            for k in range(KT):
                cols = slice(k * P, (k + 1) * P)
                last = three_passes(pe, m.bank[Y_BANK][:], m.hidden_hi[:, j % 2, cols], m.hidden_lo[:, j % 2, cols],
                                    w_hi[:, k, :], w_lo[:, k, :], j == 0 and k == 0, j == QUARTERS - 1 and k == KT - 1)
            last.then_inc(m.down_mm, 1)

        up(0)
        for b in range(B):
            last = pe.transpose(m.bank[HIDDEN_BANK][:, b * P:(b + 1) * P], m.pick_gate[:, b, :], m.ident[:])
        last.then_inc(m.gateT_mm, 1)
        up(1)
        hidden(0)
        up(2)
        down(0)
        hidden(1)
        up(3)
        down(1)
        hidden(2)
        gather(i + 1)
        hidden(3)
        down(2)
        down(3)
        pe.wait_ge(m.xg_hi_done, i + 2)
        pe.wait_ge(m.xg_lo_done, i + 2)
        pe.wait_ge(m.y_done, i + 1)
        for b in range(B):
            pe.matmul(m.bank[XG_BANKS[b]][:], m.pick_gate_T[:, b, :], m.y[:], start=True, stop=True).then_inc(
                m.scatter_mm, 1)


def _blocks(w, rows):
    return w.reshape(rows // P, P, -1).transpose(1, 0, 2)


def _positions():
    pos = np.arange(P - 1, -1, -1, dtype=np.float32)
    freq = (np.float32(1.0) / np.float32(10000.0) ** (np.arange(0, D, 2, dtype=np.float32) / np.float32(D))).astype(
        np.float32)
    ang = pos[:, None] * freq[None, :]
    return np.concatenate([np.sin(ang), np.cos(ang)], axis=-1).astype(np.float32)


def kernel(**inputs):
    from concourse import bacc
    from concourse.bass_utils import run_bass_kernel_spmd

    a = {k: np.asarray(v) for k, v in inputs.items()}
    c = np.ascontiguousarray
    unit = (P, KT * CHUNK)
    w_cross = c(np.stack([_blocks(a[f"L0_xattn_{n}"].T, D).reshape(unit) for n in ("Wq", "Wk", "Wv", "Wo")]))
    ctx_t = c(a["ctx_1024"].reshape(B, NCH, CHUNK, KT, P).transpose(0, 1, 4, 3, 2).reshape(B * NCH, *unit))

    def units(w, rows):
        r, n = w.shape
        return [_blocks(w[i:i + D, j:j + CHUNK], D).reshape(unit) for i in range(0, r, D) for j in range(0, n, CHUNK)]

    stream = []
    for i in range(L):
        qkv = a["L0_attn_W_qkv"][i]
        hd = H * DH
        for w in (a["L0_attn_W_r"][i], qkv[:, :hd], qkv[:, hd:2 * hd], qkv[:, 2 * hd:], a["L0_attn_W_o"][i],
                  a["L0_attn_W_ff1"][i], a["L0_attn_W_ff2"][i]):
            stream += units(w, D)
    for e in range(E):
        quarters = {n: units(a[f"L0_ffn_{n}"][e], D) for n in ("w0", "w1", "wo")}
        stream += [quarters[n][q] for n, q in E_ORDER]
    w_stream = c(np.stack(stream))
    arrays = {
        "x": c(a["x"]),
        "ctx_t": ctx_t,
        "mask": c(a["mask_1x1xSxS2_ik0"].reshape(P, SK)),
        "w_cross": w_cross,
        "w_stream": w_stream,
        "cross_vecs": c(np.stack([a[f"L0_xattn_{n}"].reshape(KT, P).T for n in ("bq", "bk", "bv")], axis=1)),
        "bo_row": c(a["L0_xattn_bo"]),
        "consts": np.stack([np.eye(P), np.triu(np.ones((P, P)), 1), np.tile(np.arange(P), (P, 1)),
                            np.ones((P, P))]).astype(np.float32),
        "r_t": c(_blocks(_positions().T, D).reshape(unit[0], KT * P)),
        "uv": c(np.stack([np.tile(a[f"L0_attn_{n}"].T, (2, 1)) for n in "uv"], axis=1)),
        "ff1_bias": c(a["L0_attn_b_ff1"].reshape(L, DF // P, P).transpose(2, 0, 1)),
        "layer_rows": c(np.stack([a[f"L0_attn_{n}"] for n in ("ln1_g", "ln1_b", "b_ff2", "ln2_g", "ln2_b")], axis=1)),
        "gate": c(_blocks(a["L0_ffn_gate_kernel"], D)),
    }
    nc = bacc.Bacc("TRN2", target_bir_lowering=False, num_devices=1)
    aps = {n: nc.dram_tensor(n, v.shape, mybir.dt.from_np(v.dtype), kind="ExternalInput").ap() for n, v in arrays.items()}
    out = nc.dram_tensor("out", (B, P, D), F32, kind="ExternalOutput").ap()
    build_program(nc, **aps, out=out)
    r = run_bass_kernel_spmd(nc, [arrays], core_ids=[0])
    return r.results[0]["out"]
```

```python
from contextlib import ExitStack

import concourse.bass as bass
import concourse.mybir as mybir
import numpy as np

F32 = mybir.dt.float32
F32R = mybir.dt.float32r
I32 = mybir.dt.int32
U32 = mybir.dt.uint32
ALU = mybir.AluOpType
ACT = mybir.ActivationFunctionType
X_AXIS = mybir.AxisListType.X

P = 128
B = 2
D = 512
KT = D // P
SK = 2048
CHUNK = 512
NCH = SK // CHUNK
XH, XDH = 16, 32
GROUPS = XH * XDH // P
HPG = P // XDH
L, H, DH, DF = 4, 16, 64, 2048
E, F = 8, 2048
EPS = 1e-5
MASKED = -float(2 ** 30)
X_SCALE = float(1.0 / np.float32(np.sqrt(XDH)))
L_SCALE = 1.0 / 8.0

RING = 3
S_WQ, S_WK, S_WV, S_CTX = 0, 1, 2, 3
S_WO = S_CTX + B * NCH
S_LAYER = S_WO + 1
LU = 18
U_WR, U_WQ, U_WK, U_WV, U_WO, U_FF1, U_FF2 = 0, 2, 4, 6, 8, 10, 14
S_MOE = S_LAYER + L * LU
EU = 12
E_ORDER = [("w0", 0), ("w1", 0), ("w0", 1), ("w1", 1), ("w0", 2), ("w1", 2), ("wo", 0), ("w0", 3),
           ("w1", 3), ("wo", 1), ("wo", 2), ("wo", 3)]
assert LU % RING == 0 and EU % RING == 0 and S_LAYER % RING == 0 and S_MOE % RING == 0


def nth(s):
    return s // RING + 1


def wait_unit(eng, sem, s, iteration=0, per=0, each=1):
    eng.wait_ge(sem[s % RING], (iteration * (per // RING) + nth(s)) * each)


class Memory:

    def __init__(self, nc, ctx, dram):
        self.nc, self.ctx, self.dram = nc, ctx, dram

    def sb(self, name, shape, dt=F32):
        return self.ctx.enter_context(self.nc.sbuf_tensor(name, shape, dt))

    def sems(self, names):
        return [self.ctx.enter_context(self.nc.semaphore(name)) for name in names.split()]

    def slot_sems(self, name):
        return [self.ctx.enter_context(self.nc.semaphore(f"{name}{i}")) for i in range(RING)]


def three_passes(pe, out, w_hi, w_lo, m_hi, m_lo, first, last):
    pe.matmul(out, w_hi, m_hi, start=first, stop=False)
    pe.matmul(out, w_hi, m_lo, start=False, stop=False)
    return pe.matmul(out, w_lo, m_hi, start=False, stop=last)


def split_hi(act, m, s, iteration=0, per=0, hi=None):
    wait_unit(act, m.loaded, s, iteration, per, 16)
    dst = m.w_hi[s % RING] if hi is None else hi
    act.activation(dst[:].rearrange("p k n -> p (k n)"), m.raw[:, s % RING, :], ACT.Copy).then_inc(
        m.hi_done[s % RING], 1)


def split_lo(eng, m, s, iteration=0, per=0, hi=None, lo=None):
    wait_unit(eng, m.hi_done, s, iteration, per)
    h = m.w_hi[s % RING] if hi is None else hi
    l_ = m.w_lo[s % RING] if lo is None else lo
    eng.tensor_tensor(l_[:].rearrange("p k n -> p (k n)"), m.raw[:, s % RING, :],
                      h[:].rearrange("p k n -> p (k n)").bitcast(F32), ALU.subtract).then_inc(
        m.lo_done[s % RING], 1)


class Step:

    def __init__(self, eng, sem, base=0, iteration=0, per=0):
        self.eng, self.sem, self.base, self.iteration, self.per, self.n = eng, sem, base, iteration, per, 0

    def done(self, ins):
        ins.then_inc(self.sem, 1)
        self.n += 1

    def wait(self):
        self.eng.wait_ge(self.sem, self.iteration * self.per + self.base + self.n)


def ln_scale(dve, m, step, src, t, n):
    step.done(dve.bn_stats(m.bn6[:, t, :], src))
    step.wait()
    dve.memset(m.newton[:, t:t + 1], 0.0)
    step.done(dve.bn_aggr(m.mean_var[:, t, :], m.bn6[:, t, :]))
    step.wait()
    var_eps, root0 = m.var_eps[:, t:t + 1], m.root0[:, t:t + 1]
    dve.tensor_scalar(var_eps, m.mean_var[:, t, 1:2], EPS, None, ALU.add).then_inc(m.ln_var, 1)
    dve.wait_ge(m.ln_rooted, (n - 1) * B + t + 1)
    step.done(dve.reciprocal(root0, m.ln_sqrt[:, t:t + 1]))
    step.wait()
    step.done(dve.scalar_tensor_tensor(m.newton[:, t:t + 1], root0, -0.5, root0, ALU.mult, ALU.mult))
    step.wait()
    step.done(dve.tensor_tensor(m.newton2[:, t:t + 1], m.newton[:, t:t + 1], var_eps, ALU.mult))
    step.wait()
    step.done(dve.scalar_tensor_tensor(m.rstd[:, t:t + 1], m.newton2[:, t:t + 1], 1.5, root0, ALU.add, ALU.mult))


def ln_root(act, m, n, t):
    act.wait_ge(m.ln_var, (n - 1) * B + t + 1)
    act.activation(m.ln_sqrt[:, t:t + 1], m.var_eps[:, t:t + 1], ACT.Sqrt).then_inc(m.ln_rooted, 1)


def ln_apply(dve, m, out, src, t):
    return dve.tensor_scalar(out, src, m.mean_var[:, t, 0:1], m.rstd[:, t:t + 1], ALU.subtract, ALU.mult)


def build_program(nc, x, ctx_t, mask, w_cross, w_stream, cross_vecs, bo_row, consts, r_t, uv, ff1_bias,
                  layer_rows, gate, out):
    with ExitStack() as ctx:
        m = Memory(nc, ctx, dict(x=x, ctx_t=ctx_t, mask=mask, w_cross=w_cross, w_stream=w_stream,
                                 cross_vecs=cross_vecs, bo_row=bo_row, consts=consts, r_t=r_t, uv=uv,
                                 ff1_bias=ff1_bias, layer_rows=layer_rows, gate=gate, out=out))
        common_memory(m)
        for phase_memory in (cross_memory, layer_memory, moe_memory):
            with ExitStack() as m.ctx:
                phase_memory(m)
        block = ctx.enter_context(nc.Block())

        @block.sync
        def _(sp):
            sp_program(sp, m)

        @block.gpsimd
        def _(pool):
            pool_cross(pool, m)
            pool_layers(pool, m)
            pool_moe(pool, m)

        @block.scalar
        def _(act):
            act_cross(act, m)
            act_layers(act, m)
            act_moe(act, m)

        @block.vector
        def _(dve):
            step = Step(dve, m.dve_step)
            dve_cross(dve, m, step)
            dve_layers(dve, m, step)
            dve_moe(dve, m, step)

        @block.tensor
        def _(pe):
            pe_cross(pe, m)
            pe_layers(pe, m)
            pe_moe(pe, m)


def common_memory(m):
    m.raw = m.sb("raw", [P, RING, KT * CHUNK])
    m.w_hi = [m.sb(f"w_hi{i}", [P, KT, CHUNK], F32R) for i in range(RING)]
    m.w_lo = [m.sb(f"w_lo{i}", [P, KT, CHUNK], F32R) for i in range(RING)]
    m.loaded = m.slot_sems("loaded")
    m.hi_done = m.slot_sems("hi_done")
    m.lo_done = m.slot_sems("lo_done")
    m.ident = m.sb("ident", [P, P])
    m.earlier = m.sb("earlier", [P, P])
    m.iota = m.sb("iota", [P, P])
    m.ones = m.sb("ones", [P, P])
    m.gate_sb = m.sb("gate_sb", [P, KT, E])
    m.x_res = m.sb("x_res", [P, B, D])
    m.r_hi = m.sb("r_hi", [P, KT, P], F32R)
    m.r_lo = m.sb("r_lo", [P, KT, P], F32R)
    m.uv_sb = m.sb("uv_sb", [P, 2, H])
    m.ff1_bias_sb = m.sb("ff1_bias_sb", [P, L, DF // P])
    m.bn6 = m.sb("bn6", [P, B, 6])
    m.mean_var = m.sb("mean_var", [P, B, 2])
    m.var_eps = m.sb("var_eps", [P, B])
    m.ln_sqrt = m.sb("ln_sqrt", [P, B])
    m.root0 = m.sb("root0", [P, B])
    m.newton = m.sb("newton", [P, B])
    m.newton2 = m.sb("newton2", [P, B])
    m.rstd = m.sb("rstd", [P, B])
    (m.ident_in, m.x_in, m.vecs_in, m.vecs_in2, m.mask_in, m.r_in, m.uv_in, m.bias_in, m.gate_in, m.consts_in,
     m.ln_var, m.ln_rooted, m.dve_step, m.out_done) = m.sems(
        "ident_in x_in vecs_in vecs_in2 mask_in r_in uv_in bias_in gate_in consts_in ln_var ln_rooted "
        "dve_step out_done")
    m.bank = [m.ctx.enter_context(m.nc.psum_tensor(f"bank{i}", [P, CHUNK], F32)) for i in range(8)]


S_BANKS, T_BANKS, O_BANK = (0, 1, 2, 3), (4, 5, 7), 6
T_SLOT = (0, 1, 2, 1)
NG = B * GROUPS


def cross_memory(m):
    m.ident_r = m.sb("ident_r", [P, P], F32R)
    m.cross_vec = m.sb("cross_vec", [P, 3, KT])
    m.bo_bc = m.sb("bo_bc", [P, D])
    m.q_scale = m.sb("q_scale", [P, 1])
    m.mask_max = m.sb("mask_max", [P, 1])
    m.mask_add = m.sb("mask_add", [P, SK], F32R)
    m.q_feat = m.sb("q_feat", [P, KT, B * P])
    m.q_quad = m.sb("q_quad", [P, HPG, P], F32R)
    m.k_quad = [m.sb(f"k_quad{i}", [P, KT, CHUNK], F32R) for i in range(2)]
    m.probs = m.sb("probs", [P, NCH, CHUNK])
    m.probs_T = m.sb("probs_T", [P, len(T_BANKS), CHUNK])
    m.part_max = m.sb("part_max", [P, NCH])
    m.first_max = m.sb("first_max", [P, 1])
    m.q_scale_neg = m.sb("q_scale_neg", [P, 1])
    m.shift = m.sb("shift", [P, HPG])
    m.part_sum = m.sb("part_sum", [P, HPG, NCH])
    m.row_sum = m.sb("row_sum", [P, HPG])
    m.row_inv = m.sb("row_inv", [P, NG, HPG])
    m.o_feat = m.sb("o_feat", [P, NG, P])
    m.v_grp = m.sb("v_grp", [P, SK // P, P])
    outer = m.ctx
    with ExitStack() as m.ctx:
        m.k_all = m.sb("k_all", [P, KT, SK])
        m.v_all = m.sb("v_all", [P, SK // P, D])
    with ExitStack() as m.ctx:
        m.xn = m.sb("xn", [P, B, D])
        m.xT_hi = m.sb("xT_hi", [P, KT, B * P], F32R)
        m.xT_lo = m.sb("xT_lo", [P, KT, B * P], F32R)
    with ExitStack() as m.ctx:
        m.vecT_hi = m.sb("vecT_hi", [P, KT, B * P], F32R)
        m.vecT_lo = m.sb("vecT_lo", [P, KT, B * P], F32R)
        m.o_tok = m.sb("o_tok", [P, B, D])
    m.ctx = outer
    (m.ident_ready, m.xn_ready, m.xnT_mm, m.xT_hi_done, m.xT_lo_done, m.q_mm, m.q_done, m.mask_ready,
     m.r_hi_done, m.r_ready, m.qz_zeroed, m.bo_added, m.q_scale_done, m.k_mm, m.k_done, m.v_mm, m.v_done,
     m.k_hi_done, m.k_lo_done, m.k_hi2_even, m.k_hi2_odd, m.qz_hi_done, m.qz_done, m.s_mm, m.max_done,
     m.first_max_done, m.shift_done, m.exp_done, m.pT_mm, m.pT_dve, m.pT_act, m.pv_mm, m.sum_done, m.inv_done,
     m.o_copied, m.v_part_done, m.oT_mm, m.oT_done, m.vec_mm, m.vec_hi, m.vec_lo, m.o_mm, m.x1_done) = m.sems(
        "ident_ready xn_ready xnT_mm xT_hi_done xT_lo_done q_mm q_done mask_ready r_hi_done r_ready qz_zeroed "
        "bo_added q_scale_done k_mm k_done v_mm v_done k_hi_done k_lo_done k_hi2_even k_hi2_odd qz_hi_done "
        "qz_done s_mm max_done first_max_done shift_done exp_done pT_mm pT_dve pT_act pv_mm sum_done inv_done "
        "o_copied v_part_done oT_mm oT_done vec_mm vec_hi vec_lo o_mm x1_done")


def quadrant(j):
    return slice(j % HPG * XDH, (j % HPG + 1) * XDH)


MASK_ROWS = SK // D


def ctx_slot(m, n):
    return (m.w_hi[0], m.w_lo[0]) if n % 2 == 0 else (m.k_quad[0], m.k_quad[1])


def sp_program(sp, m):
    d = m.dram

    def load(s, src):
        if s >= RING:
            wait_unit(sp, m.lo_done, s - RING)
        sp.dma_start(m.raw[:, s % RING, :], src).then_inc(m.loaded[s % RING], 16)

    sp.dma_start(m.x_res[:], d["x"].rearrange("b p d -> p b d")).then_inc(m.x_in, 16)
    load(S_WQ, d["w_cross"][0])
    sp.dma_start(m.ident[:], d["consts"][0]).then_inc(m.ident_in, 16)
    sp.dma_start(m.cross_vec[:], d["cross_vecs"]).then_inc(m.vecs_in, 16)
    load(S_WK, d["w_cross"][1])
    load(S_WV, d["w_cross"][2])
    load(S_CTX, d["ctx_t"][0])
    sp.dma_start(m.v_all[:, SK // P - MASK_ROWS:, :].rearrange("p t d -> p (t d)").bitcast(I32), d["mask"]).then_inc(
        m.mask_in, 16)
    load(S_CTX + 1, d["ctx_t"][1])
    sp.dma_start(m.v_all[:, SK // P - MASK_ROWS - 1, :], d["r_t"]).then_inc(m.r_in, 16)
    sp.dma_start(m.bo_bc[:], d["bo_row"].partition_broadcast(P)).then_inc(m.vecs_in2, 16)
    sp.dma_start(m.uv_sb[:], d["uv"]).then_inc(m.uv_in, 16)
    sp.dma_start(m.ff1_bias_sb[:], d["ff1_bias"]).then_inc(m.bias_in, 16)
    sp.dma_start(m.gate_sb[:], d["gate"]).then_inc(m.gate_in, 16)
    for n in range(2, NCH + RING):
        load(S_CTX + n, d["ctx_t"][n])
        if n < 5:
            if n > 2:
                sp.wait_ge(m.consts_in, (n - 2) * 16)
            sp.dma_start((m.earlier, m.iota, m.ones)[n - 2][:], d["consts"][n - 1]).then_inc(m.consts_in, 16)

    def keys(g):
        for j in range(HPG):
            sp.wait_ge(m.k_hi_done, (g * HPG + j + 1) * NCH)
            sp.dma_start(m.k_quad[j % 2][quadrant(j + 2), :, :].bitcast(F32),
                         m.k_quad[j % 2][quadrant(j), :, :].bitcast(F32)).then_inc(
                (m.k_hi2_even, m.k_hi2_odd)[j % 2], 16)

    for b in range(B):
        keys(b * GROUPS)
        if b == 0:
            load(S_CTX + NCH + RING, d["ctx_t"][NCH + RING])
        else:
            load(S_LAYER + 2, d["w_stream"][2])
        with sp.Fori(0, GROUPS - 1) as fb:
            keys(fb + b * GROUPS + 1)
        if b == 0:
            load(S_WO, d["w_cross"][3])
            load(S_LAYER, d["w_stream"][0])
            load(S_LAYER + 1, d["w_stream"][1])
    sp_layers(sp, m)
    sp_moe(sp, m)


def pool_cross(pool, m):
    split_lo(pool, m, S_WK)

    def context(n):
        split_lo(pool, m, S_CTX + n, hi=ctx_slot(m, n)[0], lo=ctx_slot(m, n)[1])

    def heads_done(n):
        pool.wait_ge(m.k_lo_done, n * NCH)

    def keys(g, first=False):
        for j in range(HPG):
            if not (first and j == 0):
                heads_done(g * HPG + j)
            for c in range(NCH):
                pool.wait_ge(m.k_hi_done, (g * HPG + j) * NCH + c + 1)
                pool.tensor_tensor(m.k_quad[j % 2][quadrant(j + 1), c, :],
                                   m.k_all[quadrant(j), g - b * GROUPS, c * CHUNK:(c + 1) * CHUNK],
                                   m.k_quad[j % 2][quadrant(j), c, :].bitcast(F32), ALU.subtract).then_inc(
                    m.k_lo_done, 1)

    for b in range(B):
        for n in range(b * NCH + 1, (b + 1) * NCH):
            context(n)
        if b == 0:
            wait_unit(pool, m.lo_done, S_CTX + NCH - 1)
            keys(0, first=True)
            heads_done(HPG)
            context(NCH)
            wait_unit(pool, m.lo_done, S_CTX + NCH)
        else:
            split_lo(pool, m, S_LAYER)
            split_lo(pool, m, S_LAYER + 1)
            wait_unit(pool, m.lo_done, S_LAYER + 1)
            keys(GROUPS)
            heads_done((GROUPS + 1) * HPG)
            split_lo(pool, m, S_WO)
            wait_unit(pool, m.lo_done, S_WO)
        with pool.Fori(0, GROUPS - 1) as fb:
            keys(fb + b * GROUPS + 1)
        heads_done((b + 1) * GROUPS * HPG)


def act_cross(act, m):
    act.wait_ge(m.x_in, 16)
    for t in range(B):
        ln_root(act, m, 1, t)
    split_hi(act, m, S_WQ, hi=m.k_quad[0])
    split_hi(act, m, S_WK)
    split_hi(act, m, S_WV)
    for b in range(B):
        act.wait_ge(m.xnT_mm, b + 1)
        act.activation(m.xT_hi[:, :, b * P:(b + 1) * P], m.bank[b][:].rearrange("p (k t) -> p k t", k=KT),
                       ACT.Copy).then_inc(m.xT_hi_done, 1)

    def context(n):
        if n >= 2:
            act.wait_ge(m.v_mm, (n - 1) * KT)
        if n == NCH + 1:
            act.wait_ge(m.s_mm, GROUPS * HPG * NCH)
        split_hi(act, m, S_CTX + n, hi=ctx_slot(m, n)[0])

    context(0)
    act.wait_ge(m.vecs_in, 16)
    for f in range(KT):
        act.wait_ge(m.q_mm, f // 2 + 1)
        act.activation(m.q_feat[:, f, :], m.bank[2 + f // 2][:, (f % 2) * B * P:(f % 2 + 1) * B * P], ACT.Identity,
                       bias=m.cross_vec[:, 0, f:f + 1]).then_inc(m.q_done, 1)
    context(1)
    for b in range(B):
        if b == 1:
            context(NCH + 1)
        for n in range(b * NCH, (b + 1) * NCH):
            c = n % NCH
            for f in range(KT):
                act.wait_ge(m.k_mm, n * KT + f + 1)
                act.activation(m.k_all[:, f, c * CHUNK:(c + 1) * CHUNK], m.bank[f][:], ACT.Identity,
                               bias=m.cross_vec[:, 1, f:f + 1]).then_inc(m.k_done, 1)
            if c + 2 < NCH or n + 2 == NCH:
                context(n + 2)
        if b == 1:
            act.wait_ge(m.v_mm, (B * NCH - 1) * KT)
            split_hi(act, m, S_LAYER)
            split_hi(act, m, S_LAYER + 1)

        def transposed(g, j, c):
            act.wait_ge(m.pT_mm, (g * HPG + j) * NCH + c + 1)
            act.activation(m.probs_T[:, T_SLOT[c], :], m.bank[T_BANKS[T_SLOT[c]]][:], ACT.Copy).then_inc(m.pT_act, 1)

        def exps(g, j, first=False):
            act.wait_ge(m.shift_done, g * HPG + j + 1)
            for c in range(NCH):
                if not first:
                    act.wait_ge(m.pT_mm, (g * HPG + j - 1) * NCH + c + 1)
                act.activation(m.probs[:, c, :], m.bank[S_BANKS[c]][:], ACT.Exp, bias=m.shift[:, j:j + 1],
                               scale=m.q_scale[:, 0:1], accum_out=m.part_sum[:, j, c:c + 1]).then_inc(m.exp_done, 1)

        def group(g, more):
            for j in range(1, HPG):
                transposed(g, j - 1, 0)
                transposed(g, j - 1, 1)
                transposed(g, j - 1, 2)
                exps(g, j)
            transposed(g, HPG - 1, 0)
            transposed(g, HPG - 1, 1)
            transposed(g, HPG - 1, 2)
            if more:
                exps(g + 1, 0)

        exps(b * GROUPS, 0, first=True)
        if b == 1:
            act.wait_ge(m.v_mm, B * NCH * KT)
            split_hi(act, m, S_WO)
        with act.Fori(0, GROUPS - 1) as fb:
            group(fb + b * GROUPS, True)
        group((b + 1) * GROUPS - 1, False)
    for b in range(B):
        act.wait_ge(m.vec_mm, b + 1)
        for k in range(KT):
            act.activation(m.vecT_hi[:, k, b * P:(b + 1) * P], m.bank[4 + b][:, k * P:(k + 1) * P], ACT.Identity,
                           bias=m.cross_vec[:, 2, k:k + 1]).then_inc(m.vec_hi, 1)


def dve_cross(dve, m, step):
    dve.wait_ge(m.x_in, 16)
    for b in range(B):
        ln_scale(dve, m, step, m.x_res[:, b, :], b, 1)
        step.wait()
        ln_apply(dve, m, m.xn[:, b, :], m.x_res[:, b, :], b).then_inc(m.xn_ready, 1)
    dve.wait_ge(m.ident_in, 16)
    dve.tensor_copy(m.ident_r[:], m.ident[:]).then_inc(m.ident_ready, 1)
    split_lo(dve, m, S_WQ, hi=m.k_quad[0], lo=m.k_quad[1])
    for b in range(B):
        dve.wait_ge(m.xT_hi_done, b + 1)
        dve.tensor_tensor(m.xT_lo[:, :, b * P:(b + 1) * P], m.bank[b][:].rearrange("p (k t) -> p k t", k=KT),
                          m.xT_hi[:, :, b * P:(b + 1) * P].bitcast(F32), ALU.subtract).then_inc(m.xT_lo_done, 1)
    split_lo(dve, m, S_WV)
    split_lo(dve, m, S_CTX)

    def mask_and_positions():
        dve.wait_ge(m.mask_in, 16)
        dve.tensor_scalar(m.mask_add[:], m.v_all[:, SK // P - MASK_ROWS:, :].rearrange("p t d -> p (t d)").bitcast(I32),
                          0.0, MASKED, ALU.is_equal, ALU.mult).then_inc(m.mask_ready, 1)
        dve.wait_ge(m.mask_ready, 1)
        step.done(dve.tensor_reduce(m.mask_max[:], m.mask_add[:].bitcast(F32), X_AXIS, ALU.max))
        step.wait()
        dve.tensor_scalar(m.q_scale_neg[:], m.mask_max[:], 0.0, -X_SCALE, ALU.is_equal, ALU.mult)
        dve.tensor_scalar(m.q_scale[:], m.mask_max[:], 0.0, X_SCALE, ALU.is_equal, ALU.mult).then_inc(m.q_scale_done, 1)
        positions = m.v_all[:, SK // P - MASK_ROWS - 1, :]
        dve.wait_ge(m.r_in, 16)
        dve.tensor_copy(m.r_hi[:].rearrange("p k t -> p (k t)"), positions).then_inc(m.r_hi_done, 1)
        dve.wait_ge(m.r_hi_done, 1)
        dve.tensor_tensor(m.r_lo[:].rearrange("p k t -> p (k t)"), positions,
                          m.r_hi[:].rearrange("p k t -> p (k t)").bitcast(F32), ALU.subtract).then_inc(m.r_ready, 1)
        dve.memset(m.q_quad[:].bitcast(U32), 0).then_inc(m.qz_zeroed, 1)
        dve.wait_ge(m.vecs_in2, 16)
        for b in range(B):
            dve.tensor_tensor(m.x_res[:, b, :], m.x_res[:, b, :], m.bo_bc[:], ALU.add).then_inc(m.bo_added, 1)
        dve.wait_ge(m.qz_zeroed, 1)
        dve.wait_ge(m.q_done, KT)
        dve.wait_ge(m.q_scale_done, 1)
        dve.wait_ge(m.r_ready, 1)

    for b in range(B):

        def queries(g, j):
            q = m.q_feat[quadrant(j), g - b * GROUPS, b * P:(b + 1) * P]
            dve.tensor_copy(m.q_quad[quadrant(j), j, :], q).then_inc(m.qz_hi_done, 1)
            dve.tensor_copy(m.q_quad[quadrant(j + 1), j, :], q)
            dve.wait_ge(m.qz_hi_done, g * HPG + j + 1)
            dve.tensor_tensor(m.q_quad[quadrant(j + 2), j, :], q, m.q_quad[quadrant(j), j, :].bitcast(F32),
                              ALU.subtract).then_inc(m.qz_done, 1)

        def keys(g, j, c):
            dve.tensor_copy(m.k_quad[j % 2][quadrant(j), c, :],
                            m.k_all[quadrant(j), g - b * GROUPS, c * CHUNK:(c + 1) * CHUNK]).then_inc(m.k_hi_done, 1)

        def values(g, j):
            cols = bass.ds((g - b * GROUPS) * P + j * XDH, XDH)
            dve.tensor_copy(m.v_grp[:, :, j * XDH:(j + 1) * XDH], m.v_all[:, :, cols]).then_inc(m.v_part_done, 1)

        def maximum(g, j, c):
            dve.wait_ge(m.s_mm, (g * HPG + j) * NCH + c + 1)
            dve.tensor_reduce(m.part_max[:, c:c + 1], m.bank[S_BANKS[c]][:], X_AXIS, ALU.max).then_inc(m.max_done, 1)
            if c == NCH - 2:
                dve.wait_ge(m.max_done, (g * HPG + j) * NCH + c + 1)
                dve.tensor_reduce(m.first_max[:], m.part_max[:, 0:NCH - 1], X_AXIS, ALU.max).then_inc(
                    m.first_max_done, 1)

        def shift(g, j):
            dve.wait_ge(m.first_max_done, g * HPG + j + 1)
            dve.wait_ge(m.max_done, (g * HPG + j + 1) * NCH)
            dve.scalar_tensor_tensor(m.shift[:, j:j + 1], m.part_max[:, NCH - 1:NCH], m.first_max[:], m.q_scale_neg[:],
                                     ALU.max, ALU.mult).then_inc(m.shift_done, 1)

        def transposed(g, j, c):
            dve.wait_ge(m.pT_mm, (g * HPG + j) * NCH + c + 1)
            dve.tensor_copy(m.probs_T[:, T_SLOT[c], :], m.bank[T_BANKS[T_SLOT[c]]][:]).then_inc(m.pT_dve, 1)

        def total(g, j):
            dve.wait_ge(m.exp_done, (g * HPG + j + 1) * NCH)
            dve.tensor_reduce(m.row_sum[:, j:j + 1], m.part_sum[:, j, :], X_AXIS, ALU.add).then_inc(m.sum_done, 1)

        def group(g, more):
            for j in range(1, HPG + 1):
                ahead = (g, j) if j < HPG else (g + 1, 0) if more else None
                later = (g, j + 2) if j + 2 < HPG else (g + 1, j + 2 - HPG) if more else None
                if ahead:
                    for c in range(NCH):
                        maximum(*ahead, c)
                    shift(*ahead)
                for c in range(2 if later else 0):
                    keys(*later, c)
                transposed(g, j - 1, 3)
                for c in range(2, NCH if later else 0):
                    keys(*later, c)
                total(g, j - 1)
                if more:
                    queries(g + 1, j - 1)
                    if j > 1:
                        dve.wait_ge(m.pv_mm, (g * HPG + j - 1) * NCH)
                        values(g + 1, j - 2)
            dve.wait_ge(m.sum_done, (g + 1) * HPG)
            dve.reciprocal(m.row_inv[:, bass.ds(g, 1), :].rearrange("p g h -> p (g h)"), m.row_sum[:]).then_inc(
                m.inv_done, 1)
            dve.wait_ge(m.pv_mm, (g + 1) * HPG * NCH)
            dve.tensor_copy(m.o_feat[:, bass.ds(g, 1), :].rearrange("p g t -> p (g t)"),
                            m.bank[O_BANK][:, 0:P]).then_inc(m.o_copied, 1)
            if more:
                values(g + 1, HPG - 1)

        for n in range(b * NCH, (b + 1) * NCH):
            for t in range(KT):
                dve.wait_ge(m.v_mm, n * KT + t + 1)
                dve.tensor_copy(m.v_all[:, (n % NCH) * KT + t, :], m.bank[4 + t][:]).then_inc(m.v_done, 1)
            if n == 0:
                mask_and_positions()
            if n % NCH == NCH - 2:
                for j in range(HPG):
                    queries(b * GROUPS, j)
        dve.wait_ge(m.k_done, (b + 1) * NCH * KT)
        for j in range(2):
            for c in range(NCH):
                keys(b * GROUPS, j, c)
        dve.wait_ge(m.v_done, (b + 1) * NCH * KT)
        for c in range(NCH):
            maximum(b * GROUPS, 0, c)
        shift(b * GROUPS, 0)
        for c in range(NCH):
            keys(b * GROUPS, 2, c)
        for j in range(HPG):
            values(b * GROUPS, j)
        with dve.Fori(0, GROUPS - 1) as fb:
            group(fb + b * GROUPS, True)
        group((b + 1) * GROUPS - 1, False)
    dve.wait_ge(m.inv_done, NG)
    for b in range(B):
        dve.wait_ge(m.oT_mm, b + 1)
        dve.tensor_tensor(m.o_tok[:, b, :].rearrange("p (h d) -> p h d", h=XH),
                          m.bank[b][:].rearrange("p (h d) -> p h d", h=XH),
                          m.row_inv[:, b * GROUPS:(b + 1) * GROUPS, :].rearrange("p g h -> p (g h)").unsqueeze(
                              2).to_broadcast([P, XH, XDH]), ALU.mult).then_inc(m.oT_done, 1)
    for b in range(B):
        for k in range(KT):
            dve.wait_ge(m.vec_hi, (b + 1) * KT)
            dve.scalar_tensor_tensor(m.vecT_lo[:, k, b * P:(b + 1) * P], m.bank[4 + b][:, k * P:(k + 1) * P],
                                     m.cross_vec[:, 2, k:k + 1], m.vecT_hi[:, k, b * P:(b + 1) * P].bitcast(F32),
                                     ALU.add, ALU.subtract).then_inc(m.vec_lo, 1)
    dve.wait_ge(m.bo_added, B)
    for b in range(B):
        dve.wait_ge(m.o_mm, b + 1)
        dve.tensor_tensor(m.x_res[:, b, :], m.bank[2 + b][:], m.x_res[:, b, :], ALU.add).then_inc(m.x1_done, 1)


def pe_transpose4(pe, m, bank, blocks, identity):
    for t, src in enumerate(blocks):
        last = pe.transpose(bank[:, t * P:(t + 1) * P], src, identity)
    return last


def pe_cross(pe, m):
    pe.wait_ge(m.ident_in, 16)
    for b in range(B):
        pe.wait_ge(m.xn_ready, b + 1)
        pe_transpose4(pe, m, m.bank[b], [m.xn[:, b, k * P:(k + 1) * P] for k in range(KT)], m.ident[:]).then_inc(
            m.xnT_mm, 1)
    wait_unit(pe, m.lo_done, S_WQ)
    pe.wait_ge(m.xT_lo_done, B)
    for f in range(KT):
        for k in range(KT):
            last = three_passes(pe, m.bank[2 + f // 2][:, (f % 2) * B * P:(f % 2 + 1) * B * P],
                                m.k_quad[0][:, k, f * P:(f + 1) * P], m.k_quad[1][:, k, f * P:(f + 1) * P],
                                m.xT_hi[:, k, :], m.xT_lo[:, k, :], k == 0, k == KT - 1)
        if f % 2:
            last.then_inc(m.q_mm, 1)
    for b in range(B):
        for n in range(b * NCH, (b + 1) * NCH):
            c_hi, c_lo = ctx_slot(m, n)
            wait_unit(pe, m.lo_done, S_CTX + n)
            if n == 0:
                wait_unit(pe, m.lo_done, S_WK)
                wait_unit(pe, m.lo_done, S_WV)
                pe.wait_ge(m.q_done, KT)
            for f in range(KT):
                if n % NCH:
                    pe.wait_ge(m.k_done, (n - 1) * KT + f + 1)
                for k in range(KT):
                    last = three_passes(pe, m.bank[f][:], m.w_hi[1][:, k, f * P:(f + 1) * P],
                                        m.w_lo[1][:, k, f * P:(f + 1) * P], c_hi[:, k, :], c_lo[:, k, :],
                                        k == 0, k == KT - 1)
                last.then_inc(m.k_mm, 1)
            if n == NCH:
                pe.wait_ge(m.o_copied, GROUPS)
            for t in range(KT):
                if n % NCH:
                    pe.wait_ge(m.v_done, (n - 1) * KT + t + 1)
                for k in range(KT):
                    last = three_passes(pe, m.bank[4 + t][:], c_hi[:, k, t * P:(t + 1) * P],
                                        c_lo[:, k, t * P:(t + 1) * P], m.w_hi[2][:, k, :], m.w_lo[2][:, k, :],
                                        k == 0, k == KT - 1)
                last.then_inc(m.v_mm, 1)
        pe.wait_ge(m.k_done, (b + 1) * NCH * KT)
        pe.wait_ge(m.v_done, (b + 1) * NCH * KT)
        pe.wait_ge(m.mask_ready, 1)
        pe.wait_ge(m.ident_ready, 1)

        def scores(g, j, c, first=False):
            if not first:
                pe.wait_ge(m.exp_done, (g * HPG + j - 1) * NCH + c + 1)
            pe.wait_ge(m.k_lo_done, (g * HPG + j) * NCH + c + 1)
            if c == 0:
                pe.wait_ge((m.k_hi2_even, m.k_hi2_odd)[j % 2], (g * (HPG // 2) + j // 2 + 1) * 16)
                pe.wait_ge(m.qz_done, g * HPG + j + 1)
            bank = m.bank[S_BANKS[c]][:]
            pe.matmul(bank, m.ident_r[:], m.mask_add[:, c * CHUNK:(c + 1) * CHUNK], start=True, stop=False)
            pe.matmul(bank, m.q_quad[:, j, :], m.k_quad[j % 2][:, c, :], start=False, stop=True).then_inc(m.s_mm, 1)

        def transposed(g, j, c):
            pe.wait_ge(m.exp_done, (g * HPG + j) * NCH + c + 1)
            pe_transpose4(pe, m, m.bank[T_BANKS[T_SLOT[c]]], [m.probs[:, c, t * P:(t + 1) * P] for t in range(KT)],
                          m.ident[:]).then_inc(m.pT_mm, 1)

        def values(g, j, c):
            if j == 0 and c == 0:
                pe.wait_ge(m.v_part_done, (g + 1) * HPG)
            if c < NCH - 1:
                pe.wait_ge(m.pT_act, (g * HPG + j) * (NCH - 1) + c + 1)
            else:
                pe.wait_ge(m.pT_dve, g * HPG + j + 1)
            rows = slice(j * XDH, (j + 1) * XDH)
            for t in range(KT):
                last = pe.matmul(m.bank[O_BANK][rows, 0:P], m.v_grp[:, c * KT + t, rows],
                                 m.probs_T[:, T_SLOT[c], t * P:(t + 1) * P], start=(c == 0 and t == 0),
                                 stop=(c == NCH - 1 and t == KT - 1), tile_position=(0, j * XDH))
            last.then_inc(m.pv_mm, 1)

        def group(g, more):
            for j in range(1, HPG + 1):
                ahead = (g, j) if j < HPG else (g + 1, 0) if more else None

                def ahead_scores(c):
                    if ahead:
                        scores(*ahead, c)

                ahead_scores(0)
                if j > 1:
                    values(g, j - 2, 3)
                ahead_scores(1)
                transposed(g, j - 1, 0)
                ahead_scores(2)
                ahead_scores(3)
                values(g, j - 1, 0)
                transposed(g, j - 1, 1)
                transposed(g, j - 1, 2)
                values(g, j - 1, 1)
                transposed(g, j - 1, 3)
                values(g, j - 1, 2)
            values(g, HPG - 1, 3)

        for c in range(NCH):
            scores(b * GROUPS, 0, c, first=True)
        with pe.Fori(0, GROUPS - 1) as fb:
            group(fb + b * GROUPS, True)
        group((b + 1) * GROUPS - 1, False)
    pe.wait_ge(m.o_copied, NG)
    for b in range(B):
        pe_transpose4(pe, m, m.bank[b], [m.o_feat[:, b * GROUPS + k, :] for k in range(GROUPS)], m.ident[:]).then_inc(
            m.oT_mm, 1)
    for b in range(B):
        pe.wait_ge(m.oT_done, b + 1)
        pe_transpose4(pe, m, m.bank[4 + b], [m.o_tok[:, b, k * P:(k + 1) * P] for k in range(KT)], m.ident[:]).then_inc(
            m.vec_mm, 1)
    wait_unit(pe, m.lo_done, S_WO)
    slot = S_WO % RING
    for b in range(B):
        pe.wait_ge(m.vec_lo, (b + 1) * KT)
        for k in range(KT):
            last = three_passes(pe, m.bank[2 + b][:], m.vecT_hi[:, k, b * P:(b + 1) * P],
                                m.vecT_lo[:, k, b * P:(b + 1) * P], m.w_hi[slot][:, k, :], m.w_lo[slot][:, k, :],
                                k == 0, k == KT - 1)
        last.then_inc(m.o_mm, 1)


ROW_G1, ROW_B1, ROW_BF, ROW_G2, ROW_B2 = range(5)
SG = 8
KR_BANKS, HT_BANKS = (4, 5), (0, 1)
Q_BANKS, K_BANKS, V_BANKS = (6, 7, 2, 3), (0, 1, 4, 5), (6, 7, 2, 3)
SC_BANKS, PT_BANKS, PV_BANKS = (0, 1, 4, 5), (6, 7), (2, 3)
WO_BANKS, H1T_BANKS, FF2_BANKS = (0, 1), (4, 5), (0, 1)
FF1_BANKS, FF1_TOK_BANKS = (4, 5, 0, 1, 6, 7, 2, 3), (6, 7, 2, 3)
FF1_OUTS = DF // (2 * P)
FF1_TOK = 4
FF1_TOK_ORDER = ((0, 0), (1, 0), (0, 1), (1, 1))


def layer_memory(m):
    m.rows = m.sb("rows", [P, 5, D])
    m.h_tok = m.sb("h_tok", [P, B, D])
    m.s_tok = m.sb("s_tok", [P, B, D])
    m.hT_hi = m.sb("hT_hi", [P, KT, B * P], F32R)
    m.hT_lo = m.sb("hT_lo", [P, KT, B * P], F32R)
    m.v_tok = m.sb("v_tok", [P, B, H * DH])
    m.p_lay = m.sb("p_lay", [P, SG, CHUNK])
    m.pT_lay = m.sb("pT_lay", [P, 2, CHUNK])
    m.max_lay = m.sb("max_lay", [P, SG, 4])
    m.shift_lay = m.sb("shift_lay", [P, SG, 4])
    m.sum_lay = m.sb("sum_lay", [P, SG, 4])
    m.inv_lay = m.sb("inv_lay", [P, SG, 4])
    m.vT_hi = m.sb("vT_hi", [P, H // 2, B * P], F32R)
    m.vT_lo = m.sb("vT_lo", [P, H // 2, B * P], F32R)
    m.ff_t = m.sb("ff_t", [P, 2, CHUNK])
    outer = m.ctx
    with ExitStack() as m.ctx:
        m.q_stack = m.sb("q_stack", [P, H, B * P])
        m.k_stack = m.sb("k_stack", [P, H, B * P])
    with ExitStack() as m.ctx:
        m.ff_hi = m.sb("ff_hi", [P, DF // P, B * P], F32R)
        m.ff_lo = m.sb("ff_lo", [P, DF // P, B * P], F32R)
    m.ctx = outer
    (m.rows_in, m.wo_half, m.ff2_part, m.h_ready, m.hT_mm, m.hT_hi_done, m.hT_lo_done, m.kr_mm, m.kr_tok_done,
     m.krT_mm, m.kr_act, m.kr_dve, m.lq_mm, m.lq_act, m.lq_dve, m.lk_mm, m.lk_act, m.lk_dve, m.lv_mm, m.lv_act,
     m.lv_dve, m.sc_mm, m.lmax_done, m.lshift_done, m.lexp_done, m.linv_done, m.lnorm_done, m.lpT_mm,
     m.lpT_even, m.lpT_odd, m.lpv_mm, m.vT_hi_done, m.vT_lo_done, m.wo_mm, m.h1_ready, m.h1T_mm, m.h1T_hi,
     m.h1T_lo, m.ff1_tok_mm, m.ff1_tok_act, m.ff1_tok_dve, m.ff1_mm, m.relu_done, m.ff_hi_done, m.ff_lo_done,
     m.ff2_mm, m.dve_step_l, m.x2_done) = m.sems(
        "rows_in wo_half ff2_part h_ready hT_mm hT_hi_done hT_lo_done kr_mm kr_tok_done krT_mm kr_act kr_dve "
        "lq_mm lq_act lq_dve lk_mm lk_act lk_dve lv_mm lv_act lv_dve sc_mm lmax_done lshift_done lexp_done "
        "linv_done lnorm_done lpT_mm lpT_even lpT_odd lpv_mm vT_hi_done vT_lo_done wo_mm h1_ready h1T_mm "
        "h1T_hi h1T_lo ff1_tok_mm ff1_tok_act ff1_tok_dve ff1_mm relu_done ff_hi_done ff_lo_done ff2_mm "
        "dve_step_l x2_done")


def sp_layers(sp, m):
    sp.wait_ge(m.uv_in, 16)
    with sp.Fori(0, L) as i:
        for k in range(RING, LU + RING):
            wait_unit(sp, m.lo_done, S_LAYER + k - RING, i, LU)
            sp.dma_start(m.raw[:, k % RING, :], m.dram["w_stream"][bass.ds(i * LU + k, 1)].rearrange(
                "a p n -> (a p) n")).then_inc(m.loaded[k % RING], 16)
            if k == U_WK:
                sp.wait_ge(m.h_ready, (i + 1) * B)
                sp.dma_start(m.rows[:], m.dram["layer_rows"][bass.ds(i, 1)].rearrange(
                    "a r d -> (a r) d").partition_broadcast(P)).then_inc(m.rows_in, 16)


def pool_layers(pool, m):
    split_lo(pool, m, S_LAYER + 2)
    with pool.Fori(0, L) as i:
        for k in range(RING, LU + RING):
            split_lo(pool, m, S_LAYER + k, i, LU)


def by_block(bank):
    return bank[:].rearrange("p (k t) -> p k t", t=P)


def pairs(bank):
    return bank[:].rearrange("p (k t) -> p k t", t=B * P)


def act_layers(act, m):
    act.wait_ge(m.o_mm, B)
    split_hi(act, m, S_LAYER + 2)
    for t in range(B):
        ln_root(act, m, 2, t)
    act.wait_ge(m.uv_in, 16)
    act.wait_ge(m.bias_in, 16)
    with act.Fori(0, L) as i:

        def unit(k):
            act.wait_ge(*unit_used(m, k - RING, i))
            split_hi(act, m, S_LAYER + k, i, LU)

        for u in range(2):
            act.wait_ge(m.kr_mm, i * 2 + u + 1)
            act.activation(m.ff_t[:, u, :], m.bank[KR_BANKS[u]][:], ACT.Copy).then_inc(m.kr_tok_done, 1)
            if u == 0:
                unit(RING)
            act.wait_ge(m.hT_mm, i * B + u + 1)
            act.activation(m.hT_hi[:, :, u * P:(u + 1) * P], by_block(m.bank[HT_BANKS[u]]), ACT.Copy).then_inc(
                m.hT_hi_done, 1)
        unit(RING + 1)
        for u in range(2):
            act.wait_ge(m.krT_mm, i * 2 + u + 1)
            for b in range(B):
                last = act.activation(m.k_stack[DH:P, 8 * u + 1:8 * u + 8:2, b * P:(b + 1) * P],
                                      by_block(m.bank[KR_BANKS[u]])[DH:P], ACT.Copy)
            last.then_inc(m.kr_act, 1)
        for o in range(4):
            act.wait_ge(m.lq_mm, i * 4 + o + 1)
            for t in range(2):
                head = 4 * o + 2 * t + 1
                for w in range(2):
                    last = act.activation(m.q_stack[w * DH:(w + 1) * DH, head, :],
                                          pairs(m.bank[Q_BANKS[o]])[DH:P, t, :], ACT.Identity,
                                          bias=m.uv_sb[DH:P, w, head:head + 1])
            last.then_inc(m.lq_act, 1)
            if o % 2:
                unit(5 + o // 2)
        for o in range(4):
            act.wait_ge(m.lk_mm, i * 4 + o + 1)
            act.activation(m.k_stack[0:DH, 4 * o + 1:4 * o + 4:2, :], pairs(m.bank[K_BANKS[o]])[DH:P],
                           ACT.Copy).then_inc(m.lk_act, 1)
            if o % 2:
                unit(7 + o // 2)

        def values(u):
            act.wait_ge(m.lv_mm, i * 4 + 2 * u + 2)
            act.activation(m.v_tok[:, 1, u * CHUNK:(u + 1) * CHUNK], m.bank[V_BANKS[2 * u + 1]][:],
                           ACT.Copy).then_inc(m.lv_act, 1)
            unit(9 + u)

        def exps(g):
            act.wait_ge(m.lshift_done, i * SG + g + 1)
            for t in range(4):
                last = act.activation(m.p_lay[:, g, t * P:(t + 1) * P],
                                      m.bank[SC_BANKS[g % 4]][:, t * P:(t + 1) * P], ACT.Exp,
                                      bias=m.shift_lay[:, g, t:t + 1], scale=L_SCALE,
                                      accum_out=m.sum_lay[:, g, t:t + 1])
            last.then_inc(m.lexp_done, 1)

        def transposed(g):
            act.wait_ge(m.lpT_mm, i * SG + g + 1)
            if g >= 2:
                act.wait_ge(m.lpv_mm, i * SG + g - 1)
            act.activation(m.pT_lay[:, 1, :], m.bank[PT_BANKS[1]][:], ACT.Copy).then_inc(m.lpT_odd, 1)

        def vector_hi(q):
            b, half = q // 2, q % 2
            act.wait_ge(m.lpv_mm, i * SG + 2 * q + 2)
            act.activation(m.vT_hi[:, 4 * half:4 * half + 4, b * P:(b + 1) * P], by_block(m.bank[PV_BANKS[half]]),
                           ACT.Copy).then_inc(m.vT_hi_done, 1)

        exps(0)
        exps(1)
        values(0)
        for g in range(2, 6):
            exps(g)
        values(1)
        exps(6)
        transposed(1)
        exps(7)
        transposed(3)
        vector_hi(0)
        transposed(5)
        vector_hi(1)
        transposed(7)
        vector_hi(2)
        vector_hi(3)

        def normed_hi(b):
            act.wait_ge(m.h1T_mm, i * B + b + 1)
            act.activation(m.hT_hi[:, :, b * P:(b + 1) * P], by_block(m.bank[H1T_BANKS[b]]), ACT.Copy).then_inc(
                m.h1T_hi, 1)

        ln_root(act, m, i * 2 + 3, 0)
        unit(11)
        normed_hi(0)
        unit(12)
        ln_root(act, m, i * 2 + 3, 1)
        for n in range(2):
            act.wait_ge(m.ff1_tok_mm, i * FF1_TOK + n + 1)
            act.activation(m.p_lay[:, n, :], m.bank[FF1_TOK_BANKS[n]][:], ACT.Copy).then_inc(m.ff1_tok_act, 1)
            if n == 0:
                normed_hi(1)
        unit(13)
        for f in range(FF1_OUTS):
            act.wait_ge(m.ff1_mm, i * FF1_OUTS + f + 1)
            if f >= 2:
                act.wait_ge(m.ff_lo_done, i * FF1_OUTS + f - 1)
            for t in range(2):
                last = act.activation(m.ff_t[:, f % 2, t * B * P:(t + 1) * B * P], pairs(m.bank[FF1_BANKS[f]])[:, t, :],
                                      ACT.Relu, bias=m.ff1_bias_sb[:, bass.ds(i, 1), 2 * f + t])
            last.then_inc(m.relu_done, 1)
            if f % 2:
                unit(14 + f // 2)
        unit(18)
        ln_root(act, m, i * 2 + 4, 0)
        unit(19)
        ln_root(act, m, i * 2 + 4, 1)
        unit(20)


def dve_layers(dve, m, step):
    dve.wait_ge(m.x1_done, B)
    for b in range(B):
        ln_scale(dve, m, step, m.x_res[:, b, :], b, 2)
        step.wait()
        ln_apply(dve, m, m.h_tok[:, b, :], m.x_res[:, b, :], b).then_inc(m.h_ready, 1)
    dve.wait_ge(m.uv_in, 16)
    with dve.Fori(0, L) as i:
        own = Step(dve, m.dve_step_l, 0, i, 32)
        for b in range(B):
            dve.wait_ge(m.hT_hi_done, i * B + b + 1)
            dve.tensor_tensor(m.hT_lo[:, :, b * P:(b + 1) * P], by_block(m.bank[HT_BANKS[b]]),
                              m.hT_hi[:, :, b * P:(b + 1) * P].bitcast(F32), ALU.subtract).then_inc(m.hT_lo_done, 1)
        for u in range(2):
            dve.wait_ge(m.krT_mm, i * 2 + u + 1)
            for b in range(B):
                last = dve.tensor_copy(m.k_stack[DH:P, 8 * u:8 * u + 8:2, b * P:(b + 1) * P],
                                       by_block(m.bank[KR_BANKS[u]])[0:DH])
            last.then_inc(m.kr_dve, 1)
        for o in range(4):
            dve.wait_ge(m.lq_mm, i * 4 + o + 1)
            heads = slice(4 * o, 4 * o + 4, 2)
            for w in range(2):
                last = dve.tensor_tensor(m.q_stack[w * DH:(w + 1) * DH, heads, :], pairs(m.bank[Q_BANKS[o]])[0:DH],
                                         m.uv_sb[0:DH, w, heads].unsqueeze(2).to_broadcast([DH, 2, B * P]), ALU.add)
            last.then_inc(m.lq_dve, 1)
        for o in range(4):
            dve.wait_ge(m.lk_mm, i * 4 + o + 1)
            dve.tensor_copy(m.k_stack[0:DH, 4 * o:4 * o + 4:2, :], pairs(m.bank[K_BANKS[o]])[0:DH]).then_inc(
                m.lk_dve, 1)

        def values(u):
            dve.wait_ge(m.lv_mm, i * 4 + 2 * u + 1)
            dve.tensor_copy(m.v_tok[:, 0, u * CHUNK:(u + 1) * CHUNK], m.bank[V_BANKS[2 * u]][:]).then_inc(m.lv_dve, 1)

        def maxima(g):
            dve.wait_ge(m.sc_mm, i * SG + g + 1)
            dve.tensor_reduce(m.max_lay[:, g, :], by_block(m.bank[SC_BANKS[g % 4]]), X_AXIS, ALU.max,
                              negate=True).then_inc(m.lmax_done, 1)
            dve.wait_ge(m.lmax_done, i * SG + g + 1)
            dve.tensor_scalar(m.shift_lay[:, g, :], m.max_lay[:, g, :], L_SCALE, None, ALU.mult).then_inc(
                m.lshift_done, 1)

        def normed(g):
            dve.wait_ge(m.lexp_done, i * SG + g + 1)
            dve.reciprocal(m.inv_lay[:, g, :], m.sum_lay[:, g, :]).then_inc(m.linv_done, 1)
            dve.wait_ge(m.linv_done, i * SG + g + 1)
            p = m.p_lay[:, g, :].rearrange("p (h t) -> p h t", h=4)
            dve.tensor_tensor(p, p, m.inv_lay[:, g, :].unsqueeze(2).to_broadcast([P, 4, P]), ALU.mult).then_inc(
                m.lnorm_done, 1)

        def transposed(g):
            dve.wait_ge(m.lpT_mm, i * SG + g + 1)
            if g >= 2:
                dve.wait_ge(m.lpv_mm, i * SG + g - 1)
            dve.tensor_copy(m.pT_lay[:, 0, :], m.bank[PT_BANKS[0]][:]).then_inc(m.lpT_even, 1)

        def vector_lo(q):
            b, half = q // 2, q % 2
            dve.wait_ge(m.vT_hi_done, i * 4 + q + 1)
            hi = m.vT_hi[:, 4 * half:4 * half + 4, b * P:(b + 1) * P]
            dve.tensor_tensor(m.vT_lo[:, 4 * half:4 * half + 4, b * P:(b + 1) * P], by_block(m.bank[PV_BANKS[half]]),
                              hi.bitcast(F32), ALU.subtract).then_inc(m.vT_lo_done, 1)

        values(0)
        for g in range(0, SG, 2):
            if g == 4:
                values(1)
            maxima(g)
            if g == 6:
                transposed(0)
            maxima(g + 1)
            if g == 6:
                transposed(2)
            normed(g)
            normed(g + 1)
        vector_lo(0)
        transposed(4)
        vector_lo(1)
        transposed(6)
        vector_lo(2)
        vector_lo(3)

        def layer_norm(dst, t, n, g, b, sem):
            src = m.s_tok[:, t, :]
            own.wait()
            ln_scale(dve, m, own, src, t, n)
            own.done(dve.scalar_tensor_tensor(src, src, m.mean_var[:, t, 0:1], m.rows[:, g, :], ALU.subtract, ALU.mult))
            own.wait()
            dve.scalar_tensor_tensor(dst[:, t, :], src, m.rstd[:, t:t + 1], m.rows[:, b, :], ALU.mult,
                                     ALU.add).then_inc(sem, 1)

        dve.wait_ge(m.rows_in, i * 16 + 16)
        dve.wait_ge(m.h_ready, (i + 1) * B)
        for b in range(B):
            dve.wait_ge(m.wo_mm, i * B + b + 1)
            own.done(dve.tensor_tensor(m.s_tok[:, b, :], m.bank[WO_BANKS[b]][:], m.h_tok[:, b, :], ALU.add))
            layer_norm(m.s_tok, b, i * 2 + 3, ROW_G1, ROW_B1, m.h1_ready)
            dve.wait_ge(m.h1T_hi, i * B + b + 1)
            dve.tensor_tensor(m.hT_lo[:, :, b * P:(b + 1) * P], by_block(m.bank[H1T_BANKS[b]]),
                              m.hT_hi[:, :, b * P:(b + 1) * P].bitcast(F32), ALU.subtract).then_inc(m.h1T_lo, 1)
        for n in range(2, 4):
            dve.wait_ge(m.ff1_tok_mm, i * FF1_TOK + n + 1)
            dve.tensor_copy(m.p_lay[:, n, :], m.bank[FF1_TOK_BANKS[n]][:]).then_inc(m.ff1_tok_dve, 1)
        for f in range(FF1_OUTS):
            dve.wait_ge(m.relu_done, i * FF1_OUTS + f + 1)
            hi = m.ff_hi[:, 2 * f:2 * f + 2, :].rearrange("p k t -> p (k t)")
            dve.tensor_copy(hi, m.ff_t[:, f % 2, :]).then_inc(m.ff_hi_done, 1)
            dve.wait_ge(m.ff_hi_done, i * FF1_OUTS + f + 1)
            dve.tensor_tensor(m.ff_lo[:, 2 * f:2 * f + 2, :].rearrange("p k t -> p (k t)"), m.ff_t[:, f % 2, :],
                              hi.bitcast(F32), ALU.subtract).then_inc(m.ff_lo_done, 1)
        for b in range(B):
            dve.wait_ge(m.ff2_mm, i * B + b + 1)
            own.done(dve.tensor_tensor(m.s_tok[:, b, :], m.bank[FF2_BANKS[b]][:], m.rows[:, ROW_BF, :], ALU.add))
            layer_norm(m.h_tok, b, i * 2 + 4, ROW_G2, ROW_B2, m.h_ready)
        assert own.n == own.per, own.n
    dve.wait_ge(m.h_ready, (L + 1) * B)
    for b in range(B):
        dve.tensor_tensor(m.x_res[:, b, :], m.x_res[:, b, :], m.h_tok[:, b, :], ALU.add).then_inc(m.x2_done, 1)


def unit_used(m, u, i):
    if u < U_WQ:
        return m.kr_mm, i * 2 + u + 1
    if u < U_WO:
        return (m.lq_mm, m.lk_mm, m.lv_mm)[(u - U_WQ) // 2], i * 4 + 2 * (u % 2) + 2
    if u < U_FF1:
        return (m.wo_half, i + 1) if u == U_WO else (m.wo_mm, i * B + B)
    if u < U_FF1 + 2:
        return m.ff1_tok_mm, i * FF1_TOK + u - U_FF1 + 3
    if u < U_FF2:
        return m.ff1_mm, i * FF1_OUTS + 2 * (u - U_FF1) + 2
    return (m.ff2_part, i * 3 + u - U_FF2 + 1) if u < LU - 1 else (m.ff2_mm, i * B + B)


def pe_layers(pe, m):
    wait_unit(pe, m.lo_done, S_WO)
    pe.wait_ge(m.x1_done, B)
    pe.wait_ge(m.r_ready, 1)
    with pe.Fori(0, L) as i:

        def unit(k):
            wait_unit(pe, m.lo_done, S_LAYER + k, i, LU)
            return m.w_hi[k % RING], m.w_lo[k % RING]

        for u in range(2):
            w_hi, w_lo = unit(U_WR + u)
            for k in range(KT):
                last = three_passes(pe, m.bank[KR_BANKS[u]][:], m.r_hi[:, k, :], m.r_lo[:, k, :], w_hi[:, k, :],
                                    w_lo[:, k, :], k == 0, k == KT - 1)
            last.then_inc(m.kr_mm, 1)
            pe.wait_ge(m.h_ready, i * B + u + 1)
            pe_transpose4(pe, m, m.bank[HT_BANKS[u]], [m.h_tok[:, u, k * P:(k + 1) * P] for k in range(KT)],
                          m.ident[:]).then_inc(m.hT_mm, 1)
        for u in range(2):
            pe.wait_ge(m.kr_tok_done, i * 2 + u + 1)
            pe_transpose4(pe, m, m.bank[KR_BANKS[u]], [m.ff_t[:, u, t * P:(t + 1) * P] for t in range(4)],
                          m.ident[:]).then_inc(m.krT_mm, 1)
        pe.wait_ge(m.hT_lo_done, (i + 1) * B)

        def by_feature(unit0, banks, sem, free):
            for o in range(4):
                if o % 2 == 0:
                    w_hi, w_lo = unit(unit0 + o // 2)
                free(o)
                for q in range(2):
                    cols = slice((2 * (o % 2) + q) * P, (2 * (o % 2) + q + 1) * P)
                    for k in range(KT):
                        last = three_passes(pe, m.bank[banks[o]][:, q * B * P:(q + 1) * B * P], w_hi[:, k, cols],
                                            w_lo[:, k, cols], m.hT_hi[:, k, :], m.hT_lo[:, k, :],
                                            k == 0, k == KT - 1)
                last.then_inc(sem, 1)

        def k_bank_free(o):
            if o >= 2:
                pe.wait_ge(m.kr_dve, i * 2 + o - 1)
                pe.wait_ge(m.kr_act, i * 2 + o - 1)

        by_feature(U_WQ, Q_BANKS, m.lq_mm, lambda o: None)
        by_feature(U_WK, K_BANKS, m.lk_mm, k_bank_free)

        def value_rows(u, b):
            w_hi, w_lo = unit(U_WV + u)
            pe.wait_ge(m.lq_act, i * 4 + 2 * u + b + 1)
            pe.wait_ge(m.lq_dve, i * 4 + 2 * u + b + 1)
            for k in range(KT):
                last = three_passes(pe, m.bank[V_BANKS[2 * u + b]][:], m.hT_hi[:, k, b * P:(b + 1) * P],
                                    m.hT_lo[:, k, b * P:(b + 1) * P], w_hi[:, k, :], w_lo[:, k, :],
                                    k == 0, k == KT - 1)
            last.then_inc(m.lv_mm, 1)

        def scores(g):
            if g == 0:
                pe.wait_ge(m.lk_act, i * 4 + 4)
                pe.wait_ge(m.lk_dve, i * 4 + 4)
            if g >= 4:
                pe.wait_ge(m.lexp_done, i * SG + g - 3)
            b = g // 4
            for t in range(4):
                head = 4 * (g % 4) + t
                last = pe.matmul(m.bank[SC_BANKS[g % 4]][:, t * P:(t + 1) * P], m.q_stack[:, head, b * P:(b + 1) * P],
                                 m.k_stack[:, head, b * P:(b + 1) * P], start=True, stop=True)
            last.then_inc(m.sc_mm, 1)

        def transposed(g):
            pe.wait_ge(m.lnorm_done, i * SG + g + 1)
            if g < 2:
                pe.wait_ge((m.lv_dve, m.lv_act)[g], i * 2 + 1)
            else:
                pe.wait_ge((m.lpT_even, m.lpT_odd)[g % 2], i * 4 + g // 2)
            pe_transpose4(pe, m, m.bank[PT_BANKS[g % 2]], [m.p_lay[:, g, t * P:(t + 1) * P] for t in range(4)],
                          m.ident[:]).then_inc(m.lpT_mm, 1)

        def values(g):
            pe.wait_ge((m.lpT_even, m.lpT_odd)[g % 2], i * 4 + g // 2 + 1)
            half, b = (g % 4) // 2, g // 4
            if g == 0:
                pe.wait_ge(m.lv_dve, i * 2 + 2)
                pe.wait_ge(m.lv_act, i * 2 + 2)
            if g >= 4:
                pe.wait_ge(m.vT_lo_done, i * 4 + half + 1)
            for t in range(4):
                head = 4 * (g % 4) + t
                side, block = head % 2, (head // 2) % 4
                last = pe.matmul(m.bank[PV_BANKS[half]][side * DH:(side + 1) * DH, block * P:(block + 1) * P],
                                 m.v_tok[:, b, head * DH:(head + 1) * DH], m.pT_lay[:, g % 2, t * P:(t + 1) * P],
                                 start=True, stop=True, tile_position=(0, side * DH))
            last.then_inc(m.lpv_mm, 1)

        for pair in range(4):
            value_rows(pair // 2, pair % 2)
            scores(2 * pair)
            if pair == 3:
                transposed(0)
            scores(2 * pair + 1)
        for g in range(SG):
            if g + 1 < SG:
                transposed(g + 1)
            values(g)

        def normed_by_feature(b):
            pe.wait_ge(m.h1_ready, i * B + b + 1)
            pe_transpose4(pe, m, m.bank[H1T_BANKS[b]], [m.s_tok[:, b, k * P:(k + 1) * P] for k in range(KT)],
                          m.ident[:]).then_inc(m.h1T_mm, 1)

        for b in range(B):
            for u in range(2):
                w_hi, w_lo = unit(U_WO + u)
                if u == 0:
                    pe.wait_ge(m.vT_lo_done, i * 4 + 2 * b + 2)
                for k in range(KT):
                    if (b, u, k) == (1, 1, KT - 1):
                        normed_by_feature(0)
                    last = three_passes(pe, m.bank[WO_BANKS[b]][:], m.vT_hi[:, KT * u + k, b * P:(b + 1) * P],
                                        m.vT_lo[:, KT * u + k, b * P:(b + 1) * P], w_hi[:, k, :], w_lo[:, k, :],
                                        u == 0 and k == 0, u == 1 and k == KT - 1)
                if u == 1:
                    last.then_inc(m.wo_mm, 1)
                elif b == B - 1:
                    last.then_inc(m.wo_half, 1)

        def hidden_by_token(n):
            u, b = FF1_TOK_ORDER[n]
            w_hi, w_lo = unit(U_FF1 + u)
            for k in range(KT):
                if n == 1 and k == 2:
                    normed_by_feature(1)
                last = three_passes(pe, m.bank[FF1_TOK_BANKS[n]][:], m.hT_hi[:, k, b * P:(b + 1) * P],
                                    m.hT_lo[:, k, b * P:(b + 1) * P], w_hi[:, k, :], w_lo[:, k, :],
                                    k == 0, k == KT - 1)
            last.then_inc(m.ff1_tok_mm, 1)

        def hidden_turned(u):
            pe.wait_ge(m.ff1_tok_act, i * 2 + u + 1)
            pe.wait_ge(m.ff1_tok_dve, i * 2 + u + 1)
            for f in (2 * u, 2 * u + 1):
                blocks = [m.p_lay[:, 2 * b + u, (2 * (f % 2) + q) * P:(2 * (f % 2) + q + 1) * P]
                          for q in range(2) for b in range(B)]
                pe_transpose4(pe, m, m.bank[FF1_BANKS[f]], blocks, m.ident[:]).then_inc(m.ff1_mm, 1)

        def hidden_by_feature(f):
            w_hi, w_lo = unit(U_FF1 + f // 2)
            for q in range(2):
                cols = slice((2 * (f % 2) + q) * P, (2 * (f % 2) + q + 1) * P)
                for k in range(KT):
                    last = three_passes(pe, m.bank[FF1_BANKS[f]][:, q * B * P:(q + 1) * B * P], w_hi[:, k, cols],
                                        w_lo[:, k, cols], m.hT_hi[:, k, :], m.hT_lo[:, k, :], k == 0, k == KT - 1)
            last.then_inc(m.ff1_mm, 1)

        pe.wait_ge(m.h1T_lo, i * B + 1)
        hidden_by_token(0)
        hidden_by_token(1)
        pe.wait_ge(m.h1T_lo, i * B + 2)
        hidden_by_token(2)
        hidden_by_token(3)
        hidden_turned(0)
        hidden_turned(1)
        for f in range(FF1_TOK, FF1_OUTS):
            hidden_by_feature(f)
        pe.wait_ge(m.relu_done, i * FF1_OUTS + FF1_TOK)
        for u, b in ((0, 0), (0, 1), (1, 0), (1, 1), (2, 0), (3, 0), (2, 1), (3, 1)):
            w_hi, w_lo = unit(U_FF2 + u)
            pe.wait_ge(m.ff_lo_done, i * FF1_OUTS + 2 * u + 2)
            for k in range(KT):
                last = three_passes(pe, m.bank[FF2_BANKS[b]][:], m.ff_hi[:, KT * u + k, b * P:(b + 1) * P],
                                    m.ff_lo[:, KT * u + k, b * P:(b + 1) * P], w_hi[:, k, :], w_lo[:, k, :],
                                    u == 0 and k == 0, u == 3 and k == KT - 1)
            if u == 3:
                last.then_inc(m.ff2_mm, 1)
            elif b == B - 1:
                last.then_inc(m.ff2_part, 1)


EXTRA = (B * P * 2 - 1) // (P + 1)
TURNS = E + EXTRA + 1
QUARTERS = F // CHUNK
E_RING = 2 * RING
UP_UNITS = [k for k, (name, _) in enumerate(E_ORDER) if name != "wo"]
DOWN_UNITS = [k for k, (name, _) in enumerate(E_ORDER) if name == "wo"]
UP_BANKS, HIDDEN_BANK, Y_BANK, XG_BANKS = (0, 2), 4, 5, (6, 7)
BELOW_ALL = -3e38


def moe_memory(m):
    m.xn_tok = m.sb("xn_tok", [P, B, D])
    m.xn_hi = m.sb("xn_hi", [P, B, D], F32R)
    m.xn_lo = m.sb("xn_lo", [P, B, D], F32R)
    m.xn_T = m.sb("xn_T", [P, KT, B * P])
    m.logits = m.sb("logits", [P, B, E])
    m.is_max = m.sb("is_max", [P, B, E])
    m.candidate = m.sb("candidate", [P, B, E])
    m.chosen1 = m.sb("chosen1", [P, B, E])
    m.chosen2 = m.sb("chosen2", [P, B, E])
    m.rest = m.sb("rest", [P, B, E])
    m.routed = m.sb("routed", [P, B, E])
    m.weighted1 = m.sb("weighted1", [P, B, E])
    m.position = m.sb("position", [P, B, E])
    m.best1 = m.sb("best1", [P, B])
    m.best2 = m.sb("best2", [P, B])
    m.first1 = m.sb("first1", [P, B])
    m.first2 = m.sb("first2", [P, B])
    m.gap = m.sb("gap", [P, B])
    m.gap_exp = m.sb("gap_exp", [P, B])
    m.gap_sum = m.sb("gap_sum", [P, B])
    m.weight1 = m.sb("weight1", [P, B])
    m.weight2 = m.sb("weight2", [P, B])
    m.slot_of = m.sb("slot_of", [P, B, TURNS])
    m.gate_of = m.sb("gate_of", [P, B, TURNS])
    m.crowded = m.sb("crowded", [P, EXTRA + 1, E])
    m.order = m.sb("order", [P, E])
    m.first_one = m.sb("first_one", [P, 1])
    m.extra = m.sb("extra", [P, EXTRA, E])
    m.extra_index = m.sb("extra_index", [P, EXTRA, E])
    m.extra_gate = m.sb("extra_gate", [P, B, EXTRA, E])
    m.extra_position = m.sb("extra_position", [P, B, EXTRA, E])
    m.extra_slot = m.sb("extra_slot", [P, B, EXTRA])
    m.n_crowded = m.sb("n_crowded", [P, 1])
    m.n_turns = m.sb("n_turns", [P, 1], I32)
    m.expert_f = m.sb("expert_f", [P, TURNS])
    m.expert_of = m.sb("expert_of", [P, TURNS], I32)
    more = range(RING, E_RING)
    m.raw_more = m.sb("raw_more", [P, RING, KT * CHUNK])
    m.e_raw = [m.raw[:, s, :] for s in range(RING)] + [m.raw_more[:, s, :] for s in range(RING)]
    m.e_hi = m.w_hi + [m.sb(f"w_hi{s}", [P, KT, CHUNK], F32R) for s in more]
    m.e_lo = m.w_lo + [m.sb(f"w_lo{s}", [P, KT, CHUNK], F32R) for s in more]
    m.e_loaded = m.loaded + m.slot_sems("loaded_more")
    m.e_hi_done = m.hi_done + m.slot_sems("hi_done_more")
    m.e_lo_done = m.lo_done + m.slot_sems("lo_done_more")
    m.pick = m.sb("pick", [P, B, P], F32R)
    m.pick_T = m.sb("pick_T", [P, B, P], F32R)
    m.xg_hi = m.sb("xg_hi", [P, KT, P], F32R)
    m.xg_lo = m.sb("xg_lo", [P, KT, P], F32R)
    m.silu = m.sb("silu", [P, 2, CHUNK])
    m.hidden = m.sb("hidden", [P, 2, CHUNK])
    m.hidden_hi = m.sb("hidden_hi", [P, 2, CHUNK], F32R)
    m.hidden_lo = m.sb("hidden_lo", [P, 2, CHUNK], F32R)
    m.y_hi = m.sb("y_hi", [P, D], F32R)
    m.y_lo = m.sb("y_lo", [P, D], F32R)
    (m.xn2_ready, m.xn2_hi, m.xn2_lo, m.xn2_mm, m.xn2_T, m.logit_mm, m.gap_done, m.gap_exp_done, m.routed_done,
     m.rank_mm, m.n_ready, m.pick_done, m.gather_mm, m.xg_hi_done, m.xg_lo_done, m.pickT_mm, m.pickT_done,
     m.up_mm, m.silu_done, m.hidden_done, m.hiddenT_mm, m.hidden_hi_done, m.hidden_lo_done, m.down_mm,
     m.y_hi_done, m.y_lo_done, m.scatter_mm, m.acc_done, m.table_ready) = m.sems(
        "xn2_ready xn2_hi xn2_lo xn2_mm xn2_T logit_mm gap_done gap_exp_done routed_done rank_mm n_ready "
        "pick_done gather_mm xg_hi_done xg_lo_done pickT_mm pickT_done up_mm silu_done hidden_done hiddenT_mm "
        "hidden_hi_done hidden_lo_done down_mm y_hi_done y_lo_done scatter_mm acc_done table_ready")


def e_slot(k):
    return k % E_RING


def e_wait(eng, sem, k, i, each=1):
    before = S_MOE // RING if e_slot(k) < RING else 0
    eng.wait_ge(sem[e_slot(k)], (i * (EU // E_RING) + before + k // E_RING + 1) * each)


def e_split_hi(act, m, k, i):
    s = e_slot(k)
    e_wait(act, m.e_loaded, k, i, 16)
    act.activation(m.e_hi[s][:].rearrange("p k n -> p (k n)"), m.e_raw[s], ACT.Copy).then_inc(m.e_hi_done[s], 1)


def e_split_lo(eng, m, k, i):
    s = e_slot(k)
    e_wait(eng, m.e_hi_done, k, i)
    eng.tensor_tensor(m.e_lo[s][:].rearrange("p k n -> p (k n)"), m.e_raw[s],
                      m.e_hi[s][:].rearrange("p k n -> p (k n)").bitcast(F32), ALU.subtract).then_inc(m.e_lo_done[s], 1)


def e_unit_used(m, k, i):
    if k in UP_UNITS:
        return m.up_mm, i * len(UP_UNITS) + UP_UNITS.index(k) + 1
    return m.down_mm, i * QUARTERS + DOWN_UNITS.index(k) + 1


def turns(eng, m):
    eng.wait_ge(m.n_ready, 1)
    return eng.value_load(m.n_turns[0:1, 0:1], min_val=E, max_val=E + EXTRA)


def sp_moe(sp, m):
    sp.wait_ge(m.x2_done, B)
    for s in range(RING, E_RING):
        sp.dma_start(m.e_raw[s], m.dram["w_stream"][L * LU + s]).then_inc(m.e_loaded[s], 16)
    n = turns(sp, m)
    sp.wait_ge(m.table_ready, 1)
    with sp.Fori(0, n) as i:
        expert = sp.value_load(m.expert_of[0:1, bass.ds(i, 1)], min_val=0, max_val=E - 1)
        after = sp.value_load(m.expert_of[0:1, bass.ds(i + 1, 1)], min_val=0, max_val=E - 1)
        for k in range(E_RING, EU + E_RING):
            at = expert * EU + (L * LU + k) if k < EU else after * EU + (L * LU + k - EU)
            e_wait(sp, m.e_lo_done, k - E_RING, i)
            sp.dma_start(m.e_raw[e_slot(k)], m.dram["w_stream"][bass.ds(at, 1)].rearrange("a p n -> (a p) n")
                         ).then_inc(m.e_loaded[e_slot(k)], 16)
    sp.wait_ge(m.acc_done, n * B)
    sp.dma_start(m.dram["out"].rearrange("b p d -> p b d"), m.x_res[:]).then_inc(m.out_done, 16)
    sp.wait_ge(m.out_done, 16)


def pool_moe(pool, m):
    for k in range(RING, E_RING):
        e_split_lo(pool, m, k, 0)
    with pool.Fori(0, turns(pool, m)) as i:
        for k in range(E_RING, EU + E_RING):
            if e_slot(k) in (0, 2, 3):
                e_split_lo(pool, m, k, i)


def act_moe(act, m):
    for t in range(B):
        ln_root(act, m, 2 * L + 3, t)
    for b in range(B):
        act.wait_ge(m.xn2_ready, b + 1)
        act.activation(m.xn_hi[:, b, :], m.xn_tok[:, b, :], ACT.Copy).then_inc(m.xn2_hi, 1)
    for k in range(RING, E_RING):
        e_split_hi(act, m, k, 0)
    act.wait_ge(m.gap_done, 1)
    act.activation(m.gap_exp[:], m.gap[:], ACT.Exp).then_inc(m.gap_exp_done, 1)

    def gathered(e):
        act.wait_ge(m.gather_mm, e * 2 + 1)
        act.activation(m.xg_hi[:], by_block(m.bank[XG_BANKS[0]]), ACT.Copy).then_inc(m.xg_hi_done, 1)

    gathered(0)
    with act.Fori(0, turns(act, m)) as i:

        def unit(k):
            act.wait_ge(*e_unit_used(m, k - E_RING, i))
            e_split_hi(act, m, k, i)

        def silu(j):
            act.wait_ge(m.up_mm, i * len(UP_UNITS) + 2 * j + 1)
            act.activation(m.silu[:, j % 2, :], m.bank[UP_BANKS[j % 2]][:], ACT.Silu).then_inc(m.silu_done, 1)

        def hidden(j):
            act.wait_ge(m.hiddenT_mm, i * QUARTERS + j + 1)
            act.activation(m.hidden_hi[:, j % 2, :], m.bank[HIDDEN_BANK][:], ACT.Copy).then_inc(m.hidden_hi_done, 1)

        silu(0)
        unit(6)
        unit(7)
        act.wait_ge(m.pickT_mm, i + 1)
        act.activation(m.pick_T[:].rearrange("p b t -> p (b t)"), m.bank[HIDDEN_BANK][:, 0:B * P], ACT.Copy).then_inc(
            m.pickT_done, 1)
        silu(1)
        unit(8)
        unit(9)
        hidden(0)
        silu(2)
        unit(10)
        unit(11)
        unit(12)
        hidden(1)
        silu(3)
        unit(13)
        unit(14)
        hidden(2)
        gathered(i + 1)
        hidden(3)
        unit(15)
        unit(16)
        act.wait_ge(m.down_mm, i * QUARTERS + QUARTERS)
        act.activation(m.y_hi[:], m.bank[Y_BANK][:], ACT.Copy).then_inc(m.y_hi_done, 1)
        unit(17)


def dve_moe(dve, m, step):
    dve.wait_ge(m.x2_done, B)
    for b in range(B):
        ln_scale(dve, m, step, m.x_res[:, b, :], b, 2 * L + 3)
        step.wait()
        ln_apply(dve, m, m.xn_tok[:, b, :], m.x_res[:, b, :], b).then_inc(m.xn2_ready, 1)
    for b in range(B):
        dve.wait_ge(m.xn2_mm, b + 1)
        dve.tensor_copy(m.xn_T[:, :, b * P:(b + 1) * P], by_block(m.bank[b])).then_inc(m.xn2_T, 1)
    for b in range(B):
        dve.wait_ge(m.xn2_hi, b + 1)
        dve.tensor_tensor(m.xn_lo[:, b, :], m.xn_tok[:, b, :], m.xn_hi[:, b, :].bitcast(F32), ALU.subtract).then_inc(
            m.xn2_lo, 1)
    dve.wait_ge(m.logit_mm, 1)
    dve.wait_ge(m.consts_in, 48)

    def do(ins):
        step.done(ins)
        step.wait()

    def over_experts(t):
        return t[:].unsqueeze(2).to_broadcast([P, B, E])

    iota = m.iota[:, 0:E].unsqueeze(1).to_broadcast([P, B, E])
    do(dve.tensor_copy(m.logits[:].rearrange("p b e -> p (b e)"), m.bank[2][:, 0:B * E]))
    for scores, best, first, chosen in ((m.logits, m.best1, m.first1, m.chosen1),
                                        (m.rest, m.best2, m.first2, m.chosen2)):
        do(dve.tensor_reduce(best[:], scores[:], X_AXIS, ALU.max))
        do(dve.tensor_tensor(m.is_max[:], scores[:], over_experts(best), ALU.is_equal))
        do(dve.scalar_tensor_tensor(m.candidate[:], m.is_max[:], -float(E), iota, ALU.mult, ALU.add))
        do(dve.tensor_reduce(first[:], m.candidate[:], X_AXIS, ALU.min))
        do(dve.tensor_tensor(chosen[:], m.candidate[:], over_experts(first), ALU.is_equal))
        if chosen is m.chosen1:
            do(dve.scalar_tensor_tensor(m.rest[:], chosen[:], BELOW_ALL, m.logits[:], ALU.mult, ALU.add))
    dve.tensor_tensor(m.routed[:], m.chosen1[:], m.chosen2[:], ALU.add).then_inc(m.routed_done, 1)
    dve.tensor_tensor(m.gap[:], m.best2[:], m.best1[:], ALU.subtract).then_inc(m.gap_done, 1)
    dve.wait_ge(m.gap_exp_done, 1)
    do(dve.tensor_scalar(m.gap_sum[:], m.gap_exp[:], 1.0, None, ALU.add))
    do(dve.reciprocal(m.weight1[:], m.gap_sum[:]))
    do(dve.tensor_tensor(m.weight2[:], m.gap_exp[:], m.weight1[:], ALU.mult))
    do(dve.tensor_tensor(m.weighted1[:], m.chosen1[:], over_experts(m.weight1), ALU.mult))
    do(dve.tensor_tensor(m.candidate[:], m.chosen2[:], over_experts(m.weight2), ALU.mult))
    do(dve.tensor_tensor(m.gate_of[:, :, 0:E], m.weighted1[:], m.candidate[:], ALU.add))
    do(dve.memset(m.gate_of[:, :, TURNS - 1:], 0.0))
    do(dve.memset(m.slot_of[:, :, TURNS - 1:], -1.0))
    dve.wait_ge(m.rank_mm, 1)
    rank = m.bank[3][:, 0:B * E].rearrange("p (b e) -> p b e", b=B)
    do(dve.scalar_tensor_tensor(m.position[:], rank, 1.0, m.routed[:], ALU.add, ALU.mult))
    do(dve.tensor_scalar(m.slot_of[:, :, 0:E], m.position[:], -1.0, None, ALU.add))

    def build(e):
        for b in range(B):
            last = dve.tensor_scalar(m.pick[:, b, :], m.iota[:], m.slot_of[:, b, bass.ds(e, 1)], None, ALU.is_equal)
        last.then_inc(m.pick_done, 1)

    def gathered(e):
        dve.wait_ge(m.gather_mm, e * 2 + 2)
        dve.tensor_copy(m.xg_lo[:], by_block(m.bank[XG_BANKS[1]])).then_inc(m.xg_lo_done, 1)

    build(0)
    do(dve.tensor_scalar(m.crowded[:, 0, :], m.bank[3][:, B * E:B * E + E], float(P), None, ALU.is_gt))
    do(dve.tensor_reduce(m.n_crowded[:], m.crowded[:, 0, :], X_AXIS, ALU.add))
    dve.tensor_scalar(m.n_turns[:], m.n_crowded[:], float(E), None, ALU.add).then_inc(m.n_ready, 1)
    gathered(0)
    do(dve.memset(m.expert_f[:, TURNS - 1:], 0.0))
    do(dve.tensor_copy(m.expert_f[:, 0:E], m.iota[:, 0:E]))
    for r in range(EXTRA):
        do(dve.scalar_tensor_tensor(m.order[:], m.crowded[:, r, :], -float(E), m.iota[:, 0:E], ALU.mult, ALU.add))
        do(dve.tensor_reduce(m.first_one[:], m.order[:], X_AXIS, ALU.min))
        do(dve.scalar_tensor_tensor(m.extra[:, r, :], m.order[:], m.first_one[:], m.crowded[:, r, :], ALU.is_equal,
                                    ALU.mult))
        do(dve.tensor_tensor(m.crowded[:, r + 1, :], m.crowded[:, r, :], m.extra[:, r, :], ALU.subtract))
    extra_turns = slice(E, E + EXTRA)
    extra = m.extra[:].unsqueeze(1).to_broadcast([P, B, EXTRA, E])
    step.done(dve.tensor_tensor(m.extra_index[:], m.extra[:], m.iota[:, 0:E].unsqueeze(1).to_broadcast([P, EXTRA, E]),
                                ALU.mult))
    step.done(dve.tensor_tensor(m.extra_gate[:], m.gate_of[:, :, 0:E].unsqueeze(2).to_broadcast([P, B, EXTRA, E]),
                                extra, ALU.mult))
    do(dve.tensor_tensor(m.extra_position[:], m.position[:].unsqueeze(2).to_broadcast([P, B, EXTRA, E]), extra,
                         ALU.mult))
    step.done(dve.tensor_reduce(m.expert_f[:, extra_turns], m.extra_index[:], X_AXIS, ALU.add))
    step.done(dve.tensor_reduce(m.gate_of[:, :, extra_turns], m.extra_gate[:], X_AXIS, ALU.add))
    do(dve.tensor_reduce(m.extra_slot[:], m.extra_position[:], X_AXIS, ALU.add))
    do(dve.tensor_scalar(m.slot_of[:, :, extra_turns], m.extra_slot[:], -1.0 - P, None, ALU.add))
    dve.tensor_copy(m.expert_of[:], m.expert_f[:]).then_inc(m.table_ready, 1)
    with dve.Fori(0, turns(dve, m)) as i:
        def unit(k):
            e_split_lo(dve, m, k, i)

        def hidden(j):
            bank = UP_BANKS[j % 2]
            dve.wait_ge(m.silu_done, i * QUARTERS + j + 1)
            dve.wait_ge(m.up_mm, i * len(UP_UNITS) + 2 * j + 2)
            dve.tensor_tensor(m.hidden[:, j % 2, :], m.bank[bank + 1][:], m.silu[:, j % 2, :], ALU.mult).then_inc(
                m.hidden_done, 1)

        def hidden_lo(j):
            dve.wait_ge(m.hidden_hi_done, i * QUARTERS + j + 1)
            dve.tensor_tensor(m.hidden_lo[:, j % 2, :], m.bank[HIDDEN_BANK][:], m.hidden_hi[:, j % 2, :].bitcast(F32),
                              ALU.subtract).then_inc(m.hidden_lo_done, 1)

        hidden(0)
        unit(7)
        hidden(1)
        hidden_lo(0)
        build(i + 1)
        hidden(2)
        unit(10)
        hidden_lo(1)
        unit(11)
        hidden(3)
        unit(13)
        hidden_lo(2)
        gathered(i + 1)
        hidden_lo(3)
        dve.wait_ge(m.y_hi_done, i + 1)
        dve.tensor_tensor(m.y_lo[:], m.bank[Y_BANK][:], m.y_hi[:].bitcast(F32), ALU.subtract).then_inc(m.y_lo_done, 1)
        for b in range(B):
            dve.wait_ge(m.scatter_mm, i * B + b + 1)
            dve.scalar_tensor_tensor(m.x_res[:, b, :], m.bank[XG_BANKS[b]][:], m.gate_of[:, b, bass.ds(i, 1)],
                                     m.x_res[:, b, :], ALU.mult, ALU.add).then_inc(m.acc_done, 1)
        unit(16)
        unit(17)


def pe_moe(pe, m):
    for b in range(B):
        pe.wait_ge(m.xn2_ready, b + 1)
        pe_transpose4(pe, m, m.bank[b], [m.xn_tok[:, b, k * P:(k + 1) * P] for k in range(KT)], m.ident[:]).then_inc(
            m.xn2_mm, 1)
    pe.wait_ge(m.gate_in, 16)
    pe.wait_ge(m.xn2_T, B)
    for b in range(B):
        for k in range(KT):
            last = pe.matmul(m.bank[2][:, b * E:(b + 1) * E], m.xn_T[:, k, b * P:(b + 1) * P], m.gate_sb[:, k, :],
                             start=k == 0, stop=k == KT - 1)
    last.then_inc(m.logit_mm, 1)
    pe.wait_ge(m.consts_in, 48)
    pe.wait_ge(m.routed_done, 1)
    pe.matmul(m.bank[3][:, 0:E], m.earlier[:], m.routed[:, 0, :], start=True, stop=True)
    pe.matmul(m.bank[3][:, E:2 * E], m.earlier[:], m.routed[:, 1, :], start=True, stop=False)
    pe.matmul(m.bank[3][:, E:2 * E], m.ones[:], m.routed[:, 0, :], start=False, stop=True)
    for b in range(B):
        last = pe.matmul(m.bank[3][:, 2 * E:3 * E], m.ones[:], m.routed[:, b, :], start=b == 0, stop=b == B - 1)
    last.then_inc(m.rank_mm, 1)

    def gather(e):
        pe.wait_ge(m.pick_done, e + 1)
        for part, bank in ((m.xn_hi, m.bank[XG_BANKS[0]]), (m.xn_lo, m.bank[XG_BANKS[1]])):
            for k in range(KT):
                for b in range(B):
                    last = pe.matmul(bank[:, k * P:(k + 1) * P], part[:, b, k * P:(k + 1) * P], m.pick[:, b, :],
                                     start=b == 0, stop=b == B - 1)
            last.then_inc(m.gather_mm, 1)

    pe.wait_ge(m.xn2_lo, B)
    gather(0)
    with pe.Fori(0, turns(pe, m)) as i:

        def unit(k):
            e_wait(pe, m.e_lo_done, k, i)
            return m.e_hi[e_slot(k)], m.e_lo[e_slot(k)]

        def up(j):
            if j == 0:
                pe.wait_ge(m.xg_hi_done, i + 1)
                pe.wait_ge(m.xg_lo_done, i + 1)
            for q in range(2):
                w_hi, w_lo = unit(UP_UNITS[2 * j + q])
                if q == 0 and j >= 2:
                    pe.wait_ge(m.hidden_done, i * QUARTERS + j - 1)
                for k in range(KT):
                    last = three_passes(pe, m.bank[UP_BANKS[j % 2] + q][:], m.xg_hi[:, k, :], m.xg_lo[:, k, :],
                                        w_hi[:, k, :], w_lo[:, k, :], k == 0, k == KT - 1)
                last.then_inc(m.up_mm, 1)

        def hidden(j):
            pe.wait_ge(m.hidden_done, i * QUARTERS + j + 1)
            if j:
                pe.wait_ge(m.hidden_lo_done, i * QUARTERS + j)
            else:
                pe.wait_ge(m.pickT_done, i + 1)
            pe_transpose4(pe, m, m.bank[HIDDEN_BANK], [m.hidden[:, j % 2, t * P:(t + 1) * P] for t in range(KT)],
                          m.ident[:]).then_inc(m.hiddenT_mm, 1)

        def down(j):
            w_hi, w_lo = unit(DOWN_UNITS[j])
            pe.wait_ge(m.hidden_lo_done, i * QUARTERS + j + 1)
            for k in range(KT):
                cols = slice(k * P, (k + 1) * P)
                last = three_passes(pe, m.bank[Y_BANK][:], m.hidden_hi[:, j % 2, cols], m.hidden_lo[:, j % 2, cols],
                                    w_hi[:, k, :], w_lo[:, k, :], j == 0 and k == 0, j == QUARTERS - 1 and k == KT - 1)
            last.then_inc(m.down_mm, 1)

        up(0)
        for b in range(B):
            last = pe.transpose(m.bank[HIDDEN_BANK][:, b * P:(b + 1) * P], m.pick[:, b, :].bitcast(F32), m.ident[:])
        last.then_inc(m.pickT_mm, 1)
        up(1)
        hidden(0)
        up(2)
        down(0)
        hidden(1)
        up(3)
        down(1)
        hidden(2)
        gather(i + 1)
        hidden(3)
        down(2)
        down(3)
        pe.wait_ge(m.xg_hi_done, i + 2)
        pe.wait_ge(m.xg_lo_done, i + 2)
        pe.wait_ge(m.y_hi_done, i + 1)
        for b in range(B):
            pe.matmul(m.bank[XG_BANKS[b]][:], m.pick_T[:, b, :], m.y_hi[:], start=True, stop=False)
        pe.wait_ge(m.y_lo_done, i + 1)
        for b in range(B):
            pe.matmul(m.bank[XG_BANKS[b]][:], m.pick_T[:, b, :], m.y_lo[:], start=False, stop=True).then_inc(
                m.scatter_mm, 1)


def _blocks(w, rows):
    return w.reshape(rows // P, P, -1).transpose(1, 0, 2)


def _positions():
    pos = np.arange(P - 1, -1, -1, dtype=np.float32)
    freq = (np.float32(1.0) / np.float32(10000.0) ** (np.arange(0, D, 2, dtype=np.float32) / np.float32(D))).astype(
        np.float32)
    ang = pos[:, None] * freq[None, :]
    return np.concatenate([np.sin(ang), np.cos(ang)], axis=-1).astype(np.float32)


def kernel(**inputs):
    from concourse import bacc
    from concourse.bass_utils import run_bass_kernel_spmd

    a = {k: np.asarray(v) for k, v in inputs.items()}
    c = np.ascontiguousarray
    unit = (P, KT * CHUNK)
    w_cross = c(np.stack([_blocks(a[f"L0_xattn_{n}"].T, D).reshape(unit) for n in ("Wq", "Wk", "Wv", "Wo")]))
    ctx_t = c(a["ctx_1024"].reshape(B, NCH, CHUNK, KT, P).transpose(0, 1, 4, 3, 2).reshape(B * NCH, *unit))

    def units(w, rows):
        r, n = w.shape
        return [_blocks(w[i:i + D, j:j + CHUNK], D).reshape(unit) for i in range(0, r, D) for j in range(0, n, CHUNK)]

    stream = []
    for i in range(L):
        qkv = a["L0_attn_W_qkv"][i]
        hd = H * DH
        for w in (a["L0_attn_W_r"][i], qkv[:, :hd], qkv[:, hd:2 * hd], qkv[:, 2 * hd:], a["L0_attn_W_o"][i],
                  a["L0_attn_W_ff1"][i], a["L0_attn_W_ff2"][i]):
            stream += units(w, D)
    for e in range(E):
        quarters = {n: units(a[f"L0_ffn_{n}"][e], D) for n in ("w0", "w1", "wo")}
        stream += [quarters[n][q] for n, q in E_ORDER]
    w_stream = c(np.stack(stream))
    arrays = {
        "x": c(a["x"]),
        "ctx_t": ctx_t,
        "mask": c(a["mask_1x1xSxS2_ik0"].reshape(P, SK)),
        "w_cross": w_cross,
        "w_stream": w_stream,
        "cross_vecs": c(np.stack([a[f"L0_xattn_{n}"].reshape(KT, P).T for n in ("bq", "bk", "bv")], axis=1)),
        "bo_row": c(a["L0_xattn_bo"]),
        "consts": np.stack([np.eye(P), np.triu(np.ones((P, P)), 1), np.tile(np.arange(P), (P, 1)),
                            np.ones((P, P))]).astype(np.float32),
        "r_t": c(_blocks(_positions().T, D).reshape(unit[0], KT * P)),
        "uv": c(np.stack([np.tile(a[f"L0_attn_{n}"].T, (2, 1)) for n in "uv"], axis=1)),
        "ff1_bias": c(a["L0_attn_b_ff1"].reshape(L, DF // P, P).transpose(2, 0, 1)),
        "layer_rows": c(np.stack([a[f"L0_attn_{n}"] for n in ("ln1_g", "ln1_b", "b_ff2", "ln2_g", "ln2_b")], axis=1)),
        "gate": c(_blocks(a["L0_ffn_gate_kernel"], D)),
    }
    nc = bacc.Bacc("TRN2", target_bir_lowering=False, num_devices=1)
    aps = {n: nc.dram_tensor(n, v.shape, mybir.dt.from_np(v.dtype), kind="ExternalInput").ap()
           for n, v in arrays.items()}
    out = nc.dram_tensor("out", (B, P, D), F32, kind="ExternalOutput").ap()
    build_program(nc, **aps, out=out)
    r = run_bass_kernel_spmd(nc, [arrays], core_ids=[0])
    return r.results[0]["out"]
```
